# Optimizing a Trainium2 kernel written in Bass

```python
import numpy as np
import jax
import jax.numpy as jnp

def _softmax(x, axis=-1):
    return jax.nn.softmax(x, axis=axis)

def _gelu(x):
    return jax.nn.gelu(x, approximate=True)

def _silu(x):
    return jax.nn.silu(x)

def _sigmoid(x):
    return jax.nn.sigmoid(x)

def _layernorm(x, axis=-1, eps=1e-05):
    m = jnp.mean(x, axis=axis, keepdims=True)
    v = jnp.var(x, axis=axis, keepdims=True)
    return (x - m) / jnp.sqrt(v + eps)

def _scatter_add(tgt, idx, src, axis=0):
    return tgt.at[idx].add(src)

def _segment_sum(src, seg, n):
    return jax.ops.segment_sum(src, seg, n)
kernel_name = 'mk_decoder_postln_d4_seqx_r8_a9c818'

def setup_inputs(seed: int=0):
    np.random.seed(seed)
    _w = jnp.asarray

    def _rec_inputs():
        import jax
        import jax.numpy as jnp
        _rk = jax.random.key(seed)
        x = -1.394e-06 + 0.9999 * jax.random.normal(jax.random.fold_in(_rk, 1), (16, 64, 128), jnp.float32)
        _lenS = 64 - jax.random.randint(jax.random.fold_in(_rk, 7), (16,), 0, max(1, 64 // 4) + 1, jnp.int32)
        _lenS2 = 64 - jax.random.randint(jax.random.fold_in(_rk, 8), (16,), 0, max(1, 64 // 4) + 1, jnp.int32)
        _ctx_1024P = jax.random.normal(jax.random.fold_in(_rk, 11), (16, 16, 128), jnp.float32)
        _ctx_1024c = jax.random.dirichlet(jax.random.fold_in(_rk, 511), 0.3 * jnp.ones((16,), jnp.float32), (16, 64))
        _ctx_1024t = jnp.einsum('bsk,bkd->bsd', _ctx_1024c, _ctx_1024P)
        _ctx_1024t = _ctx_1024t * jax.lax.rsqrt(jnp.mean(jnp.square(_ctx_1024t)) + 1e-12) * 0.953939
        ctx_1024 = -0.000292821 + 1.00034 * (_ctx_1024t + 0.3 * jax.random.normal(jax.random.fold_in(_rk, 611), (16, 64, 128), jnp.float32))
        _validS = jnp.arange(64)[None, :] < _lenS[:, None]
        _validS2 = jnp.arange(64)[None, :] < _lenS2[:, None]
        _causal = jnp.tril(jnp.ones((64, 64), dtype=bool))
        mask_BxSx1_ff1 = jnp.where(jnp.ones((16, 64, 1), dtype=bool), 1.0, 0.0).astype(jnp.float32)
        mask_BxS2_bk0 = jnp.logical_not(jnp.broadcast_to(_validS2[:, :], (16, 64)))
        mask_SxS2_bk1 = jnp.broadcast_to(_validS2[0:1, :], (64, 64))
        mask_Bx1xSxS2_ik1 = jnp.where(jnp.broadcast_to(_validS2[:, None, None, :], (16, 1, 64, 64)), 1, 0).astype(jnp.int32)
        return (x, ctx_1024, mask_BxSx1_ff1, mask_BxS2_bk0, mask_SxS2_bk1, mask_Bx1xSxS2_ik1)
    x, ctx_1024, mask_BxSx1_ff1, mask_BxS2_bk0, mask_SxS2_bk1, mask_Bx1xSxS2_ik1 = _rec_inputs()

    def _L0_attn_setup():
        import jax, jax.numpy as jnp
        import numpy as np
        D_MODEL = 128
        NHEAD = 16

        def unitnorm(v):
            n = jnp.sqrt(jnp.sum(v * v, axis=-1, keepdims=True))
            return v / jnp.maximum(n, 1e-12)

        def _reference_tuple_inner(inp, Wq_w, Wq_b, Wk_w, Wk_b, Wv_w, Wv_b, Wo_w, Wo_b, Ww_w, Ww_b, Wr_w, Wr_b):
            src = inp
            S, B, d = inp.shape
            n = NHEAD
            k = (src @ Wk_w.T + Wk_b).reshape(S, B, n, -1)
            v = (src @ Wv_w.T + Wv_b).reshape(S, B, n, -1)
            q = (inp @ Wq_w.T + Wq_b).reshape(S, B, n, -1)
            k = unitnorm(k)
            q = unitnorm(q)
            w = jax.nn.sigmoid(src @ Ww_w.T + Ww_b)
            A = jnp.einsum('sbnq,sbnv->bnvq', k, v * w[:, :, :, None])
            r = jax.nn.sigmoid(inp @ Wr_w.T + Wr_b)
            out = jnp.einsum('sbnq,bnvq->sbnv', q, A) * r[:, :, :, None]
            out = out.reshape(S, B, d)
            out = out @ Wo_w.T + Wo_b
            return (out, A)
        key = jax.random.key(seed)
        ks = jax.random.split(key, 14)
        d = D_MODEL
        sc = 1.0 / np.sqrt(d)
        inp = jax.random.normal(ks[0], (256, 8, d), dtype=jnp.float32)

        def lin(kw, kb, out_dim):
            W = jax.random.uniform(kw, (out_dim, d), minval=-sc, maxval=sc, dtype=jnp.float32)
            b = jax.random.uniform(kb, (out_dim,), minval=-sc, maxval=sc, dtype=jnp.float32)
            return (W, b)
        Wq_w, Wq_b = lin(ks[1], ks[2], d)
        Wk_w, Wk_b = lin(ks[3], ks[4], d)
        Wv_w, Wv_b = lin(ks[5], ks[6], d)
        Wo_w, Wo_b = lin(ks[7], ks[8], d)
        Ww_w, Ww_b = lin(ks[9], ks[10], NHEAD)
        Wr_w, Wr_b = lin(ks[11], ks[12], NHEAD)
        return {'inp': inp, 'Wq_w': Wq_w, 'Wq_b': Wq_b, 'Wk_w': Wk_w, 'Wk_b': Wk_b, 'Wv_w': Wv_w, 'Wv_b': Wv_b, 'Wo_w': Wo_w, 'Wo_b': Wo_b, 'Ww_w': Ww_w, 'Ww_b': Ww_b, 'Wr_w': Wr_w, 'Wr_b': Wr_b}
    _L0_attn_all = _L0_attn_setup()
    _L0_attn_in = {k: v for k, v in _L0_attn_all.items() if k in ('Wq_w', 'Wq_b', 'Wk_w', 'Wk_b', 'Wv_w', 'Wv_b', 'Wo_w', 'Wo_b', 'Ww_w', 'Ww_b', 'Wr_w', 'Wr_b')}
    del _L0_attn_all

    def _L0_xattn_setup():
        import jax, jax.numpy as jnp
        import numpy as np
        NUM_HEADS = 16
        KEY_DIM = 128
        VALUE_DIM = 128
        OUTPUT_DIM = 128
        D_MODEL = 128

        def _split_heads(x, H):
            B, S, D = x.shape
            return x.reshape(B, S, H, D // H).transpose(0, 2, 1, 3)
        key = jax.random.key(seed)
        ks = jax.random.split(key, 12)
        B, S = (2, 256)
        inp = {'V': jax.random.normal(ks[0], (B, S, D_MODEL), dtype=jnp.float32), 'Q': jax.random.normal(ks[1], (B, S, D_MODEL), dtype=jnp.float32), 'K': jax.random.normal(ks[2], (B, S, D_MODEL), dtype=jnp.float32), 'mask': jnp.ones((B, S, 1), dtype=jnp.float32), 'WQ': jax.random.normal(ks[3], (D_MODEL, KEY_DIM), dtype=jnp.float32) * (1.0 / np.sqrt(D_MODEL)), 'bQ': jnp.zeros((KEY_DIM,), dtype=jnp.float32), 'WK': jax.random.normal(ks[4], (D_MODEL, KEY_DIM), dtype=jnp.float32) * (1.0 / np.sqrt(D_MODEL)), 'bK': jnp.zeros((KEY_DIM,), dtype=jnp.float32), 'WV': jax.random.normal(ks[5], (D_MODEL, VALUE_DIM), dtype=jnp.float32) * (1.0 / np.sqrt(D_MODEL)), 'bV': jnp.zeros((VALUE_DIM,), dtype=jnp.float32), 'WO': jax.random.normal(ks[6], (VALUE_DIM, OUTPUT_DIM), dtype=jnp.float32) * (1.0 / np.sqrt(VALUE_DIM)), 'bO': jnp.zeros((OUTPUT_DIM,), dtype=jnp.float32)}
        return inp
    _L0_xattn_all = _L0_xattn_setup()
    _L0_xattn_in = {k: v for k, v in _L0_xattn_all.items() if k in ('WQ', 'bQ', 'WK', 'bK', 'WV', 'bV', 'WO', 'bO')}
    del _L0_xattn_all

    def _L0_ffn_setup():
        import jax, jax.numpy as jnp
        import numpy as np
        DIM = 128
        DEPTH = 2
        HEADS = 8
        DIM_HEAD = 64
        WINDOW = 64
        INNER = HEADS * DIM_HEAD
        HID = int(DIM * 4 * 2 / 3)
        B, N = (2, 1024)
        QK_SCALE = 8.0

        def shift_token(t):
            t1, t2 = jnp.split(t, 2, axis=-1)
            t2 = jnp.pad(t2, ((0, 0), (1, 0), (0, 0)))[:, :-1]
            return jnp.concatenate([t1, t2], axis=-1)

        def l2norm(t):
            return t / jnp.clip(jnp.linalg.norm(t, axis=-1, keepdims=True), 1e-12)

        def rotate_half(x):
            x1, x2 = jnp.split(x, 2, axis=-1)
            return jnp.concatenate([-x2, x1], axis=-1)

        def rotary_xpos(q, k):
            n = q.shape[-2]
            half_idx = jnp.arange(0, DIM_HEAD, 2, dtype=jnp.float32)
            inv_freq = 1.0 / 10000.0 ** (half_idx / DIM_HEAD)
            t = jnp.arange(n, dtype=jnp.float32)
            freqs = t[:, None] * inv_freq[None, :]
            freqs = jnp.concatenate([freqs, freqs], axis=-1)
            base = (half_idx + 0.4 * DIM_HEAD) / (1.4 * DIM_HEAD)
            power = (t - n // 2) / float(WINDOW // 2)
            scale = base[None, :] ** power[:, None]
            scale = jnp.concatenate([scale, scale], axis=-1)
            cos, sin = (jnp.cos(freqs), jnp.sin(freqs))
            q = q * cos * scale + rotate_half(q) * sin * scale
            k = k * cos / scale + rotate_half(k) * sin / scale
            return (q, k)

        def local_attention(q, k, v):
            b, h, n, d = q.shape
            w = n // WINDOW
            bq = q.reshape(b, h, w, WINDOW, d) * QK_SCALE
            bk = k.reshape(b, h, w, WINDOW, d)
            bv = v.reshape(b, h, w, WINDOW, d)

            def look_around(t):
                p = jnp.pad(t, ((0, 0), (0, 0), (1, 0), (0, 0), (0, 0)))
                return jnp.concatenate([p[:, :, :w], p[:, :, 1:]], axis=3)
            bk, bv = (look_around(bk), look_around(bv))
            bt = jnp.arange(n).reshape(w, WINDOW)
            btp = jnp.pad(bt, ((1, 0), (0, 0)), constant_values=-1)
            btk = jnp.concatenate([btp[:w], btp[1:]], axis=1)
            sim = jnp.einsum('bhwid,bhwjd->bhwij', bq, bk)
            i = bt[:, :, None]
            j = btk[:, None, :]
            mask = (i < j) | (i > j + WINDOW) | (j == -1)
            sim = jnp.where(mask, -jnp.finfo(sim.dtype).max, sim)
            attn = jax.nn.softmax(sim, axis=-1)
            out = jnp.einsum('bhwij,bhwjd->bhwid', attn, bv)
            return out.reshape(b, h, n, d)

        def _layer(x, wqkv, qs, ksc, wo, lg, lb, w1, b1, w2, b2):
            b, n, _ = x.shape
            h = shift_token(x)
            qkv = h @ wqkv
            q, k, v = jnp.split(qkv, 3, axis=-1)
            to_heads = lambda t: t.reshape(b, n, HEADS, DIM_HEAD).transpose(0, 2, 1, 3)
            q, k, v = (to_heads(q), to_heads(k), to_heads(v))
            q = l2norm(q) * qs
            k = l2norm(k) * ksc
            q, k = rotary_xpos(q, k)
            o = local_attention(q, k, v)
            o = o.transpose(0, 2, 1, 3).reshape(b, n, INNER)
            x = x + o @ wo
            h = shift_token(x)
            mu = h.mean(-1, keepdims=True)
            var = h.var(-1, keepdims=True)
            h = (h - mu) / jnp.sqrt(var + 1e-05) * lg + lb
            h = h @ w1 + b1
            a, g = jnp.split(h, 2, axis=-1)
            h = a * jax.nn.gelu(g, approximate=False)
            x = x + h @ w2 + b2
            return x
        key = jax.random.key(seed)
        ks = jax.random.split(key, 6)
        return {'x': jax.random.normal(ks[0], (B, N, DIM), jnp.float32), 'wqkv': jax.random.normal(ks[1], (DEPTH, DIM, 3 * INNER), jnp.float32) * 0.02, 'q_scale': jnp.ones((DEPTH, DIM_HEAD), jnp.float32), 'k_scale': jnp.ones((DEPTH, DIM_HEAD), jnp.float32), 'wo': jax.random.normal(ks[2], (DEPTH, INNER, DIM), jnp.float32) * 0.02, 'ln_g': jnp.ones((DEPTH, DIM), jnp.float32), 'ln_b': jnp.zeros((DEPTH, DIM), jnp.float32), 'w1': jax.random.normal(ks[3], (DEPTH, DIM, 2 * HID), jnp.float32) * 0.02, 'b1': jnp.zeros((DEPTH, 2 * HID), jnp.float32), 'w2': jax.random.normal(ks[4], (DEPTH, HID, DIM), jnp.float32) * 0.02, 'b2': jnp.zeros((DEPTH, DIM), jnp.float32)}
    _L0_ffn_all = _L0_ffn_setup()
    _L0_ffn_in = {k: v for k, v in _L0_ffn_all.items() if k in ('wqkv', 'q_scale', 'k_scale', 'wo', 'ln_g', 'ln_b', 'w1', 'b1', 'w2', 'b2')}
    del _L0_ffn_all

    def _L1_attn_setup():
        import jax, jax.numpy as jnp
        import numpy as np
        HIDDEN_DIM = 128
        NUM_HEADS = 16
        HEAD_DIM = HIDDEN_DIM // NUM_HEADS
        SCALAR_NORM = float(np.sqrt(HIDDEN_DIM / NUM_HEADS))
        key = jax.random.key(seed)
        k1, k2 = jax.random.split(key)
        B, N, D = (2, 256, HIDDEN_DIM)
        x = jax.random.normal(k1, (B, N, D), dtype=jnp.float32)
        limit = float(np.sqrt(6.0 / (D + 3 * D)))
        W_qkv = jax.random.uniform(k2, (3 * D, D), dtype=jnp.float32, minval=-limit, maxval=limit)
        return {'x': x, 'W_qkv': W_qkv}
    _L1_attn_all = _L1_attn_setup()
    _L1_attn_in = {k: v for k, v in _L1_attn_all.items() if k in ('W_qkv',)}
    del _L1_attn_all

    def _L1_xattn_setup():
        import jax, jax.numpy as jnp
        import numpy as np
        DIM = 128
        NHEADS = 16
        HEAD_DIM = DIM // NHEADS

        def _split_heads(x):
            B, S, _ = x.shape
            return x.reshape(B, S, NHEADS, HEAD_DIM).transpose(0, 2, 1, 3)
        key = jax.random.key(seed)
        ks = jax.random.split(key, 11)
        B, S = (4, 256)
        scale = 1.0 / np.sqrt(DIM)
        inp = {'Q': jax.random.normal(ks[0], (B, S, DIM), jnp.float32), 'K': jax.random.normal(ks[1], (B, S, DIM), jnp.float32), 'V': jax.random.normal(ks[2], (B, S, DIM), jnp.float32), 'Wq': jax.random.normal(ks[3], (DIM, DIM), jnp.float32) * scale, 'bq': jnp.zeros((DIM,), jnp.float32), 'Wk': jax.random.normal(ks[4], (DIM, DIM), jnp.float32) * scale, 'bk': jnp.zeros((DIM,), jnp.float32), 'Wv': jax.random.normal(ks[5], (DIM, DIM), jnp.float32) * scale, 'bv': jnp.zeros((DIM,), jnp.float32), 'Wo': jax.random.normal(ks[6], (DIM, DIM), jnp.float32) * scale, 'bo': jnp.zeros((DIM,), jnp.float32)}
        return inp
    _L1_xattn_all = _L1_xattn_setup()
    _L1_xattn_in = {k: v for k, v in _L1_xattn_all.items() if k in ('Wq', 'bq', 'Wk', 'bk', 'Wv', 'bv', 'Wo', 'bo')}
    del _L1_xattn_all

    def _L1_ffn_setup():
        import jax, jax.numpy as jnp
        import numpy as np
        NUM_EXPERTS = 8
        TOP_K = 2
        HIDDEN = 128
        INTER_TOTAL = 1024
        B, S = (2, 256)
        key = jax.random.key(seed)
        k1, k2, k3, k4, k5, k6 = jax.random.split(key, 6)
        T = B * S
        x = jax.random.normal(k1, (B, S, HIDDEN), dtype=jnp.float32)
        scores = jax.random.uniform(k2, (T, NUM_EXPERTS), dtype=jnp.float32)
        expert_weights = jax.random.uniform(k3, (T, TOP_K), dtype=jnp.float32)
        top_experts = jax.random.randint(k4, (T, TOP_K), 0, NUM_EXPERTS, dtype=jnp.int32)
        w1 = jax.random.normal(k5, (HIDDEN, INTER_TOTAL), dtype=jnp.float32) * 0.02
        w2 = jax.random.normal(k6, (INTER_TOTAL, HIDDEN), dtype=jnp.float32) * 0.02
        return {'x': x, 'scores': scores, 'expert_weights': expert_weights, 'top_experts': top_experts, 'w1': w1, 'w2': w2}
    _L1_ffn_all = _L1_ffn_setup()
    _L1_ffn_in = {k: v for k, v in _L1_ffn_all.items() if k in ('scores', 'expert_weights', 'top_experts', 'w1', 'w2')}
    del _L1_ffn_all

    def _L2_attn_setup():
        import jax, jax.numpy as jnp
        import numpy as np
        DIM = 128
        BATCH = 4
        SEQ = 512
        key = jax.random.key(seed)
        ks = jax.random.split(key, 5)
        s = 1.0 / np.sqrt(DIM)
        x = jax.random.normal(ks[0], (BATCH, SEQ, DIM), dtype=jnp.float32)
        W_in = jax.random.uniform(ks[1], (DIM, DIM), jnp.float32, -s, s)
        b_in = jax.random.uniform(ks[2], (DIM,), jnp.float32, -s, s)
        W_out = jax.random.uniform(ks[3], (DIM, DIM), jnp.float32, -s, s)
        b_out = jax.random.uniform(ks[4], (DIM,), jnp.float32, -s, s)
        decay = jnp.float32(0.25)
        mix = jnp.float32(0.5)
        return {'x': x, 'W_in': W_in, 'b_in': b_in, 'W_out': W_out, 'b_out': b_out, 'decay': decay, 'mix': mix}
    _L2_attn_all = _L2_attn_setup()
    _L2_attn_in = {k: v for k, v in _L2_attn_all.items() if k in ('W_in', 'b_in', 'W_out', 'b_out', 'decay', 'mix')}
    del _L2_attn_all

    def _L2_xattn_setup():
        import jax, jax.numpy as jnp
        import numpy as np
        B, T, D, H = (2, 256, 128, 32)
        NEG = -1000000000.0
        key = jax.random.key(seed)
        ks = jax.random.split(key, 8)
        q = jax.random.normal(ks[0], (B, T, D), jnp.float32)
        k = jax.random.normal(ks[1], (B, T, D), jnp.float32)
        v = jax.random.normal(ks[2], (B, T, D), jnp.float32)
        Wqkv = jax.random.normal(ks[3], (D, 3 * D), jnp.float32) * 0.02
        bqkv = jax.random.normal(ks[4], (3 * D,), jnp.float32) * 0.02
        Wo = jax.random.normal(ks[5], (D, D), jnp.float32) * 0.02
        bo = jax.random.normal(ks[6], (D,), jnp.float32) * 0.02
        key_padding_mask = jnp.zeros((B, T), bool).at[1, T - 128:].set(True)
        attn_mask = jnp.triu(jnp.ones((T, T), bool), k=1)
        return {'q': q, 'k': k, 'v': v, 'Wqkv': Wqkv, 'bqkv': bqkv, 'Wo': Wo, 'bo': bo, 'key_padding_mask': key_padding_mask, 'attn_mask': attn_mask, 'n_heads': H}
    _L2_xattn_all = _L2_xattn_setup()
    _L2_xattn_in = {k: v for k, v in _L2_xattn_all.items() if k in ('Wqkv', 'bqkv', 'Wo', 'bo')}
    del _L2_xattn_all

    def _L2_ffn_setup():
        import jax, jax.numpy as jnp
        import numpy as np
        E = 16
        H = 128
        F = 256
        TOP_K = 1
        B, S = (2, 128)
        key = jax.random.key(seed)
        ks = jax.random.split(key, 7)
        s = 0.02
        return {'hidden_states': jax.random.normal(ks[0], (B, S, H), jnp.float32), 'w_router': jax.random.normal(ks[1], (E, H), jnp.float32) * s, 'gate_up_proj': jax.random.normal(ks[2], (E, H, 2 * F), jnp.float32) * s, 'down_proj': jax.random.normal(ks[3], (E, F, H), jnp.float32) * s, 'w_gate': jax.random.normal(ks[4], (F, H), jnp.float32) * s, 'w_up': jax.random.normal(ks[5], (F, H), jnp.float32) * s, 'w_down': jax.random.normal(ks[6], (H, F), jnp.float32) * s}
    _L2_ffn_all = _L2_ffn_setup()
    _L2_ffn_in = {k: v for k, v in _L2_ffn_all.items() if k in ('w_router', 'gate_up_proj', 'down_proj', 'w_gate', 'w_up', 'w_down')}
    del _L2_ffn_all

    def _L3_attn_setup():
        import jax, jax.numpy as jnp
        import numpy as np
        B, L, D_IN, D_OUT, H = (2, 256, 128, 128, 16)
        HD = D_OUT // H
        key = jax.random.key(seed)
        ks = jax.random.split(key, 7)
        s = 0.02
        return {'x': jax.random.normal(ks[0], (B, L, D_IN), dtype=jnp.float32), 'W_q': jax.random.normal(ks[1], (D_IN, D_OUT), dtype=jnp.float32) * s, 'W_k': jax.random.normal(ks[2], (D_IN, D_OUT), dtype=jnp.float32) * s, 'W_v': jax.random.normal(ks[3], (D_IN, D_OUT), dtype=jnp.float32) * s, 'W_o': jax.random.normal(ks[4], (D_OUT, D_OUT), dtype=jnp.float32) * s, 'b_o': jnp.zeros((D_OUT,), dtype=jnp.float32), 'rel_emb': jax.random.normal(ks[5], (2 * L - 1, HD), dtype=jnp.float32)}
    _L3_attn_all = _L3_attn_setup()
    _L3_attn_in = {k: v for k, v in _L3_attn_all.items() if k in ('W_q', 'W_k', 'W_v', 'W_o', 'b_o', 'rel_emb')}
    del _L3_attn_all

    def _L3_xattn_setup():
        import jax, jax.numpy as jnp
        import numpy as np
        B, S, D, H = (2, 256, 128, 16)
        DK = D // H
        key = jax.random.key(seed)
        ks = jax.random.split(key, 8)
        return {'query': jax.random.normal(ks[0], (B, S, D), dtype=jnp.float32), 'key': jax.random.normal(ks[1], (B, S, D), dtype=jnp.float32), 'value': jax.random.normal(ks[2], (B, S, D), dtype=jnp.float32), 'mask': jax.random.randint(ks[3], (B, 1, S, S), 0, 2, dtype=jnp.int32), 'Wq': jax.random.normal(ks[4], (D, D), dtype=jnp.float32) / np.sqrt(D), 'Wk': jax.random.normal(ks[5], (D, D), dtype=jnp.float32) / np.sqrt(D), 'Wv': jax.random.normal(ks[6], (D, D), dtype=jnp.float32) / np.sqrt(D), 'Wo': jax.random.normal(ks[7], (D, D), dtype=jnp.float32) / np.sqrt(D)}
    _L3_xattn_all = _L3_xattn_setup()
    _L3_xattn_in = {k: v for k, v in _L3_xattn_all.items() if k in ('Wq', 'Wk', 'Wv', 'Wo')}
    del _L3_xattn_all

    def _L3_ffn_setup():
        import jax, jax.numpy as jnp
        import numpy as np
        HIDDEN = 128
        INTER = 512
        N_EXPERTS = 8
        TOP_K = 2
        INIT_STD = 0.02
        key = jax.random.key(seed)
        ks = jax.random.split(key, 6)
        x = jax.random.normal(ks[0], (2, 128, HIDDEN), dtype=jnp.float32)
        Wg = jax.random.normal(ks[1], (N_EXPERTS, HIDDEN), dtype=jnp.float32) * INIT_STD
        W1 = jax.random.normal(ks[2], (N_EXPERTS, HIDDEN, INTER), dtype=jnp.float32) * INIT_STD
        b1 = jnp.zeros((N_EXPERTS, INTER), dtype=jnp.float32)
        W2 = jax.random.normal(ks[3], (N_EXPERTS, INTER, HIDDEN), dtype=jnp.float32) * INIT_STD
        b2 = jnp.zeros((N_EXPERTS, HIDDEN), dtype=jnp.float32)
        return {'x': x, 'Wg': Wg, 'W1': W1, 'b1': b1, 'W2': W2, 'b2': b2}
    _L3_ffn_all = _L3_ffn_setup()
    _L3_ffn_in = {k: v for k, v in _L3_ffn_all.items() if k in ('Wg', 'W1', 'b1', 'W2', 'b2')}
    del _L3_ffn_all
    return {'x': x, 'ctx_1024': ctx_1024, 'mask_BxSx1_ff1': mask_BxSx1_ff1, 'mask_BxS2_bk0': mask_BxS2_bk0, 'mask_SxS2_bk1': mask_SxS2_bk1, 'mask_Bx1xSxS2_ik1': mask_Bx1xSxS2_ik1, 'L0_attn_Wq_w': _L0_attn_in['Wq_w'], 'L0_attn_Wq_b': _L0_attn_in['Wq_b'], 'L0_attn_Wk_w': _L0_attn_in['Wk_w'], 'L0_attn_Wk_b': _L0_attn_in['Wk_b'], 'L0_attn_Wv_w': _L0_attn_in['Wv_w'], 'L0_attn_Wv_b': _L0_attn_in['Wv_b'], 'L0_attn_Wo_w': _L0_attn_in['Wo_w'], 'L0_attn_Wo_b': _L0_attn_in['Wo_b'], 'L0_attn_Ww_w': _L0_attn_in['Ww_w'], 'L0_attn_Ww_b': _L0_attn_in['Ww_b'], 'L0_attn_Wr_w': _L0_attn_in['Wr_w'], 'L0_attn_Wr_b': _L0_attn_in['Wr_b'], 'L0_xattn_WQ': _L0_xattn_in['WQ'], 'L0_xattn_bQ': _L0_xattn_in['bQ'], 'L0_xattn_WK': _L0_xattn_in['WK'], 'L0_xattn_bK': _L0_xattn_in['bK'], 'L0_xattn_WV': _L0_xattn_in['WV'], 'L0_xattn_bV': _L0_xattn_in['bV'], 'L0_xattn_WO': _L0_xattn_in['WO'], 'L0_xattn_bO': _L0_xattn_in['bO'], 'L0_ffn_wqkv': _L0_ffn_in['wqkv'], 'L0_ffn_q_scale': _L0_ffn_in['q_scale'], 'L0_ffn_k_scale': _L0_ffn_in['k_scale'], 'L0_ffn_wo': _L0_ffn_in['wo'], 'L0_ffn_ln_g': _L0_ffn_in['ln_g'], 'L0_ffn_ln_b': _L0_ffn_in['ln_b'], 'L0_ffn_w1': _L0_ffn_in['w1'], 'L0_ffn_b1': _L0_ffn_in['b1'], 'L0_ffn_w2': _L0_ffn_in['w2'], 'L0_ffn_b2': _L0_ffn_in['b2'], 'L1_attn_W_qkv': _L1_attn_in['W_qkv'], 'L1_xattn_Wq': _L1_xattn_in['Wq'], 'L1_xattn_bq': _L1_xattn_in['bq'], 'L1_xattn_Wk': _L1_xattn_in['Wk'], 'L1_xattn_bk': _L1_xattn_in['bk'], 'L1_xattn_Wv': _L1_xattn_in['Wv'], 'L1_xattn_bv': _L1_xattn_in['bv'], 'L1_xattn_Wo': _L1_xattn_in['Wo'], 'L1_xattn_bo': _L1_xattn_in['bo'], 'L1_ffn_scores': _L1_ffn_in['scores'], 'L1_ffn_expert_weights': _L1_ffn_in['expert_weights'], 'L1_ffn_top_experts': _L1_ffn_in['top_experts'], 'L1_ffn_w1': _L1_ffn_in['w1'], 'L1_ffn_w2': _L1_ffn_in['w2'], 'L2_attn_W_in': _L2_attn_in['W_in'], 'L2_attn_b_in': _L2_attn_in['b_in'], 'L2_attn_W_out': _L2_attn_in['W_out'], 'L2_attn_b_out': _L2_attn_in['b_out'], 'L2_attn_decay': _L2_attn_in['decay'], 'L2_attn_mix': _L2_attn_in['mix'], 'L2_xattn_Wqkv': _L2_xattn_in['Wqkv'], 'L2_xattn_bqkv': _L2_xattn_in['bqkv'], 'L2_xattn_Wo': _L2_xattn_in['Wo'], 'L2_xattn_bo': _L2_xattn_in['bo'], 'L2_ffn_w_router': _L2_ffn_in['w_router'], 'L2_ffn_gate_up_proj': _L2_ffn_in['gate_up_proj'], 'L2_ffn_down_proj': _L2_ffn_in['down_proj'], 'L2_ffn_w_gate': _L2_ffn_in['w_gate'], 'L2_ffn_w_up': _L2_ffn_in['w_up'], 'L2_ffn_w_down': _L2_ffn_in['w_down'], 'L3_attn_W_q': _L3_attn_in['W_q'], 'L3_attn_W_k': _L3_attn_in['W_k'], 'L3_attn_W_v': _L3_attn_in['W_v'], 'L3_attn_W_o': _L3_attn_in['W_o'], 'L3_attn_b_o': _L3_attn_in['b_o'], 'L3_attn_rel_emb': _L3_attn_in['rel_emb'], 'L3_xattn_Wq': _L3_xattn_in['Wq'], 'L3_xattn_Wk': _L3_xattn_in['Wk'], 'L3_xattn_Wv': _L3_xattn_in['Wv'], 'L3_xattn_Wo': _L3_xattn_in['Wo'], 'L3_ffn_Wg': _L3_ffn_in['Wg'], 'L3_ffn_W1': _L3_ffn_in['W1'], 'L3_ffn_b1': _L3_ffn_in['b1'], 'L3_ffn_W2': _L3_ffn_in['W2'], 'L3_ffn_b2': _L3_ffn_in['b2']}

def reference(x, ctx_1024, mask_BxSx1_ff1, mask_BxS2_bk0, mask_SxS2_bk1, mask_Bx1xSxS2_ik1, L0_attn_Wq_w, L0_attn_Wq_b, L0_attn_Wk_w, L0_attn_Wk_b, L0_attn_Wv_w, L0_attn_Wv_b, L0_attn_Wo_w, L0_attn_Wo_b, L0_attn_Ww_w, L0_attn_Ww_b, L0_attn_Wr_w, L0_attn_Wr_b, L0_xattn_WQ, L0_xattn_bQ, L0_xattn_WK, L0_xattn_bK, L0_xattn_WV, L0_xattn_bV, L0_xattn_WO, L0_xattn_bO, L0_ffn_wqkv, L0_ffn_q_scale, L0_ffn_k_scale, L0_ffn_wo, L0_ffn_ln_g, L0_ffn_ln_b, L0_ffn_w1, L0_ffn_b1, L0_ffn_w2, L0_ffn_b2, L1_attn_W_qkv, L1_xattn_Wq, L1_xattn_bq, L1_xattn_Wk, L1_xattn_bk, L1_xattn_Wv, L1_xattn_bv, L1_xattn_Wo, L1_xattn_bo, L1_ffn_scores, L1_ffn_expert_weights, L1_ffn_top_experts, L1_ffn_w1, L1_ffn_w2, L2_attn_W_in, L2_attn_b_in, L2_attn_W_out, L2_attn_b_out, L2_attn_decay, L2_attn_mix, L2_xattn_Wqkv, L2_xattn_bqkv, L2_xattn_Wo, L2_xattn_bo, L2_ffn_w_router, L2_ffn_gate_up_proj, L2_ffn_down_proj, L2_ffn_w_gate, L2_ffn_w_up, L2_ffn_w_down, L3_attn_W_q, L3_attn_W_k, L3_attn_W_v, L3_attn_W_o, L3_attn_b_o, L3_attn_rel_emb, L3_xattn_Wq, L3_xattn_Wk, L3_xattn_Wv, L3_xattn_Wo, L3_ffn_Wg, L3_ffn_W1, L3_ffn_b1, L3_ffn_W2, L3_ffn_b2):
    import jax
    import jax.numpy as jnp

    def _L0_attn_ref(inp, Wq_w, Wq_b, Wk_w, Wk_b, Wv_w, Wv_b, Wo_w, Wo_b, Ww_w, Ww_b, Wr_w, Wr_b):
        import jax, jax.numpy as jnp
        import numpy as np
        D_MODEL = 128
        NHEAD = 16

        def unitnorm(v):
            n = jnp.sqrt(jnp.sum(v * v, axis=-1, keepdims=True))
            return v / jnp.maximum(n, 1e-12)

        def _reference_tuple_inner(inp, Wq_w, Wq_b, Wk_w, Wk_b, Wv_w, Wv_b, Wo_w, Wo_b, Ww_w, Ww_b, Wr_w, Wr_b):
            src = inp
            S, B, d = inp.shape
            n = NHEAD
            k = (src @ Wk_w.T + Wk_b).reshape(S, B, n, -1)
            v = (src @ Wv_w.T + Wv_b).reshape(S, B, n, -1)
            q = (inp @ Wq_w.T + Wq_b).reshape(S, B, n, -1)
            k = unitnorm(k)
            q = unitnorm(q)
            w = jax.nn.sigmoid(src @ Ww_w.T + Ww_b)
            A = jnp.einsum('sbnq,sbnv->bnvq', k, v * w[:, :, :, None])
            r = jax.nn.sigmoid(inp @ Wr_w.T + Wr_b)
            out = jnp.einsum('sbnq,bnvq->sbnv', q, A) * r[:, :, :, None]
            out = out.reshape(S, B, d)
            out = out @ Wo_w.T + Wo_b
            return (out, A)
        return _reference_tuple_inner(inp, Wq_w, Wq_b, Wk_w, Wk_b, Wv_w, Wv_b, Wo_w, Wo_b, Ww_w, Ww_b, Wr_w, Wr_b)[0]

    def _L0_xattn_ref(V, Q, K, mask, WQ, bQ, WK, bK, WV, bV, WO, bO):
        import jax, jax.numpy as jnp
        import numpy as np
        NUM_HEADS = 16
        KEY_DIM = 128
        VALUE_DIM = 128
        OUTPUT_DIM = 128
        D_MODEL = 128

        def _split_heads(x, H):
            B, S, D = x.shape
            return x.reshape(B, S, H, D // H).transpose(0, 2, 1, 3)
        H = NUM_HEADS
        B, S, _ = Q.shape
        q = _split_heads(Q @ WQ + bQ, H)
        k = _split_heads(K @ WK + bK, H)
        scores = jnp.einsum('bhqd,bhkd->bhqk', q, k) / jnp.sqrt(jnp.float32(KEY_DIM))
        cross = jnp.einsum('bqi,bki->bqk', mask, mask)[:, None]
        scores = jnp.where(cross > 0, scores, -jnp.inf)
        w = jax.nn.softmax(scores, axis=-1)
        v = _split_heads(V @ WV + bV, H)
        ctx = jnp.einsum('bhqk,bhkd->bhqd', w, v)
        ctx = ctx.transpose(0, 2, 1, 3).reshape(B, S, -1)
        out = ctx @ WO + bO
        return out * mask

    def _L0_ffn_ref(x, wqkv, q_scale, k_scale, wo, ln_g, ln_b, w1, b1, w2, b2):
        import jax, jax.numpy as jnp
        import numpy as np
        DIM = 128
        DEPTH = 2
        HEADS = 8
        DIM_HEAD = 64
        WINDOW = 64
        INNER = HEADS * DIM_HEAD
        HID = int(DIM * 4 * 2 / 3)
        B, N = (2, 1024)
        QK_SCALE = 8.0

        def shift_token(t):
            t1, t2 = jnp.split(t, 2, axis=-1)
            t2 = jnp.pad(t2, ((0, 0), (1, 0), (0, 0)))[:, :-1]
            return jnp.concatenate([t1, t2], axis=-1)

        def l2norm(t):
            return t / jnp.clip(jnp.linalg.norm(t, axis=-1, keepdims=True), 1e-12)

        def rotate_half(x):
            x1, x2 = jnp.split(x, 2, axis=-1)
            return jnp.concatenate([-x2, x1], axis=-1)

        def rotary_xpos(q, k):
            n = q.shape[-2]
            half_idx = jnp.arange(0, DIM_HEAD, 2, dtype=jnp.float32)
            inv_freq = 1.0 / 10000.0 ** (half_idx / DIM_HEAD)
            t = jnp.arange(n, dtype=jnp.float32)
            freqs = t[:, None] * inv_freq[None, :]
            freqs = jnp.concatenate([freqs, freqs], axis=-1)
            base = (half_idx + 0.4 * DIM_HEAD) / (1.4 * DIM_HEAD)
            power = (t - n // 2) / float(WINDOW // 2)
            scale = base[None, :] ** power[:, None]
            scale = jnp.concatenate([scale, scale], axis=-1)
            cos, sin = (jnp.cos(freqs), jnp.sin(freqs))
            q = q * cos * scale + rotate_half(q) * sin * scale
            k = k * cos / scale + rotate_half(k) * sin / scale
            return (q, k)

        def local_attention(q, k, v):
            b, h, n, d = q.shape
            w = n // WINDOW
            bq = q.reshape(b, h, w, WINDOW, d) * QK_SCALE
            bk = k.reshape(b, h, w, WINDOW, d)
            bv = v.reshape(b, h, w, WINDOW, d)

            def look_around(t):
                p = jnp.pad(t, ((0, 0), (0, 0), (1, 0), (0, 0), (0, 0)))
                return jnp.concatenate([p[:, :, :w], p[:, :, 1:]], axis=3)
            bk, bv = (look_around(bk), look_around(bv))
            bt = jnp.arange(n).reshape(w, WINDOW)
            btp = jnp.pad(bt, ((1, 0), (0, 0)), constant_values=-1)
            btk = jnp.concatenate([btp[:w], btp[1:]], axis=1)
            sim = jnp.einsum('bhwid,bhwjd->bhwij', bq, bk)
            i = bt[:, :, None]
            j = btk[:, None, :]
            mask = (i < j) | (i > j + WINDOW) | (j == -1)
            sim = jnp.where(mask, -jnp.finfo(sim.dtype).max, sim)
            attn = jax.nn.softmax(sim, axis=-1)
            out = jnp.einsum('bhwij,bhwjd->bhwid', attn, bv)
            return out.reshape(b, h, n, d)

        def _layer(x, wqkv, qs, ksc, wo, lg, lb, w1, b1, w2, b2):
            b, n, _ = x.shape
            h = shift_token(x)
            qkv = h @ wqkv
            q, k, v = jnp.split(qkv, 3, axis=-1)
            to_heads = lambda t: t.reshape(b, n, HEADS, DIM_HEAD).transpose(0, 2, 1, 3)
            q, k, v = (to_heads(q), to_heads(k), to_heads(v))
            q = l2norm(q) * qs
            k = l2norm(k) * ksc
            q, k = rotary_xpos(q, k)
            o = local_attention(q, k, v)
            o = o.transpose(0, 2, 1, 3).reshape(b, n, INNER)
            x = x + o @ wo
            h = shift_token(x)
            mu = h.mean(-1, keepdims=True)
            var = h.var(-1, keepdims=True)
            h = (h - mu) / jnp.sqrt(var + 1e-05) * lg + lb
            h = h @ w1 + b1
            a, g = jnp.split(h, 2, axis=-1)
            h = a * jax.nn.gelu(g, approximate=False)
            x = x + h @ w2 + b2
            return x
        for l in range(DEPTH):
            x = _layer(x, wqkv[l], q_scale[l], k_scale[l], wo[l], ln_g[l], ln_b[l], w1[l], b1[l], w2[l], b2[l])
        return x

    def _L1_attn_ref(x, W_qkv):
        import jax, jax.numpy as jnp
        import numpy as np
        HIDDEN_DIM = 128
        NUM_HEADS = 16
        HEAD_DIM = HIDDEN_DIM // NUM_HEADS
        SCALAR_NORM = float(np.sqrt(HIDDEN_DIM / NUM_HEADS))
        b, n, d = x.shape
        h, hd = (NUM_HEADS, HEAD_DIM)
        qkv = x @ W_qkv.T
        q, k, v = jnp.split(qkv, 3, axis=-1)
        q = q.reshape(b, n, h, hd).transpose(0, 2, 1, 3)
        k = k.reshape(b, n, h, hd).transpose(0, 2, 1, 3)
        v = v.reshape(b, n, h, hd).transpose(0, 2, 1, 3)
        scores = jnp.einsum('bhik,bhjk->bhij', q, k) / SCALAR_NORM
        attn = jax.nn.softmax(scores, axis=-1)
        out = jnp.einsum('bhij,bhjk->bhik', attn, v)
        return out.transpose(0, 2, 1, 3).reshape(b, n, d)

    def _L1_xattn_ref(Q, K, V, Wq, bq, Wk, bk, Wv, bv, Wo, bo):
        import jax, jax.numpy as jnp
        import numpy as np
        DIM = 128
        NHEADS = 16
        HEAD_DIM = DIM // NHEADS

        def _split_heads(x):
            B, S, _ = x.shape
            return x.reshape(B, S, NHEADS, HEAD_DIM).transpose(0, 2, 1, 3)
        q = _split_heads(Q @ Wq + bq)
        k = _split_heads(K @ Wk + bk)
        v = _split_heads(V @ Wv + bv)
        scores = jnp.einsum('bhqd,bhkd->bhqk', q, k) / np.sqrt(HEAD_DIM)
        attn = jax.nn.softmax(scores, axis=-1)
        out = jnp.einsum('bhqk,bhkd->bhqd', attn, v)
        B, H, S, hd = out.shape
        out = out.transpose(0, 2, 1, 3).reshape(B, S, H * hd)
        return out @ Wo + bo

    def _L1_ffn_ref(x, scores, expert_weights, top_experts, w1, w2):
        import jax, jax.numpy as jnp
        import numpy as np
        NUM_EXPERTS = 8
        TOP_K = 2
        HIDDEN = 128
        INTER_TOTAL = 1024
        B, S = (2, 256)
        in_shape = x.shape
        T = in_shape[0] * in_shape[1]
        H = in_shape[-1]
        x_flat = x.reshape(T, H)
        flat_experts = top_experts.reshape(-1)
        flat_weights = expert_weights.reshape(-1)
        order = jnp.argsort(flat_experts, stable=True)
        token_idx = order // TOP_K
        xg = x_flat[token_idx]
        h = jax.nn.gelu(xg @ w1, approximate=True)
        y = h @ w2
        w_sorted = flat_weights[order]
        out = jnp.zeros((T, H), dtype=x.dtype).at[token_idx].add(w_sorted[:, None] * y)
        return out.reshape(in_shape)

    def _L2_attn_ref(x, W_in, b_in, W_out, b_out, decay, mix):
        import jax, jax.numpy as jnp
        import numpy as np
        DIM = 128
        BATCH = 4
        SEQ = 512
        shifted = jnp.pad(x, ((0, 0), (1, 0), (0, 0)))[:, :-1]
        inp = mix * x + (1.0 - mix) * shifted
        h = jax.nn.relu(jnp.einsum('bsd,ed->bse', inp, W_in) + b_in)

        def step(state, h_t):
            state = state * decay + h_t
            return (state, state)
        h_t_major = jnp.swapaxes(h, 0, 1)
        _, states = jax.lax.scan(step, jnp.zeros((x.shape[0], x.shape[2]), x.dtype), h_t_major)
        states = jnp.swapaxes(states, 0, 1)
        return jnp.einsum('bsd,ed->bse', states, W_out) + b_out

    def _L2_xattn_ref(q, k, v, Wqkv, bqkv, Wo, bo, key_padding_mask, attn_mask, n_heads):
        import jax, jax.numpy as jnp
        import numpy as np
        B, T, D, H = (2, 256, 128, 32)
        NEG = -1000000000.0
        Bq, T1, Dm = q.shape
        T2 = k.shape[1]
        dh = Dm // n_heads
        x = jnp.concatenate([q, k, v], axis=1)
        proj = x @ Wqkv + bqkv
        proj = proj.reshape(Bq, -1, 3, n_heads, dh)
        qp = proj[:, :T1, 0]
        kp = proj[:, T1:T1 + T2, 1]
        vp = proj[:, T1 + T2:, 2]
        scores = jnp.einsum('bqhd,bkhd->bhqk', qp, kp) / np.sqrt(dh).astype(qp.dtype)
        mask = key_padding_mask[:, None, None, :] | attn_mask[None, None, :, :]
        scores = jnp.where(mask, NEG, scores)
        attn = jax.nn.softmax(scores, axis=-1)
        y = jnp.einsum('bhqk,bkhd->bqhd', attn, vp)
        y = y.reshape(Bq, T1, Dm)
        return y @ Wo + bo

    def _L2_ffn_ref(hidden_states, w_router, gate_up_proj, down_proj, w_gate, w_up, w_down):
        import jax, jax.numpy as jnp
        import numpy as np
        E = 16
        H = 128
        F = 256
        TOP_K = 1
        B, S = (2, 128)
        b, s, h = hidden_states.shape
        x = hidden_states.reshape(-1, h)
        logits = x @ w_router.T
        _, top_idx = jax.lax.top_k(logits, TOP_K)
        mask = jax.nn.one_hot(top_idx, E, dtype=logits.dtype).sum(axis=1)
        scores = jax.nn.sigmoid(logits) * mask
        masked_inputs = scores.T[:, :, None] * x[None, :, :]
        gate_up = jnp.einsum('eth,ehf->etf', masked_inputs, gate_up_proj)
        gate, up = jnp.split(gate_up, 2, axis=-1)
        expert_out = jnp.einsum('etf,efh->eth', up * jax.nn.silu(gate), down_proj)
        shared = jax.nn.silu(x @ w_gate.T) * (x @ w_up.T) @ w_down.T
        out = shared + expert_out.sum(axis=0)
        return out.reshape(b, s, h)

    def _L3_attn_ref(x, W_q, W_k, W_v, W_o, b_o, rel_emb):
        import jax, jax.numpy as jnp
        import numpy as np
        B, L, D_IN, D_OUT, H = (2, 256, 128, 128, 16)
        HD = D_OUT // H
        b, n, _ = x.shape

        def split_heads(t):
            return t.reshape(b, n, H, HD).transpose(0, 2, 1, 3)
        q = split_heads(x @ W_q)
        k = split_heads(x @ W_k)
        v = split_heads(x @ W_v)
        scores = jnp.einsum('bhqd,bhkd->bhqk', q, k)
        pos = jnp.arange(n)
        rel_idx = pos[None, :] - pos[:, None] + (n - 1)
        rel = rel_emb[rel_idx]
        scores = scores + jnp.einsum('bhld,lrd->bhlr', q, rel)
        causal = pos[None, :] > pos[:, None]
        scores = jnp.where(causal[None, None], -jnp.inf, scores)
        attn = jax.nn.softmax(scores / np.sqrt(HD).astype(np.float32), axis=-1)
        ctx = jnp.einsum('bhqk,bhkd->bhqd', attn, v)
        ctx = ctx.transpose(0, 2, 1, 3).reshape(b, n, D_OUT)
        return ctx @ W_o + b_o

    def _L3_xattn_ref(query, key, value, mask, Wq, Wk, Wv, Wo):
        import jax, jax.numpy as jnp
        import numpy as np
        B, S, D, H = (2, 256, 128, 16)
        DK = D // H
        b, s, d = query.shape

        def proj(x, W):
            return (x @ W.T).reshape(b, s, H, DK).transpose(0, 2, 1, 3)
        q = proj(query, Wq)
        k = proj(key, Wk)
        v = proj(value, Wv)
        scores = jnp.einsum('bhqd,bhkd->bhqk', q, k) / jnp.sqrt(jnp.float32(DK))
        scores = jnp.where(mask == 0, jnp.float32(-1000000000.0), scores)
        attn = jax.nn.softmax(scores, axis=-1)
        out = jnp.einsum('bhqk,bhkd->bhqd', attn, v)
        out = out.transpose(0, 2, 1, 3).reshape(b, s, d)
        return out @ Wo.T

    def _L3_ffn_ref(x, Wg, W1, b1, W2, b2):
        import jax, jax.numpy as jnp
        import numpy as np
        HIDDEN = 128
        INTER = 512
        N_EXPERTS = 8
        TOP_K = 2
        INIT_STD = 0.02
        orig_shape = x.shape
        xt = x.reshape(-1, HIDDEN)
        T = xt.shape[0]
        logits = xt @ Wg.T
        topk_logits, topk_idx = jax.lax.top_k(logits, TOP_K)
        w = jax.nn.softmax(topk_logits, axis=-1)
        rows = jnp.arange(T)[:, None]
        gates = jnp.zeros((T, N_EXPERTS), xt.dtype).at[rows, topk_idx].add(w)
        h = jnp.einsum('th,ehi->tei', xt, W1) + b1
        h = jax.nn.gelu(h, approximate=False)
        o = jnp.einsum('tei,eih->teh', h, W2) + b2
        y = jnp.einsum('te,teh->th', gates, o)
        return y.reshape(orig_shape)
    x = _layernorm(x + _L0_attn_ref(x, L0_attn_Wq_w, L0_attn_Wq_b, L0_attn_Wk_w, L0_attn_Wk_b, L0_attn_Wv_w, L0_attn_Wv_b, L0_attn_Wo_w, L0_attn_Wo_b, L0_attn_Ww_w, L0_attn_Ww_b, L0_attn_Wr_w, L0_attn_Wr_b), axis=-1)
    x = _layernorm(x + _L0_xattn_ref(ctx_1024, x, ctx_1024, mask_BxSx1_ff1, L0_xattn_WQ, L0_xattn_bQ, L0_xattn_WK, L0_xattn_bK, L0_xattn_WV, L0_xattn_bV, L0_xattn_WO, L0_xattn_bO), axis=-1)
    x = _layernorm(x + _L0_ffn_ref(x, L0_ffn_wqkv, L0_ffn_q_scale, L0_ffn_k_scale, L0_ffn_wo, L0_ffn_ln_g, L0_ffn_ln_b, L0_ffn_w1, L0_ffn_b1, L0_ffn_w2, L0_ffn_b2), axis=-1)
    x = _layernorm(x + _L1_attn_ref(x, L1_attn_W_qkv), axis=-1)
    x = _layernorm(x + _L1_xattn_ref(x, ctx_1024, ctx_1024, L1_xattn_Wq, L1_xattn_bq, L1_xattn_Wk, L1_xattn_bk, L1_xattn_Wv, L1_xattn_bv, L1_xattn_Wo, L1_xattn_bo), axis=-1)
    x = _layernorm(x + _L1_ffn_ref(x, L1_ffn_scores, L1_ffn_expert_weights, L1_ffn_top_experts, L1_ffn_w1, L1_ffn_w2), axis=-1)
    x = _layernorm(x + _L2_attn_ref(x, L2_attn_W_in, L2_attn_b_in, L2_attn_W_out, L2_attn_b_out, L2_attn_decay, L2_attn_mix), axis=-1)
    x = _layernorm(x + _L2_xattn_ref(x, ctx_1024, ctx_1024, L2_xattn_Wqkv, L2_xattn_bqkv, L2_xattn_Wo, L2_xattn_bo, mask_BxS2_bk0, mask_SxS2_bk1, 32), axis=-1)
    x = _layernorm(x + _L2_ffn_ref(x, L2_ffn_w_router, L2_ffn_gate_up_proj, L2_ffn_down_proj, L2_ffn_w_gate, L2_ffn_w_up, L2_ffn_w_down), axis=-1)
    x = _layernorm(x + _L3_attn_ref(x, L3_attn_W_q, L3_attn_W_k, L3_attn_W_v, L3_attn_W_o, L3_attn_b_o, L3_attn_rel_emb), axis=-1)
    x = _layernorm(x + _L3_xattn_ref(x, ctx_1024, ctx_1024, mask_Bx1xSxS2_ik1, L3_xattn_Wq, L3_xattn_Wk, L3_xattn_Wv, L3_xattn_Wo), axis=-1)
    x = _layernorm(x + _L3_ffn_ref(x, L3_ffn_Wg, L3_ffn_W1, L3_ffn_b1, L3_ffn_W2, L3_ffn_b2), axis=-1)
    return x

_drawn_inputs = setup_inputs


def setup_inputs(seed=0):
    import zlib

    import numpy as np

    out = dict(_drawn_inputs(seed))
    spreads = {'L0_xattn_bQ': (0.0, 0.8),
     'L0_xattn_bK': (0.0, 0.8),
     'L0_xattn_bV': (0.0, 0.1),
     'L0_xattn_bO': (0.0, 0.1),
     'L0_ffn_q_scale': (1.0, 0.6),
     'L0_ffn_k_scale': (1.0, 0.6),
     'L0_ffn_ln_g': (1.0, 0.6),
     'L0_ffn_ln_b': (0.0, 0.8),
     'L0_ffn_b1': (0.0, 0.8),
     'L0_ffn_b2': (0.0, 0.1),
     'L1_xattn_bq': (0.0, 0.414),
     'L1_xattn_bk': (0.0, 0.8),
     'L1_xattn_bv': (0.0, 0.1),
     'L1_xattn_bo': (0.0, 0.1),
     'L3_attn_b_o': (0.0, 0.1),
     'L3_ffn_b1': (0.0, 0.459),
     'L3_ffn_b2': (0.0, 0.1)}
    factors = {'L0_attn_Wq_b': 5.518,
     'L0_attn_Wk_b': 5.708,
     'L0_attn_Wv_b': 6.298,
     'L0_attn_Ww_b': 8.0,
     'L0_attn_Wr_b': 8.0,
     'L0_ffn_w1': 6.355,
     'L0_ffn_w2': 6.247,
     'L2_xattn_bqkv': 6.827,
     'L2_ffn_w_router': 8.0,
     'L2_ffn_gate_up_proj': 8.0,
     'L2_ffn_down_proj': 8.0,
     'L2_ffn_w_gate': 5.273,
     'L2_ffn_w_up': 5.33,
     'L2_ffn_w_down': 5.259,
     'L3_attn_W_q': 8.0,
     'L3_attn_W_k': 8.0,
     'L3_attn_rel_emb': 8.0}
    for name, (base, spread) in spreads.items():
        noise = np.random.default_rng([zlib.crc32(name.encode()), seed]).standard_normal(out[name].shape)
        drawn = base * np.exp(spread * noise) if base else spread * noise
        out[name] = jnp.asarray(drawn.astype(out[name].dtype))
    for name, factor in factors.items():
        out[name] = (out[name] * factor).astype(out[name].dtype)
    return out
```

```python
from contextlib import ExitStack

import numpy as np
import concourse.bass as bass
from concourse import mybir

ALU = mybir.AluOpType
ACT = mybir.ActivationFunctionType
F32 = mybir.dt.float32
I32 = mybir.dt.int32
U8 = mybir.dt.uint8
BF16 = mybir.dt.bfloat16
AX = mybir.AxisListType

P = 128
B, S = 16, 64
TOK = B * S
HALF = TOK // 2
NB = HALF // S
NT = HALF // P
HID = int(P * 4 * 2 / 3)
CH = [(0, 128), (128, 128), (256, HID - 256)]
EPS = 1e-5
BIG = 3e38
NE2, NF2 = 16, 256
NE3, NF3 = 8, 512
ATT = ["x0", "a1", "x1", "x2", "a3", "x3"]

FIRST = [("Aw", 416), ("Ab", 416), ("ident", 128), ("blocks", 128), ("seq_of", 8), ("neghalf", 1)]
REST = [("Ao", 128), ("Abo", 128), ("fold", 64), ("par16", 2), ("par32", 2), ("pair16", 8), ("pair32", 16),
        ("causal", 64), ("not_first", 512), ("down16", 16), ("down8", 8), ("cosq", 64), ("sinq", 64),
        ("cosk", 64), ("sink", 64)]
for _a in ATT:
    REST += [(f"{_a}.q", 128), (f"{_a}.k", 128), (f"{_a}.v", 128), (f"{_a}.o", 128),
             (f"{_a}.bq", 1), (f"{_a}.bk", 1), (f"{_a}.bv", 128), (f"{_a}.bo", 128)]
for _l in range(2):
    REST += [(f"f{_l}.b1a", 3), (f"f{_l}.b1g", 3), (f"f{_l}.b2", 1), (f"f{_l}.g", 1), (f"f{_l}.b", 1),
             (f"f{_l}.qs", 64), (f"f{_l}.ks", 64), (f"f{_l}.qsr", 64), (f"f{_l}.ksr", 64)]
REST += [("ema.in", 128), ("ema.out", 128), ("ema.bin", 1), ("ema.bout", 128),
         ("decay", 1), ("mix", 1), ("e2.r", 16), ("e2.g", 256), ("e2.u", 256), ("e2.d", 256),
         ("e3.r", 8), ("e3.b1", 32), ("e3.b2", 128), ("rel", 64)]
EARLY = []
for _l in range(2):
    EARLY += [(f"f{_l}.wqkv", 1536), (f"f{_l}.wo", 512), (f"f{_l}.w1", 2 * HID), (f"f{_l}.w2", 384)]
EARLY += [("g.w1", 1024), ("g.w2", 1024)]


def columns(names):
    at, n = {}, 0
    for name, w in names:
        at[name] = (n, w)
        n += w
    return at, n


class Tally:

    def __init__(self):
        self.count = {}

    def __call__(self, sem, n=1):
        self.count[id(sem)] = self.count.get(id(sem), 0) + n
        return self.count[id(sem)]

    def now(self, sem):
        return self.count.get(id(sem), 0)


def attention_order(units, tiles):
    last = units - tiles
    for i in range(units + 6):
        for lag, step in enumerate(["scores", "turn", "values", "fold", "residual", "finish"]):
            u = i - lag
            if 0 <= u < units:
                if step in ("scores", "turn", "values"):
                    yield step, u
                elif u >= last:
                    yield step, u - last


def lagged(steps, n):
    for i in range(n + len(steps)):
        for lag, step in sorted(enumerate(steps), key=lambda s: s[1] != "rotate"):
            if 0 <= i - lag < n:
                yield step, i - lag


LOCAL = ["rotate", "turn_qk", "scores", "soft", "turn", "values", "out", "shift", "stats", "norm"]
MIX0 = ["project", "scale", "state", "mix"]
TAIL = ["back", "residual", "finish"]


def decoder(nc, small, early, xperm, xtok, ctxT, mrow, mcol, mtok, pad_rows, att_rows, ik_rows, exw,
            gup, down, e3w1, e3w2, out):
    at, width = columns(FIRST + REST)
    eat, ewidth = columns(EARLY)
    n_first = sum(n for _, n in FIRST)
    scratch = nc.dram_tensor("rel_scratch", (NB, P * 512), F32, kind="Internal")
    with ExitStack() as ctx:
        def sb(name, shape, dt=F32):
            return ctx.enter_context(nc.sbuf_tensor(name, shape, dt))

        def sem(name):
            return ctx.enter_context(nc.semaphore(name))

        W = sb("W", [P, width])
        big = sb("big", [P, ewidth + NT * 1024])
        pairs = sb("pairs", [P, 8, HALF])
        X = sb("X", [P, NT, P])
        X1 = sb("X1", [P, NT, P])
        XB = sb("XB", [P, NT, P])
        XT = sb("XT", [P, HALF])
        HT = sb("HT", [P, NB, S])
        CT = sb("CT", [P, HALF])
        Q = sb("Q", [P, NB, 2, S])
        VX = sb("VX", [P, NT, 8, 34])
        VX32 = sb("VX32", [P, NT, 16, 18])
        sm = sb("sm", [P, 4, 512])
        mx = sb("mx", [P, 4, 8])
        pr = sb("pr", [P, 2, 8, 2, S])
        pT = sb("pT", [P, 2, 8, P])
        rs = sb("rs", [P, 2, 8, 2])
        ON = sb("ON", [P, NT, 2, P])
        oT = sb("oT", [P, 2, P])
        cap = sb("cap", [P, 3, NB, S])
        bkm = sb("bkm", [P, 6, 16])
        relp = sb("relp", [P, 8, S])
        rot = sb("rot", [P, 2, 4, S])
        m_row = sb("m_row", [P, NB, S])
        m_col = sb("m_col", [P, NB])
        m_tok = sb("m_tok", [P, NT])
        m_pad = sb("m_pad", [P, NB, S], U8)
        m_att = sb("m_att", [P, S], U8)
        m_ik = sb("m_ik", [P, NB, S], I32)
        ew2 = sb("ew2", [P, NT, 2])
        ew = sb("ew", [P, NT])
        omix = sb("omix", [P, 1])
        res = sb("res", [P, 2, P])
        st = sb("st", [P, 2, 6])
        mv = sb("mv", [P, 2, 2])
        veps = sb("veps", [P, 2, 1])
        rstd = sb("rstd", [P, 2, 1])
        YF = sb("YF", [P, HALF])
        G = sb("G", [P, 4, HALF])
        OTall = sb("OTall", [P, B, S])
        OTh = sb("OTh", [P, HALF])
        lg = sb("lg", [P, NT, 16])
        one = sb("one", [P, NT, 16])
        two = sb("two", [P, NT, 16])
        tmp = sb("tmp", [P, NT, 16])
        sig = sb("sig", [P, NT, 16])
        gate = sb("gate", [P, NT, 16])
        col = sb("col", [P, 8, NT])
        oneT = sb("oneT", [NE2, HALF], BF16)
        pick = sb("pick", [NE2, NE2, P], BF16)
        gT = sb("gT", [NE3, HALF])
        QM = sb("QM", [P, 4, 2, 2, S])
        PM = sb("PM", [P, 4, 2, P])
        HS = sb("HS", [P, 2, 2, S])
        ss = sb("ss", [P, NT, 16])
        rn = sb("rn", [P, NT, 16])

        def w(name, a=0, b=None):
            o, n = at[name]
            return W[:, o + a:o + (n if b is None else b)]

        def early_w(name, a=0, b=None):
            o, n = eat[name]
            return big[:, o + a:o + (n if b is None else b)]

        M1, M2 = pairs[:, 0:4, :], pairs[:, 4:8, :]
        RAW = big[:, ewidth:ewidth + NT * 1024].rearrange("p (t i n) -> p t i n", t=NT, i=2)
        KT = [pT[:, 1, 0:4, :], pT[:, 1, 4:8, :]]
        QMs = [QM, ON[:, :, :, :].rearrange("p t b n -> p (t b n)").rearrange("p (j b c q) -> p j b c q", j=4, b=2, c=2)]
        oT0 = pT[:, 0, :, :].rearrange("p (j r) n -> p j (r n)", j=2).rearrange(
            "p j (r b q) -> p j r b q", r=4, b=2)
        VS = G
        RB = [QM[:, 0:2].rearrange("p a b c q -> p (a b c q)"), QM[:, 2:4].rearrange("p a b c q -> p (a b c q)"),
              PM[:, 0:2].rearrange("p a b q -> p (a b q)"), PM[:, 2:4].rearrange("p a b q -> p (a b q)")]

        def room(a, n, pattern, **k):
            return big[:, a:a + n].rearrange(pattern, **k)
        XP = big[:, 0:HALF]
        Z = room(512, 832, "p (j n) -> p j n", j=2)
        SQ = room(1536, 512, "p (j n) -> p j n", j=2)
        RN = room(2048, 64, "p (j n) -> p j n", j=2)
        SS = room(2112, 64, "p (j n) -> p j n", j=2)
        SG = room(2176, 64, "p (j n) -> p j n", j=2)
        QK = room(2304, 512, "p (j n) -> p j n", j=2)
        VW = room(2816, 256, "p (j n) -> p j n", j=2)
        VJ = room(3072, 2048, "p (j s n) -> p j s n", j=2, s=8)
        AM = room(5120, 2048, "p (j s n) -> p j s n", j=2, s=8)
        QTp = room(7168, 256, "p (j n) -> p j n", j=2)
        gu_w = room(0, 8192, "p (e n) -> p e n", e=NE2)
        dn_w = room(8192, 4096, "p (e c n) -> p e c n", e=NE2, c=2)
        w1_w = room(0, 4096, "p (e n) -> p e n", e=NE3)
        w2_w = room(4096, 4096, "p (e c n) -> p e c n", e=NE3, c=4)

        bank = [ctx.enter_context(nc.psum_tensor(f"bank{i}", [P, 512], F32)) for i in range(8)]
        S0, S1, T0, T1, F0, F1, OB, YB = bank

        first_in = sem("first_in")
        rest_in = sem("rest_in")
        pool_init = sem("pool_init")
        init_pool = sem("init_pool")
        init_dve = sem("init_dve")
        turn_done = sem("turn_done")
        go_pe, go_act, go_dve, go_pool = (sem(f"go_{e}") for e in ("pe", "act", "dve", "pool"))
        turn_sems = [turn_done]

        def tsem(name):
            q = sem(name)
            turn_sems.append(q)
            return q

        xp_in, x_in, ctx_in, masks_in, ew_in = (tsem(n) for n in ("xp_in", "x_in", "ctx_in", "masks_in", "ew_in"))
        f0_in, f1_in, g_in, e2_in, e3_in = (tsem(n) for n in ("f0_in", "f1_in", "g_in", "e2_in", "e3_in"))
        rel_stored = [tsem(f"rel_stored{i}") for i in range(2)]
        rel_back = [tsem(f"rel_back{i}") for i in range(4)]
        out_sent = tsem("out_sent")
        dve_link, act_link, pool_link = tsem("dve_link"), tsem("act_link"), tsem("pool_link")
        (proj_full, qT_full, state_full, mix_full, q_full, k_full, v_full, scored, turned, valued, folded, y_full,
         x_turned, qk_full, rot_full, shifted, restored, normed, up_full, down_full, rel_full, logit_full,
         choice_full, picked, gate_full, o3_full, v2_full, valued2, b2_full) = (tsem(n) for n in (
             "proj_full", "qT_full", "state_full", "mix_full", "q_full", "k_full", "v_full", "scored", "turned",
             "valued", "folded", "y_full", "x_turned", "qk_full", "rot_full", "shifted", "restored", "normed",
             "up_full", "down_full", "rel_full", "logit_full", "choice_full", "picked", "gate_full", "o3_full", "v2_full", "valued2",
             "b2_full"))
        (sig_ready, qT_ready, ot_stored, k_split, exped, pt_ready, o_ready, xt_ready, squared, raw_ready, v2_ready, qm_ready,
         kt_ready, pm_ready, ot_ready, hs_ready, h2_ready, act_ready, yf_ready, rel_ready, choice_ready,
         gt_ready) = (tsem(n) for n in (
             "sig_ready", "qT_ready", "ot_stored", "k_split", "exped", "pt_ready", "o_ready", "xt_ready", "squared", "raw_ready",
             "v2_ready", "qm_ready", "kt_ready", "pm_ready", "ot_ready", "hs_ready", "h2_ready", "act_ready",
             "yf_ready", "rel_ready", "choice_ready", "gt_ready"))
        (z_ready, ss_ready, qk_ready, vw_ready, am_ready, q_split, v_split, capped, mx_ready, centered, on_ready,
         var_ready, x_ready, summed, m2_ready, rotated, zr_ready, sum_ready, x1_ready, back_used, hn_ready, h_ready, rel_added, y_used,
         inp_ready, ema_ready, lg_ready, one_ready, xs_ready, xe_ready, o3_used, gap_ready, acc_ready) = (
             tsem(n) for n in (
                 "z_ready", "ss_ready", "qk_ready", "vw_ready", "am_ready", "q_split", "v_split", "capped",
                 "mx_ready", "centered", "on_ready", "var_ready", "x_ready", "summed", "m2_ready", "rotated", "zr_ready", "sum_ready",
                 "x1_ready", "back_used", "hn_ready", "h_ready", "rel_added", "y_used", "inp_ready", "ema_ready", "lg_ready",
                 "one_ready", "xs_ready", "xe_ready", "o3_used", "gap_ready", "acc_ready"))
        (sq_ready, rn_ready, vj_ready, oth_ready, xb_ready, on_clear, pcentered, rstd_ready, m1_ready, pn_ready,
         zeroed, ew_ready) = (tsem(n) for n in (
             "sq_ready", "rn_ready", "vj_ready", "oth_ready", "xb_ready", "on_clear", "pcentered", "rstd_ready",
             "m1_ready", "pn_ready", "zeroed", "ew_ready"))

        att = {
            "x0": dict(i=0, heads=16, scale=P ** -0.5, mask=0, ctx=True),
            "a1": dict(i=1, heads=16, scale=8 ** -0.5, mask=None, ctx=False),
            "x1": dict(i=2, heads=16, scale=8 ** -0.5, mask=None, ctx=True),
            "x2": dict(i=3, heads=32, scale=4 ** -0.5, mask=1, ctx=True),
            "a3": dict(i=4, heads=16, scale=8 ** -0.5, mask="rel", ctx=False),
            "x3": dict(i=5, heads=16, scale=8 ** -0.5, mask=2, ctx=True),
        }
        LAST_NORM = 12 * NT

        def tile(ap, t):
            return ap[:, t * P:(t + 1) * P]

        def PR(t):
            return pr[:, t % 2, 0:4, :, :].rearrange("p h b k -> p (h b k)")

        def bc(ap, shape, dim):
            return ap.unsqueeze(dim).to_broadcast(shape)

        block = ctx.enter_context(nc.Block())

        @block.sync
        def _(sp):
            def next_turn():
                sp.wait_ge(turn_done, 4)
                for q in turn_sems:
                    sp.sem_clear(q)
                for q in (go_pe, go_act, go_dve, go_pool):
                    sp.sem_inc(q, 1)

            sp.dma_start(W[:, 0:n_first], small[:, 0:n_first]).then_inc(first_in, 16)
            sp.dma_start(XP, xperm[:, 0:HALF]).then_inc(xp_in, 16)
            sp.dma_start(W[:, n_first:], small[:, n_first:]).then_inc(rest_in, 16)
            next_turn()
            sp.dma_start(XP, xperm[:, HALF:]).then_inc(xp_in, 16)
            next_turn()
            with sp.Fori(0, 2) as it:
                sp.dma_start(X[:, :, :], xtok[:, bass.ds(it * NT, NT), :]).then_inc(x_in, 16)
                sp.dma_start(CT[:, :], ctxT[:, bass.ds(it * HALF, HALF)]).then_inc(ctx_in, 16)
                sp.dma_start(m_row[:, :, :], mrow[:, bass.ds(it * NB, NB), :]).then_inc(masks_in, 16)
                sp.dma_start(m_col[:, :], mcol[:, bass.ds(it * NB, NB)]).then_inc(masks_in, 16)
                sp.dma_start(m_tok[:, :], mtok[:, bass.ds(it * NT, NT)]).then_inc(masks_in, 16)
                sp.dma_start(m_pad[:, :, :], pad_rows[:, bass.ds(it * NB, NB), :]).then_inc(masks_in, 16)
                sp.dma_start(m_att[:, :], att_rows).then_inc(masks_in, 16)
                sp.dma_start(m_ik[:, :, :], ik_rows[:, bass.ds(it * NB, NB), :]).then_inc(masks_in, 16)
                sp.dma_start(ew2[:, :, :], exw[:, bass.ds(it * NT, NT), :]).then_inc(ew_in, 16)
                a1, a2 = eat["f1.wqkv"][0], eat["g.w1"][0]
                sp.dma_start(big[:, 0:a1], early[:, 0:a1]).then_inc(f0_in, 16)
                sp.dma_start(big[:, a1:a2], early[:, a1:a2]).then_inc(f1_in, 16)
                sp.dma_start(big[:, a2:ewidth], early[:, a2:ewidth]).then_inc(g_in, 16)
                sp.wait_ge(down_full, 3)
                for e in range(0, NE2, 4):
                    sp.dma_start(gu_w[:, e:e + 4, :], gup[e:e + 4].rearrange("e p n -> p e n")).then_inc(e2_in, 16)
                    for c in range(2):
                        sp.dma_start(dn_w[:, e:e + 4, c, :], down[e:e + 4, c * P:(c + 1) * P, :].rearrange(
                            "e p n -> p e n")).then_inc(e2_in, 16)
                sp.wait_ge(down_full, 4)
                for e in range(0, NE3, 4):
                    sp.dma_start(w1_w[:, e:e + 4, :], e3w1[e:e + 4].rearrange("e p n -> p e n")).then_inc(e3_in, 16)
                    for c in range(4):
                        sp.dma_start(w2_w[:, e:e + 4, c, :], e3w2[e:e + 4, c * P:(c + 1) * P, :].rearrange(
                            "e p n -> p e n")).then_inc(e3_in, 16)
                for b in range(NB + 1):
                    if b < NB:
                        sp.wait_ge(rel_ready, b + 1)
                        sp.dma_start(scratch.ap()[b].rearrange("(p n) -> p n", n=512),
                                     G[:, b % 4, :]).then_inc(rel_stored[b % 2], 16)
                    if b >= 1:
                        sp.wait_ge(rel_stored[(b - 1) % 2], 16 * ((b - 1) // 2 + 1))
                        if b - 1 >= 4:
                            sp.wait_ge(rel_added, b - 4)
                        for c in range(2):
                            skew = bass.AP(tensor=scratch, offset=(b - 1) * P * 512 + c * S * 512 + S - 1,
                                           ap=[[511, S], [1, 512]])
                            sp.dma_start(RB[(b - 1) % 4][c * S:(c + 1) * S, :], skew).then_inc(
                                rel_back[(b - 1) % 4], 16)
                for t in range(NT):
                    sp.wait_ge(x_ready, LAST_NORM - NT + t + 1)
                    sp.dma_start(out[:, bass.ds(it * NT + t, 1), :], X[:, t:t + 1, :]).then_inc(out_sent, 16)
                sp.wait_ge(out_sent, 16 * NT)
                next_turn()

        @block.tensor
        def _(pe):
            due = Tally()
            hold = {}

            def fill(b, used_by):
                if b in hold:
                    pe.wait_ge(*hold[b])
                hold[b] = (used_by, due(used_by))
                return bank[b]

            def end_of_turn():
                pe.drain().then_inc(turn_done, 1)
                pe.wait_ge(go_pe, 1)
                pe.sem_clear(go_pe)
                hold.clear()
                due.count.clear()

            mm = pe.matmul
            ident = w("ident")
            pe.wait_ge(first_in, 16)
            with pe.Fori(0, 2):
                pe.wait_ge(xp_in, 16)
                for step, g in lagged(MIX0, 4):
                    j = g % 2
                    if step == "project":
                        ps = fill(j, z_ready)
                        mm(ps[:, 0:416], tile(XP, g), w("Aw"), start=True, stop=True).then_inc(proj_full, 1)
                    if step == "state":
                        pe.wait_ge(qk_ready, due(qk_ready))
                        pe.transpose(fill(2, qT_ready)[:, 0:P], QK[:, j, 0:P], ident).then_inc(qT_full, 1)
                        pe.wait_ge(vj_ready, due(vj_ready))
                        for h in range(2):
                            mm(fill(4 + h, am_ready)[:, :], QK[:, j, P:2 * P],
                               VJ[:, j, 4 * h:4 * h + 4, :].rearrange("p s n -> p (s n)"),
                               start=True, stop=True).then_inc(state_full, 1)
                    if step == "mix":
                        pe.wait_ge(am_ready, 2 * g + 2)
                        pe.wait_ge(qT_ready, g + 1)
                        ps = fill(6, ot_stored)
                        for c in range(8):
                            last = mm(ps[:, 16 * c:16 * c + 16], AM[:, j, c, :], QTp[:, j, 16 * c:16 * c + 16],
                                      start=True, stop=True)
                        last.then_inc(mix_full, 1)
                end_of_turn()

            def x_to_features(src, t):
                pe.transpose(fill(5, xt_ready)[:, 0:P], src[:, t, :], ident).then_inc(x_turned, 1)

            def attention(name):
                a = att[name]
                src = CT if a["ctx"] else XT
                subs = a["heads"] // 16
                units = subs * NT
                n = 16 if subs == 1 else 8
                V, blk = (VX, 34) if subs == 1 else (VX32, 18)
                if not a["ctx"]:
                    pe.wait_ge(*hold[5])
                ps = fill(5, k_split)
                if subs == 2:
                    due(k_split)
                    hold[5] = (k_split, due.now(k_split))
                mm(ps[:, :], w(f"{name}.k"), src[:, :], start=True, stop=True).then_inc(k_full, 1)
                k_done = due.now(k_split)
                ps = fill(6, v_split)
                for t in range(NT):
                    last = mm(tile(ps, t), tile(src, t), w(f"{name}.v"), start=True, stop=True)
                last.then_inc(v_full, 1)
                pe.wait_ge(xt_ready, due.now(xt_ready))
                ps = fill(4, q_split)
                mm(ps[:, :], w(f"{name}.q"), XT[:, :], start=True, stop=True).then_inc(q_full, 1)
                pe.wait_ge(*hold[4])
                if name == "a3":
                    for b in range(NB):
                        ps = fill(4 if b % 2 == 0 else 6, rel_ready)
                        mm(ps[:, :], Q[:, b, :, :].rearrange("p c q -> p (c q)"),
                           relp[:, :, :].rearrange("p h k -> p (h k)"), start=True, stop=True).then_inc(rel_full, 1)
                freed = {None: centered, "rel": rel_added}.get(a["mask"], capped)
                pt_at = {}
                on_at = {}
                for step, u in attention_order(units, NT):
                    s_, t = divmod(u, NT)
                    if step == "scores":
                        if t == 0:
                            pe.wait_ge(k_split, k_done - (subs - 1 - s_))
                        for b in range(2):
                            ps = fill(b, freed)
                            mm(ps[:, :].rearrange("p (h k) -> p h k", h=8),
                               Q[:, 2 * t + b, :, :].rearrange("p c q -> p (c q)"),
                               pairs[:, :, (2 * t + b) * S:(2 * t + b + 1) * S],
                               start=True, stop=True).then_inc(scored, 1)
                    if step == "turn":
                        pe.wait_ge(exped, due(exped, 2))
                        for h in range(2):
                            ps = fill(2 + h, pt_ready)
                            for p in range(4):
                                last = pe.transpose(tile(ps, p), pr[:, u % 2, 4 * h + p, :, :].rearrange(
                                    "p b k -> p (b k)"), ident)
                            last.then_inc(turned, 1)
                        pt_at[u] = due.now(pt_ready)
                    if step == "values":
                        pe.wait_ge(pt_ready, pt_at[u])
                        if u == 0:
                            pe.wait_ge(v_split, due.now(v_split))
                        ps = fill(6, on_ready)
                        for p in range(8):
                            last = mm(ps[:, p * blk:(p + 1) * blk], pT[:, u % 2, p, :], V[:, t, 8 * s_ + p, :],
                                      start=True, stop=True)
                        last.then_inc(valued, 1)
                        on_at[t] = due.now(on_ready)
                    if step == "fold":
                        pe.wait_ge(on_ready, on_at[u])
                        ps = fill(4, o_ready)
                        for b in range(2):
                            last = mm(ps[:, b * S:(b + 1) * S], ON[:, u, b, :], w("fold"), start=True, stop=True)
                        last.then_inc(folded, 1)
                    if step == "residual":
                        pe.wait_ge(o_ready, due.now(o_ready) - (min(u + 1, NT - 1) - u))
                        mm(fill(7, y_used)[:, 0:P], oT[:, u % 2, :], w(f"{name}.o"), start=True, stop=True).then_inc(y_full, 1)
                    if step == "finish":
                        pe.wait_ge(x_ready, due(x_ready))
                        x_to_features(X, u)

            def tail():
                pe.wait_ge(yf_ready, due.now(yf_ready))
                for step, t in lagged(TAIL, NT):
                    if step == "back":
                        pe.transpose(fill(7, y_used)[:, 0:P], tile(YF, t), ident).then_inc(y_full, 1)
                    if step == "finish":
                        pe.wait_ge(x_ready, due(x_ready))
                        x_to_features(X, t)

            def first_ffn(l):
                pe.wait_ge(f0_in if l == 0 else f1_in, 16)
                o = {}
                for t in range(NT):
                    pe.wait_ge(xt_ready, due.now(xt_ready) - (NT - 1 - t))
                    h = HT[:, 2 * t:2 * t + 2, :].rearrange("p b k -> p (b k)")
                    for i in range(2):
                        mm(fill(4 * (1 - t % 2) + i, raw_ready)[:, :], h,
                           early_w(f"f{l}.wqkv", 512 * i, 512 * i + 512), start=True, stop=True).then_inc(qk_full, 1)
                    mm(fill(6 + t % 2, v2_ready)[:, :], h, early_w(f"f{l}.wqkv", 1024, 1536),
                       start=True, stop=True).then_inc(v2_full, 1)
                    o["v", t] = due.now(v2_ready)
                for step, t in lagged(LOCAL, NT):
                    if step == "turn_qk":
                        for i, used in enumerate((qm_ready, kt_ready)):
                            pe.wait_ge(zr_ready, due(zr_ready))
                            ps = fill(2 + i, used)
                            for p in range(4):
                                last = pe.transpose(tile(ps, p), RAW[:, t, i, p * P:(p + 1) * P], ident)
                            last.then_inc(rot_full, 1)
                            o["qk"[i], t] = due.now(used)
                    if step == "scores":
                        pe.wait_ge(qm_ready, o["q", t])
                        pe.wait_ge(kt_ready, o["k", t])
                        ps = fill(0, capped)
                        for p in range(4):
                            for b in range(2):
                                last = mm(ps[:, p * P + b * S:p * P + (b + 1) * S],
                                          QMs[t % 2][:, p, b, :, :].rearrange("p c q -> p (c q)"),
                                          KT[t % 2][:, p, b * S:(b + 1) * S], start=True, stop=True)
                        last.then_inc(scored, 1)
                    if step == "turn":
                        pe.wait_ge(pn_ready, due(pn_ready))
                        ps = fill(2, pm_ready)
                        for p in range(4):
                            last = pe.transpose(tile(ps, p), PR(t)[:, p * P:(p + 1) * P], ident)
                        last.then_inc(turned, 1)
                        o["p", t] = due.now(pm_ready)
                    if step == "values":
                        pe.wait_ge(pm_ready, o["p", t])
                        pe.wait_ge(v2_ready, o["v", t])
                        for h, b in enumerate((1, 6)):
                            ps = fill(b, ot_ready)
                            for p in (2 * h, 2 * h + 1):
                                last = mm(ps[:, (p % 2) * 256:(p % 2) * 256 + 256], VS[:, t, p * P:(p + 1) * P],
                                          PM[:, p, :, :].rearrange("p b n -> p (b n)"), start=True, stop=True)
                            last.then_inc(valued2, 1)
                        o["o", t] = due.now(ot_ready)
                    if step == "out":
                        pe.wait_ge(ot_ready, o["o", t])
                        ps = fill(7, x1_ready)
                        o["x", t] = due.now(x1_ready)
                        for p in range(4):
                            last = mm(ps[:, 0:P], oT0[:, t % 2, p, :, :].rearrange("p b q -> p (b q)"),
                                      early_w(f"f{l}.wo", p * P, (p + 1) * P), start=(p == 0), stop=(p == 3))
                        last.then_inc(y_full, 1)
                    if step == "shift":
                        pe.wait_ge(x1_ready, o["x", t])
                        pe.transpose(fill(3, hs_ready)[:, 0:P], X1[:, t, :], ident).then_inc(shifted, 1)
                        o["s", t] = due.now(hs_ready)
                    if step == "stats":
                        pe.wait_ge(hs_ready, o["s", t])
                        pe.transpose(fill(3, back_used)[:, 0:P], HS[:, t % 2, :, :].rearrange("p b k -> p (b k)"),
                                     ident).then_inc(restored, 1)
                    if step == "norm":
                        pe.wait_ge(hn_ready, due(hn_ready))
                        pe.transpose(fill(3, h2_ready)[:, 0:P], res[:, t % 2, :], ident).then_inc(normed, 1)
                pe.wait_ge(h2_ready, due.now(h2_ready))
                due(exped, NT)

                def up(c):
                    a, n = CH[c]
                    for i, b in enumerate((4, 5)):
                        ps = fill(b, h_ready if i == 0 else act_ready)
                        mm(ps[0:n, :], early_w(f"f{l}.w1", i * HID + a, i * HID + a + n), XT[:, :],
                           start=True, stop=True).then_inc(up_full, 1)

                def down_(c):
                    _, n = CH[c]
                    pe.wait_ge(h_ready, due.now(h_ready) - (min(c + 1, 2) - c))
                    ps = fill(6, yf_ready) if c == 0 else OB
                    last = mm(ps[:, :], early_w(f"f{l}.w2", c * P, (c + 1) * P)[0:n, :], sm[0:n, c, :],
                              start=(c == 0), stop=(c == 2))
                    if c == 2:
                        last.then_inc(down_full, 1)
                up(0)
                up(1)
                down_(0)
                up(2)
                down_(1)
                down_(2)
                pe.wait_ge(yf_ready, due.now(yf_ready))
                if l == 1:
                    for step, t in lagged(TAIL, NT):
                        if step == "back":
                            pe.transpose(fill(7, y_used)[:, 0:P], tile(YF, t), ident).then_inc(y_full, 1)
                        if step == "finish":
                            pe.wait_ge(x_ready, due(x_ready))
                            x_to_features(X, t)
                    return
                for step, t in lagged(["back", "residual"], NT):
                    if step == "back":
                        pe.transpose(fill(7, x1_ready)[:, 0:P], tile(YF, t), ident).then_inc(y_full, 1)
                        o["x", t] = due.now(x1_ready)
                    if step == "residual":
                        pe.wait_ge(x1_ready, o["x", t])
                        x_to_features(XB, t)

            def gelu_ffn():
                pe.wait_ge(g_in, 16)
                pe.wait_ge(*hold[5])
                for c in range(9):
                    if c < 8:
                        mm(fill(4 + c % 2, act_ready)[:, :], early_w("g.w1", c * P, (c + 1) * P), XT[:, :],
                           start=True, stop=True).then_inc(up_full, 1)
                    if c >= 1:
                        pe.wait_ge(act_ready, due.now(act_ready) - (1 if c < 8 else 0))
                        ps = fill(6, yf_ready) if c == 1 else OB
                        last = mm(ps[:, :], early_w("g.w2", (c - 1) * P, c * P), G[:, (c - 1) % 4, :],
                                  start=(c == 1), stop=(c == 8))
                last.then_inc(down_full, 1)
                tail()

            def ema():
                pe.wait_ge(inp_ready, due(inp_ready))
                mm(fill(4, act_ready)[:, :], w("ema.in"), YF[:, :], start=True, stop=True).then_inc(up_full, 1)
                pe.wait_ge(ema_ready, due(ema_ready))
                for step, t in lagged(TAIL, NT):
                    if step == "back":
                        mm(fill(7, y_used)[:, 0:P], tile(G[:, 1, :], t), w("ema.out"), start=True, stop=True).then_inc(y_full, 1)
                    if step == "finish":
                        pe.wait_ge(x_ready, due(x_ready))
                        x_to_features(X, t)

            def logits(name, n):
                pe.wait_ge(*hold[5])
                ps = fill(6, lg_ready)
                for t in range(NT):
                    last = mm(ps[:, t * n:(t + 1) * n], tile(XT, t), w(name), start=True, stop=True)
                last.then_inc(logit_full, 1)

            def top1_ffn():
                logits("e2.r", NE2)
                h_at, up_at = {}, {}

                def up(k):
                    if k == 0:
                        rhs = XT[:, :]
                    else:
                        pe.wait_ge(xe_ready, k)
                        rhs = G[:, k % 2, :]
                    for c in range(2):
                        for i, b in enumerate((4 + c, 2 + c)):
                            ps = fill(b, act_ready if i == 0 else h_ready)
                            lhs = (w("e2.g" if i == 0 else "e2.u", c * P, (c + 1) * P) if k == 0 else
                                   gu_w[:, k - 1, i * NF2 + c * P:i * NF2 + (c + 1) * P])
                            mm(ps[:, :], lhs, rhs, start=True, stop=True).then_inc(up_full, 1)
                    h_at[k] = due.now(h_ready)

                def choose(k):
                    mm(fill(0, xe_ready)[:, :], pick[:, k - 1, :], oneT[:, :], start=True,
                       stop=True).then_inc(picked, 1)

                def down_(k):
                    pe.wait_ge(h_ready, h_at[k])
                    for c in range(2):
                        first, stop = (k == 0 and c == 0), (k == NE2 and c == 1)
                        ps = fill(6, yf_ready) if first else OB
                        lhs = w("e2.d", c * P, (c + 1) * P) if k == 0 else dn_w[:, k - 1, c, :]
                        last = mm(ps[:, :], lhs, sm[:, 2 * (k % 2) + c, :], start=first, stop=stop)
                    if k == NE2:
                        last.then_inc(down_full, 1)

                up(0)
                down_(0)
                pe.wait_ge(one_ready, due(one_ready))
                ps = fill(1, choice_ready)
                for t in range(NT):
                    last = pe.transpose(ps[0:NE2, t * P:(t + 1) * P], one[:, t, :], ident)
                last.then_inc(choice_full, 1)
                pe.wait_ge(xs_ready, due(xs_ready))
                for t in range(NT):
                    x_to_features(XB, t)
                pe.wait_ge(*hold[1])
                pe.wait_ge(e2_in, 16 * 12)
                choose(1)
                for k in range(1, NE2 + 1):
                    up(k)
                    if k < NE2:
                        choose(k + 1)
                    if k >= 2:
                        down_(k - 1)
                down_(NE2)
                tail()

            def top2_ffn():
                logits("e3.r", NE3)
                act_at = {}

                def up(e):
                    for c in range(4):
                        mm(fill(4 + c % 2, act_ready)[:, :], w1_w[:, e, c * P:(c + 1) * P], XT[:, :],
                           start=True, stop=True).then_inc(up_full, 1)
                    act_at[e] = due.now(act_ready)

                def down_(e):
                    pe.wait_ge(act_ready, act_at[e])
                    h = G if e % 2 == 0 else sm
                    ps = fill(2 + e % 2, o3_used)
                    for t in range(NT):
                        for c in range(4):
                            last = mm(tile(ps, t), tile(h[:, c, :], t), w2_w[:, e, c, :],
                                      start=(c == 0), stop=(c == 3))
                    last.then_inc(o3_full, 1)

                pe.wait_ge(e3_in, 16 * 10)
                up(0)
                pe.wait_ge(one_ready, due(one_ready))
                ps = fill(0, gt_ready)
                for t in range(NT):
                    last = pe.transpose(ps[0:NE3, t * P:(t + 1) * P], gate[:, t, 0:NE3], ident)
                last.then_inc(gate_full, 1)
                pe.wait_ge(*hold[0])
                ps = fill(1, acc_ready)
                for t in range(NT):
                    last = mm(tile(ps, t), tile(gT, t), w("e3.b2")[0:NE3, :], start=True, stop=True)
                last.then_inc(b2_full, 1)
                for e in range(1, NE3 + 1):
                    if e < NE3:
                        up(e)
                    down_(e - 1)

            pe.wait_ge(rest_in, 16)
            pe.wait_ge(init_pool, 1)
            pe.wait_ge(init_dve, 1)
            with pe.Fori(0, 2):
                pe.wait_ge(oth_ready, due(oth_ready))
                for step, t in lagged(TAIL, NT):
                    if step == "back":
                        mm(fill(7, y_used)[:, 0:P], tile(OTh, t), w("Ao"), start=True, stop=True).then_inc(y_full, 1)
                    if step == "finish":
                        pe.wait_ge(x_ready, due(x_ready))
                        x_to_features(X, t)
                pe.wait_ge(ctx_in, 16)
                attention("x0")
                first_ffn(0)
                first_ffn(1)
                attention("a1")
                attention("x1")
                gelu_ffn()
                ema()
                attention("x2")
                top1_ffn()
                attention("a3")
                attention("x3")
                top2_ffn()
                end_of_turn()

        @block.scalar
        def _(act):
            due = Tally()

            def end_of_turn():
                act.drain().then_inc(turn_done, 1)
                act.wait_ge(go_act, 1)
                act.sem_clear(go_act)
                due.count.clear()

            def inverse_roots(dst, src):
                act.wait_ge(ss_ready, due(ss_ready))
                act.activation(src, src, ACT.Ln).then_inc(act_link, 1)
                act.wait_ge(act_link, due(act_link))
                act.activation(dst, src, ACT.Exp, scale=-0.5).then_inc(rn_ready, 1)

            act.wait_ge(first_in, 16)
            with act.Fori(0, 2) as it:
                for step, g in lagged(MIX0, 4):
                    j = g % 2
                    if step == "project":
                        act.wait_ge(z_ready, g + 1)
                        act.activation(SQ[:, j, :], Z[:, j, 0:256], ACT.Square).then_inc(sq_ready, 1)
                        act.activation(SG[:, j, :], Z[:, j, 384:416], ACT.Exp, scale=-1.0).then_inc(sig_ready, 1)
                        inverse_roots(RN[:, j, :], SS[:, j, :])
                    if step == "state":
                        act.wait_ge(qT_full, g + 1)
                        act.copy(QTp[:, j, :], T0[:, 0:P]).then_inc(qT_ready, 1)
                    if step == "mix":
                        act.wait_ge(mix_full, g + 1)
                        act.copy(OTall[:, :, bass.ds(it * 32 + g * 8, 8)],
                                 OB[:, 0:P].rearrange("p (j i) -> p i j", i=16)).then_inc(ot_stored, 1)
                end_of_turn()

            def stream_out(t, shifted_too):
                act.wait_ge(x_turned, due(x_turned))
                if shifted_too:
                    src = F1[:, 0:P].rearrange("p (b k) -> p b k", b=2)
                    act.copy(HT[0:S, 2 * t:2 * t + 2, :], src[0:S])
                    act.copy(HT[S:P, 2 * t:2 * t + 2, 1:S], src[S:P, :, 0:S - 1]).then_inc(xt_ready, 1)
                else:
                    act.copy(tile(XT, t), F1[:, 0:P]).then_inc(xt_ready, 1)

            def attention(name, shift_out=False):
                a = att[name]
                subs = a["heads"] // 16
                units = subs * NT
                pair = w("pair16") if subs == 1 else w("pair32")
                ready = centered if a["mask"] is None else pcentered

                def split_keys(s_):
                    for p in range(8):
                        g = 8 * s_ + p
                        last = act.activation(pairs[:, p, :], F1[:, :], ACT.Identity, bias=bkm[:, a["i"], g:g + 1],
                                              scale=pair[:, g:g + 1])
                    last.then_inc(k_split, 1)
                act.wait_ge(k_full, due(k_full))
                split_keys(0)
                if name == "a3":
                    for b in range(NB):
                        act.wait_ge(rel_full, b + 1)
                        if b >= 4:
                            act.wait_ge(rel_stored[b % 2], 16 * ((b - 4) // 2 + 1))
                        act.copy(G[:, b % 4, :], (F0 if b % 2 == 0 else OB)[:, :]).then_inc(rel_ready, 1)
                for step, u in attention_order(units, NT):
                    s_, t = divmod(u, NT)
                    if step == "scores":
                        if s_ > 0 and t == 0:
                            act.wait_ge(scored, due.now(scored))
                            split_keys(1)
                        for b in range(2):
                            due(scored)
                            act.wait_ge(ready, due(ready))
                            act.activation(pr[:, u % 2, :, b, :],
                                           sm[:, 2 * (u % 2) + b, :].rearrange("p (h k) -> p h k", h=8),
                                           ACT.Exp, scale=a["scale"]).then_inc(exped, 1)
                    if step == "turn":
                        for h in range(2):
                            act.wait_ge(turned, due(turned))
                            act.copy(pT[:, u % 2, 4 * h:4 * h + 4, :],
                                     bank[2 + h][:, :].rearrange("p (h n) -> p h n", h=4)).then_inc(pt_ready, 1)
                    if step == "fold":
                        act.wait_ge(folded, due(folded))
                        act.copy(oT[:, u % 2, :], F0[:, 0:P]).then_inc(o_ready, 1)
                    if step == "finish":
                        stream_out(u, shift_out)

            def tail(bias=None, shift_out=False, steps=TAIL, start=True):
                if start:
                    act.wait_ge(down_full, due(down_full))
                    if bias is None:
                        act.copy(YF[:, :], OB[:, :]).then_inc(yf_ready, 1)
                    else:
                        act.activation(YF[:, :], OB[:, :], ACT.Identity, bias=bias).then_inc(yf_ready, 1)
                for step, t in lagged(steps, NT):
                    if step == steps[-1]:
                        stream_out(t, shift_out)

            def first_ffn(l):
                for t in range(NT):
                    for i in range(2):
                        u = 2 * t + i
                        if u >= 4:
                            act.wait_ge(summed, 2 * NT * l + u - 3)
                        act.wait_ge(qk_full, due(qk_full))
                        act.activation(sm[:, u % 4, :], bank[4 * (1 - t % 2) + i][:, :], ACT.Square).then_inc(squared, 1)
                        act.copy(RAW[:, t, i, :], bank[4 * (1 - t % 2) + i][:, :]).then_inc(raw_ready, 1)
                    act.wait_ge(v2_full, due(v2_full))
                    act.copy(VS[:, t, :], bank[6 + t % 2][:, :]).then_inc(v2_ready, 1)
                inverse_roots(rn[:, :, :], ss[:, :, :])
                if l == 0:
                    act.wait_ge(zeroed, 2)
                for step, t in lagged(LOCAL, NT):
                    if step == "turn_qk":
                        if t >= 2:
                            act.wait_ge(scored, due(scored))
                        act.wait_ge(rot_full, due(rot_full))
                        for c in range(2):
                            r = slice(c * S, (c + 1) * S)
                            last = act.copy(QMs[t % 2][r, :, :, c, :].rearrange("p a b q -> p (a b) q"),
                                            T0[r, :].rearrange("p (a q) -> p a q", q=S))
                        last.then_inc(qm_ready, 1)
                        act.wait_ge(rot_full, due(rot_full))
                        act.copy(KT[t % 2], T1[:, :].rearrange("p (a n) -> p a n", a=4)).then_inc(kt_ready, 1)
                    if step == "scores":
                        if t >= 2:
                            act.wait_ge(turned, due.now(turned) + 1)
                        act.wait_ge(pcentered, due(pcentered))
                        act.activation(PR(t), sm[:, t % 2, :], ACT.Exp,
                                       scale=8.0).then_inc(exped, 1)
                    if step == "turn":
                        if t >= 1:
                            act.wait_ge(valued2, 2 * (NT * l + t))
                        act.wait_ge(turned, due(turned))
                        for b in range(2):
                            r = slice(b * S, (b + 1) * S)
                            last = act.copy(PM[r, :, b, :], T0[r, :].rearrange("p (a n) -> p a n", a=4))
                        last.then_inc(pm_ready, 1)
                    if step == "values":
                        for h, bk in enumerate((S1, OB)):
                            act.wait_ge(valued2, 2 * (NT * l + t) + h + 1)
                            for c in range(2):
                                r = slice(c * S, (c + 1) * S)
                                last = act.copy(
                                    oT0[r, t % 2, 2 * h:2 * h + 2, :, :].rearrange("p a b q -> p (a b) q"),
                                    bk[r, :].rearrange("p (a c q) -> p a c q", c=2, q=S)[:, :, c, :])
                            last.then_inc(ot_ready, 1)
                    if step == "shift":
                        act.wait_ge(shifted, due(shifted))
                        src = T1[:, 0:P].rearrange("p (b k) -> p b k", b=2)
                        act.copy(HS[0:S, t % 2, :, :], src[0:S])
                        act.copy(HS[S:P, t % 2, :, 1:S], src[S:P, :, 0:S - 1]).then_inc(hs_ready, 1)
                    if step == "norm":
                        act.wait_ge(normed, due(normed))
                        act.activation(tile(XT, t), T1[:, 0:P], ACT.Identity, bias=w(f"f{l}.b"),
                                       scale=w(f"f{l}.g")).then_inc(h2_ready, 1)
                due(scored, 2)
                for c in range(3):
                    n = CH[c][1]
                    act.wait_ge(up_full, due(up_full, 2))
                    act.activation(sm[0:n, c, :], F1[0:n, :], ACT.Gelu,
                                   bias=w(f"f{l}.b1g", c, c + 1)[0:n]).then_inc(act_ready, 1)
                if l == 0:
                    tail(w("f0.b2"), shift_out=True, steps=["back", "residual"])
                else:
                    tail(w("f1.b2"))

            def gelu_ffn():
                for c in range(8):
                    act.wait_ge(up_full, due(up_full))
                    act.activation(G[:, c % 4, :], bank[4 + c % 2][:, :], ACT.Gelu_apprx_tanh).then_inc(act_ready, 1)
                tail()

            def ema():
                act.wait_ge(up_full, due(up_full))
                act.activation(G[:, 0, :], F0[:, :], ACT.Relu, bias=w("ema.bin")).then_inc(act_ready, 1)
                tail(start=False)

            def top1_ffn():
                def gates(k):
                    for c in range(2):
                        act.wait_ge(up_full, due(up_full))
                        act.activation(sm[:, 2 * (k % 2) + c, :], bank[4 + c][:, :], ACT.Silu).then_inc(act_ready, 1)
                        due(up_full)
                act.wait_ge(lg_ready, due(lg_ready))
                act.activation(sig[:, :, :], lg[:, :, :], ACT.Sigmoid).then_inc(sig_ready, 1)
                gates(0)
                act.wait_ge(choice_full, due(choice_full))
                act.copy(oneT[:, :], S1[0:NE2, :]).then_inc(choice_ready, 1)
                for t in range(NT):
                    act.wait_ge(x_turned, due(x_turned))
                    act.copy(HT[:, 2 * t:2 * t + 2, :].rearrange("p b k -> p (b k)"), F1[:, 0:P]).then_inc(xt_ready, 1)
                for k in range(1, NE2 + 1):
                    gates(k)
                tail()

            def top2_ffn():
                due(lg_ready)

                def gelus(e):
                    h = G if e % 2 == 0 else sm
                    for c in range(4):
                        act.wait_ge(up_full, due(up_full))
                        act.activation(h[:, c, :], bank[4 + c % 2][:, :], ACT.Gelu,
                                       bias=w("e3.b1", 4 * e + c, 4 * e + c + 1)).then_inc(act_ready, 1)
                act.wait_ge(gap_ready, due(gap_ready))
                act.activation(col[:, 4, :], col[:, 3, :], ACT.Exp).then_inc(sig_ready, 1)
                gelus(0)
                act.wait_ge(gate_full, due(gate_full))
                act.copy(gT[:, :], S0[0:NE3, :]).then_inc(gt_ready, 1)
                for e in range(1, NE3):
                    gelus(e)

            act.wait_ge(rest_in, 16)
            act.wait_ge(init_dve, 1)
            act.wait_ge(init_pool, 1)
            with act.Fori(0, 2):
                act.wait_ge(zeroed, 1)
                tail(start=False)
                attention("x0", shift_out=True)
                first_ffn(0)
                first_ffn(1)
                attention("a1")
                attention("x1")
                gelu_ffn()
                ema()
                attention("x2")
                top1_ffn()
                attention("a3")
                attention("x3")
                top2_ffn()
                end_of_turn()

        @block.vector
        def _(dve):
            due = Tally()

            def link(ins):
                ins.then_inc(dve_link, 1)
                dve.wait_ge(dve_link, due(dve_link))

            def end_of_turn():
                dve.drain().then_inc(turn_done, 1)
                dve.wait_ge(go_dve, 1)
                dve.sem_clear(go_dve)
                due.count.clear()

            tt, ts, stt = dve.tensor_tensor, dve.tensor_scalar, dve.scalar_tensor_tensor
            dve.wait_ge(first_in, 16)
            with dve.Fori(0, 2):
                for step, g in lagged(MIX0, 4):
                    j = g % 2
                    if step == "project":
                        if g >= 2:
                            dve.wait_ge(sig_ready, g - 1)
                            dve.wait_ge(vw_ready, g - 1)
                        dve.wait_ge(proj_full, g + 1)
                        tt(Z[:, j, :], bank[j][:, 0:416], w("Ab"), ALU.add).then_inc(z_ready, 1)
                        dve.wait_ge(sq_ready, g + 1)
                        link(dve.tensor_reduce(SS[:, j, :], SQ[:, j, :].rearrange("p (h d) -> p h d", d=8), AX.X,
                                               ALU.add))
                        ts(SS[:, j, :], SS[:, j, :], 1e-24, None, ALU.max).then_inc(ss_ready, 1)
                    if step == "scale":
                        dve.wait_ge(rn_ready, g + 1)
                        dve.wait_ge(sig_ready, g + 1)
                        if g >= 2:
                            dve.wait_ge(vj_ready, g - 1)
                            dve.wait_ge(state_full, 2 * g - 2)
                        link(ts(SG[:, j, :], SG[:, j, :], 1.0, None, ALU.add))
                        link(dve.reciprocal(SG[:, j, :], SG[:, j, :]))
                        link(tt(RN[:, j, 0:16], RN[:, j, 0:16], SG[:, j, 16:32], ALU.mult))
                        tt(QK[:, j, :].rearrange("p (h d) -> p h d", d=8),
                           Z[:, j, 0:256].rearrange("p (h d) -> p h d", d=8),
                           bc(RN[:, j, :], [P, 32, 8], 2), ALU.mult).then_inc(qk_ready, 1)
                        tt(VW[:, j, :].rearrange("p (h d) -> p h d", d=8),
                           Z[:, j, 256:384].rearrange("p (h d) -> p h d", d=8),
                           bc(SG[:, j, 0:16], [P, 16, 8], 2), ALU.mult).then_inc(vw_ready, 1)
                    if step == "state":
                        if g >= 2:
                            dve.wait_ge(mix_full, g - 1)
                        for h in range(2):
                            dve.wait_ge(state_full, 2 * g + h + 1)
                            tt(AM[:, j, 4 * h:4 * h + 4, :], bank[4 + h][:, :].rearrange("p (s n) -> p s n", s=4),
                               bc(w("blocks"), [P, 4, P], 1), ALU.mult).then_inc(am_ready, 1)
                end_of_turn()

            dve.wait_ge(rest_in, 16)
            for name in ATT:
                a = att[name]
                n = a["heads"] // 2
                ts(bkm[:, a["i"], 0:n], w("pair16") if n == 8 else w("pair32"), w(f"{name}.bk"), None, ALU.mult)
            tt(relp[:, :, :], bc(w("rel"), [P, 8, S], 1), bc(w("pair16"), [P, 8, S], 2), ALU.mult)
            for l in range(2):
                for i, (table, scale) in enumerate((("cosq", "qs"), ("sinq", "qsr"), ("cosk", "ks"), ("sink", "ksr"))):
                    tt(rot[:, l, i, :], w(table), w(f"f{l}.{scale}"), ALU.mult)
            ts(w("not_first"), w("not_first"), w("decay"), None, ALU.mult)
            ts(omix[:, :], w("mix"), -1.0, 1.0, ALU.mult, ALU.add)
            dve.tensor_copy(pick[:, :, :], bc(w("ident")[0:NE2, 0:NE2], [NE2, NE2, P], 2)).then_inc(init_dve, 1)
            dve.wait_ge(init_dve, 1)

            def stats(src, t):
                link(dve.bn_stats(st[:, t % 2, :], src))
                dve.bn_aggr(mv[:, t % 2, :], st[:, t % 2, :]).then_inc(var_ready, 1)

            def finish(src, t):
                dve.wait_ge(rstd_ready, due(rstd_ready))
                ts(X[:, t, :], src, mv[:, t % 2, 0:1], rstd[:, t % 2, :], ALU.subtract, ALU.mult).then_inc(x_ready, 1)
                due(x_ready)

            def own_norms_done():
                if due.now(x_ready):
                    dve.wait_ge(x_ready, due.now(x_ready))

            def residual(t, other):
                own_norms_done()
                dve.wait_ge(y_full, due(y_full))
                tt(res[:, t % 2, :], YB[:, 0:P], other, ALU.add).then_inc(y_used, 1)
                dve.wait_ge(y_used, due(y_used))
                stats(res[:, t % 2, :], t)

            def masks():
                dve.wait_ge(masks_in, 16 * 6)
                c0, c1, c2 = (cap[:, i, :, :] for i in range(3))
                link(tt(c0, m_row[:, :, :], bc(m_col[:, :], [P, NB, S], 2), ALU.mult))
                link(ts(c0, c0, 0.0, BIG, ALU.is_gt, ALU.mult))
                link(ts(c0, c0, -BIG, 10.0, ALU.add, ALU.mult))
                ts(c0, c0, BIG, None, ALU.add)
                link(tt(c1, m_pad[:, :, :], bc(m_att[:, :], [P, NB, S], 1), ALU.max))
                f = YF[:, :].rearrange("p (b k) -> p b k", b=NB)
                link(ts(f, c1, 0.0, BIG, ALU.is_equal, ALU.mult))
                link(stt(c1, c1, -1e9 / att["x2"]["scale"], f, ALU.mult, ALU.add))
                link(ts(f, m_ik[:, :, :], 0.0, -1e9 / att["x3"]["scale"], ALU.is_equal, ALU.mult))
                link(ts(c2, m_ik[:, :, :], 0.0, BIG, ALU.not_equal, ALU.mult))
                link(tt(c2, c2, f, ALU.add))

            def attention(name):
                a = att[name]
                subs = a["heads"] // 16
                units = subs * NT
                n = 16 if subs == 1 else 8
                d = n // 2
                V, blk = (VX, 34) if subs == 1 else (VX32, 18)
                par = w("par16") if subs == 1 else w("par32")
                dve.wait_ge(v_full, due(v_full))
                for b in range(2):
                    r = slice(b * S, (b + 1) * S)
                    last = tt(
                        V[r, :, :, b * n:(b + 1) * n],
                        OB[r, :].rearrange("p (t h d) -> p t h d", t=NT, d=n),
                        bc(w(f"{name}.bv")[r].rearrange("p (h d) -> p h d", d=n), [S, NT, P // n, n], 1), ALU.add)
                last.then_inc(v_split, 1)
                dve.wait_ge(q_full, due(q_full))
                for c in range(2):
                    last = ts(Q[:, :, c, :], F0[:, :].rearrange("p (b q) -> p b q", b=NB), w(f"{name}.bq"),
                              par[:, c:c + 1], ALU.add, ALU.mult)
                last.then_inc(q_split, 1)
                for step, u in attention_order(units, NT):
                    s_, t = divmod(u, NT)
                    if step == "scores":
                        if u >= 2:
                            dve.wait_ge(exped, due(exped, 2))
                        for b in range(2):
                            slot = 2 * (u % 2) + b
                            dve.wait_ge(scored, due(scored))
                            sc = bank[b][:, :].rearrange("p (h k) -> p h k", h=8)
                            dst = sm[:, slot, :].rearrange("p (h k) -> p h k", h=8)
                            top = mx[:, slot, :]
                            if a["mask"] is None:
                                link(dve.tensor_reduce(top, sc, AX.X, ALU.max))
                                tt(dst, sc, bc(top, [P, 8, S], 2), ALU.subtract).then_inc(centered, 1)
                                continue
                            if a["mask"] == "rel":
                                dve.wait_ge(rel_back[(2 * t + b) % 4], 32 * ((2 * t + b) // 4 + 1))
                                tt(sm[:, slot, :], bank[b][:, :], RB[(2 * t + b) % 4], ALU.add).then_inc(rel_added, 1)
                                dve.wait_ge(rel_added, due(rel_added))
                                link(tt(dst, dst, bc(w("causal"), [P, 8, S], 1), ALU.min))
                            else:
                                tt(dst, sc, bc(cap[:, a["mask"], 2 * t + b, :], [P, 8, S], 1),
                                   ALU.min).then_inc(capped, 1)
                                dve.wait_ge(capped, due(capped))
                            dve.tensor_reduce(top, dst, AX.X, ALU.max).then_inc(mx_ready, 1)
                    if step == "values":
                        dve.wait_ge(valued, due(valued))
                        o = OB[:, 0:8 * blk].rearrange("p (h n) -> p h n", h=8)
                        link(dve.reciprocal(rs[:, u % 2, :, :], o[:, :, 2 * n:2 * n + 2]))
                        if u == 0:
                            dve.wait_ge(on_clear, due(on_clear))
                        for c in range(2):
                            r = slice(c * S, (c + 1) * S)
                            src = o[r, :, 0:2 * n].rearrange("p h (b c d) -> p b c h d", b=2, c=2)
                            dst = ON[r, t, :, :].rearrange("p b (h c d) -> p b c h d", c=2, d=d)
                            last = tt(dst[:, :, c, 8 * s_:8 * s_ + 8, :], src[:, :, c, :, :],
                                      bc(rs[r, u % 2, :, :].rearrange("p h b -> p b h"), [S, 2, 8, d], 3), ALU.mult)
                        last.then_inc(on_ready, 1)
                    if step == "residual":
                        if u == 0:
                            dve.wait_ge(xb_ready, due(xb_ready))
                        if name == "x0":
                            own_norms_done()
                            dve.wait_ge(y_full, due(y_full))
                            stt(res[:, u % 2, :], YB[:, 0:P], m_tok[:, u:u + 1], XB[:, u, :], ALU.mult,
                                ALU.add).then_inc(y_used, 1)
                            dve.wait_ge(y_used, due(y_used))
                            stats(res[:, u % 2, :], u)
                        else:
                            residual(u, XB[:, u, :])
                    if step == "finish":
                        finish(res[:, u % 2, :], u)
                due(exped, 4)

            def first_ffn(l):
                cur = X if l == 0 else XB
                for u in range(2 * NT + 1):
                    if u < 2 * NT:
                        t, i = divmod(u, 2)
                        dve.wait_ge(squared, due(squared))
                        dve.tensor_reduce(ss[:, t, 8 * i:8 * i + 8],
                                          sm[:, u % 4, :].rearrange("p (h d) -> p h d", d=S), AX.X,
                                          ALU.add).then_inc(summed, 1)
                        dve.wait_ge(raw_ready, due(raw_ready))
                        z = RAW[:, t, i, :].rearrange("p (h c d) -> p h c d", h=8, c=2)
                        m = M2[:, u % 4, :].rearrange("p (h c d) -> p h c d", h=8, c=2)
                        table = rot[:, l, 2 * i + 1, :].rearrange("p (c d) -> p c d", c=2)
                        for c in range(2):
                            last = tt(m[:, :, c, :], z[:, :, 1 - c, :], bc(table[:, c, :], [P, 8, 32], 1), ALU.mult)
                        last.then_inc(m2_ready, 1)
                    if u == 2 * NT - 1:
                        dve.wait_ge(summed, due(summed, 2 * NT))
                        ts(ss[:, :, :], ss[:, :, :], 1e-24, None, ALU.max).then_inc(ss_ready, 1)
                    if u >= 1:
                        v = u - 1
                        dve.wait_ge(m1_ready, due(m1_ready))
                        dve.wait_ge(m2_ready, due(m2_ready))
                        tt(RAW[:, v // 2, v % 2, :], M1[:, v % 4, :], M2[:, v % 4, :], ALU.add).then_inc(rotated, 1)
                dve.wait_ge(rotated, due(rotated, 2 * NT))
                dve.wait_ge(rn_ready, due(rn_ready))
                for step, t in lagged(LOCAL, NT):
                    if step == "rotate":
                        for i in range(2):
                            zr = RAW[:, t, i, :].rearrange("p (h d) -> p h d", d=S)
                            tt(zr, zr, bc(rn[:, t, 8 * i:8 * i + 8], [P, 8, S], 2), ALU.mult).then_inc(zr_ready, 1)
                    if step == "scores":
                        dve.wait_ge(scored, due(scored))
                        tt(sm[:, t % 2, :].rearrange("p (h k) -> p h k", h=8),
                           S0[:, :].rearrange("p (h k) -> p h k", h=8), bc(w("causal"), [P, 8, S], 1),
                           ALU.min).then_inc(capped, 1)
                        dve.wait_ge(capped, due(capped))
                        dve.tensor_reduce(mx[:, t % 2, :], sm[:, t % 2, :].rearrange("p (h k) -> p h k", h=8), AX.X,
                                          ALU.max).then_inc(mx_ready, 1)
                    if step == "soft":
                        dve.wait_ge(exped, due(exped))
                        link(dve.tensor_reduce(mx[:, 2 + t % 2, :], PR(t).rearrange("p (g k) -> p g k", g=8), AX.X,
                                               ALU.add))
                        dve.reciprocal(mx[:, 2 + t % 2, :], mx[:, 2 + t % 2, :]).then_inc(sum_ready, 1)
                    if step == "out":
                        dve.wait_ge(y_full, due(y_full))
                        tt(X1[:, t, :], YB[:, 0:P], cur[:, t, :], ALU.add).then_inc(x1_ready, 1)
                    if step == "stats":
                        dve.wait_ge(restored, due(restored))
                        dve.tensor_copy(res[:, t % 2, :], T1[:, 0:P]).then_inc(back_used, 1)
                        dve.wait_ge(back_used, due(back_used))
                        stats(res[:, t % 2, :], t)
                    if step == "norm":
                        dve.wait_ge(rstd_ready, due(rstd_ready))
                        ts(res[:, t % 2, :], res[:, t % 2, :], mv[:, t % 2, 0:1], rstd[:, t % 2, :], ALU.subtract,
                           ALU.mult).then_inc(hn_ready, 1)
                for c in range(3):
                    n = CH[c][1]
                    dve.wait_ge(act_ready, due(act_ready))
                    stt(sm[0:n, c, :], F0[0:n, :], w(f"f{l}.b1a", c, c + 1)[0:n], sm[0:n, c, :], ALU.add,
                        ALU.mult).then_inc(h_ready, 1)
                if l == 0:
                    for t in range(NT):
                        dve.wait_ge(y_full, due(y_full))
                        tt(XB[:, t, :], YB[:, 0:P], X1[:, t, :], ALU.add).then_inc(x1_ready, 1)
                    return
                for step, t in lagged(TAIL, NT):
                    if step == "residual":
                        own_norms_done()
                        dve.wait_ge(y_full, due(y_full))
                        tt(res[:, t % 2, :], YB[:, 0:P], X1[:, t, :], ALU.add).then_inc(y_used, 1)
                        dve.wait_ge(y_used, due(y_used))
                        link(tt(res[:, t % 2, :], res[:, t % 2, :], X[:, t, :], ALU.add))
                        stats(res[:, t % 2, :], t)
                    if step == "finish":
                        finish(res[:, t % 2, :], t)

            def plain_tail(other):
                for step, t in lagged(TAIL, NT):
                    if step == "residual":
                        residual(t, other[:, t, :])
                    if step == "finish":
                        finish(res[:, t % 2, :], t)

            def gelu_ffn():
                due(act_ready, 8)
                dve.wait_ge(ew_ready, due(ew_ready))
                for step, t in lagged(TAIL, NT):
                    if step == "residual":
                        own_norms_done()
                        dve.wait_ge(y_full, due(y_full))
                        stt(res[:, t % 2, :], YB[:, 0:P], ew[:, t:t + 1], X[:, t, :], ALU.mult, ALU.add).then_inc(y_used, 1)
                        dve.wait_ge(y_used, due(y_used))
                        stats(res[:, t % 2, :], t)
                    if step == "finish":
                        finish(res[:, t % 2, :], t)

            def ema():
                dve.wait_ge(xt_ready, XT_BEFORE_EMA)
                x = XT[:, :].rearrange("p (b k) -> p b k", b=NB)
                y = YF[:, :].rearrange("p (b k) -> p b k", b=NB)
                link(ts(YF[:, :], XT[:, :], w("mix"), None, ALU.mult))
                stt(y[:, :, 1:S], x[:, :, 0:S - 1], omix[:, :], y[:, :, 1:S], ALU.mult, ALU.add).then_inc(inp_ready, 1)
                dve.wait_ge(act_ready, due(act_ready))
                dve.tensor_tensor_scan(G[:, 1, :], w("not_first"), G[:, 0, :], 0.0, ALU.mult,
                                       ALU.add).then_inc(ema_ready, 1)
                dve.wait_ge(xb_ready, due(xb_ready))
                plain_tail(XB)

            def choose_first(dst, src, n, table):
                link(dve.tensor_reduce(col[:, 0, :], src, AX.X, ALU.max))
                link(tt(tmp[:, :, 0:n], src, bc(col[:, 0, :], [P, NT, n], 2), ALU.is_equal))
                link(tt(tmp[:, :, 0:n], tmp[:, :, 0:n], bc(table, [P, NT, n], 1), ALU.mult))
                link(dve.tensor_reduce(col[:, 1, :], tmp[:, :, 0:n], AX.X, ALU.max))
                return tt(dst, tmp[:, :, 0:n], bc(col[:, 1, :], [P, NT, n], 2), ALU.is_equal)

            def top1_ffn():
                dve.wait_ge(logit_full, due(logit_full))
                dve.tensor_copy(lg[:, :, :], OB[:, 0:NT * NE2].rearrange("p (t e) -> p t e", t=NT)).then_inc(lg_ready, 1)
                dve.wait_ge(lg_ready, due(lg_ready))
                choose_first(one[:, :, :], lg[:, :, :], NE2, w("down16")).then_inc(one_ready, 1)
                dve.wait_ge(one_ready, due(one_ready))
                dve.wait_ge(sig_ready, due(sig_ready))
                link(tt(gate[:, :, :], one[:, :, :], sig[:, :, :], ALU.mult))
                link(dve.tensor_reduce(col[:, 2, :], gate[:, :, :], AX.X, ALU.add))
                for t in range(NT):
                    last = ts(XB[:, t, :], X[:, t, :], col[:, 2, t:t + 1], None, ALU.mult)
                last.then_inc(xs_ready, 1)

                def hidden(k):
                    for c in range(2):
                        dve.wait_ge(act_ready, due(act_ready))
                        dve.wait_ge(up_full, UP_BEFORE_TOP1 + 4 * k + 2 * c + 2)
                        tt(sm[:, 2 * (k % 2) + c, :], bank[2 + c][:, :], sm[:, 2 * (k % 2) + c, :],
                           ALU.mult).then_inc(h_ready, 1)

                def tokens(k):
                    dve.wait_ge(picked, due(picked))
                    tt(G[:, k % 2, :], HT[:, :, :].rearrange("p b k -> p (b k)"), S0[:, :], ALU.mult).then_inc(xe_ready, 1)
                hidden(0)
                dve.wait_ge(xt_ready, XT_BEFORE_EMA + 3 * NT)
                tokens(1)
                for k in range(1, NE2 + 1):
                    if k < NE2:
                        tokens(k + 1)
                    hidden(k)
                plain_tail(X)

            def top2_ffn():
                dve.wait_ge(logit_full, due(logit_full))
                l8, g8 = lg[:, :, 0:NE3], gate[:, :, 0:NE3]
                dve.tensor_copy(l8, OB[:, 0:NT * NE3].rearrange("p (t e) -> p t e", t=NT)).then_inc(lg_ready, 1)
                dve.wait_ge(lg_ready, due(lg_ready))
                link(choose_first(one[:, :, 0:NE3], l8, NE3, w("down8")))
                link(dve.tensor_copy(col[:, 2, :], col[:, 0, :]))
                link(stt(l8, one[:, :, 0:NE3], -BIG, l8, ALU.mult, ALU.add))
                link(choose_first(two[:, :, 0:NE3], l8, NE3, w("down8")))
                tt(col[:, 3, :], col[:, 0, :], col[:, 2, :], ALU.subtract).then_inc(gap_ready, 1)
                dve.wait_ge(sig_ready, due(sig_ready))
                link(ts(col[:, 5, :], col[:, 4, :], 1.0, None, ALU.add))
                link(dve.reciprocal(col[:, 5, :], col[:, 5, :]))
                link(tt(col[:, 6, :], col[:, 5, :], col[:, 4, :], ALU.mult))
                link(tt(g8, one[:, :, 0:NE3], bc(col[:, 5, :], [P, NT, NE3], 2), ALU.mult))
                link(tt(two[:, :, 0:NE3], two[:, :, 0:NE3], bc(col[:, 6, :], [P, NT, NE3], 2), ALU.mult))
                tt(g8, g8, two[:, :, 0:NE3], ALU.add).then_inc(one_ready, 1)
                dve.wait_ge(one_ready, due(one_ready))
                dve.wait_ge(b2_full, 1)
                tt(XB[:, :, :], S1[:, :].rearrange("p (t n) -> p t n", t=NT), X[:, :, :], ALU.add).then_inc(acc_ready, 1)
                dve.wait_ge(acc_ready, 1)
                for e in range(NE3):
                    dve.wait_ge(o3_full, e + 1)
                    if e >= 1:
                        dve.wait_ge(o3_used, e)
                    for t in range(NT):
                        last = stt(XB[:, t, :], tile(bank[2 + e % 2], t), gate[:, t, e:e + 1], XB[:, t, :],
                                   ALU.mult, ALU.add)
                    last.then_inc(o3_used, 1)
                dve.wait_ge(o3_used, NE3)
                for step, t in lagged(["residual", "finish"], NT):
                    if step == "residual":
                        own_norms_done()
                        stats(XB[:, t, :], t)
                    if step == "finish":
                        finish(XB[:, t, :], t)

            XT_BEFORE_EMA = 7 * NT
            UP_BEFORE_TOP1 = 2 * 3 * 2 + 8 + 1
            dve.wait_ge(init_pool, 1)
            with dve.Fori(0, 2):
                dve.wait_ge(xb_ready, due(xb_ready))
                plain_tail(XB)
                masks()
                attention("x0")
                first_ffn(0)
                first_ffn(1)
                attention("a1")
                attention("x1")
                gelu_ffn()
                ema()
                attention("x2")
                top1_ffn()
                attention("a3")
                attention("x3")
                top2_ffn()
                end_of_turn()

        @block.gpsimd
        def _(pool):
            due = Tally()

            def link(ins):
                ins.then_inc(pool_link, 1)
                pool.wait_ge(pool_link, due(pool_link))

            def end_of_turn():
                pool.drain().then_inc(turn_done, 1)
                pool.wait_ge(go_pool, 1)
                pool.sem_clear(go_pool)
                due.count.clear()

            tt, ts = pool.tensor_tensor, pool.tensor_scalar
            half = w("neghalf")
            pool.wait_ge(first_in, 16)
            with pool.Fori(0, 2):
                for step, g in lagged(MIX0, 4):
                    j = g % 2
                    if step == "scale":
                        pool.wait_ge(vw_ready, g + 1)
                        if g >= 2:
                            pool.wait_ge(state_full, 2 * g - 2)
                        tt(VJ[:, j, :, :], bc(VW[:, j, :], [P, 8, P], 1), bc(w("seq_of"), [P, 8, P], 2),
                           ALU.mult).then_inc(vj_ready, 1)
                end_of_turn()

            pool.memset(VX[:, :, :, :], 0.0)
            pool.memset(VX32[:, :, :, :], 0.0).then_inc(pool_init, 1)
            pool.wait_ge(pool_init, 1)
            n_init = 1
            for b in range(2):
                r = slice(b * S, (b + 1) * S)
                for v, c in ((VX, 32), (VX32, 16)):
                    pool.memset(v[r, :, :, c + b:c + b + 1], 1.0).then_inc(pool_init, 1)
                    n_init += 1
                    pool.wait_ge(pool_init, n_init)
            pool.sem_inc(init_pool, 1)
            pool.wait_ge(rest_in, 16)

            def norms(n=NT):
                for t in range(n):
                    rstds(t)

            def rstds(t):
                pool.wait_ge(var_ready, due(var_ready))
                link(ts(veps[:, t % 2, :], mv[:, t % 2, 1:2], EPS, None, ALU.add))
                tt(rstd[:, t % 2, :], veps[:, t % 2, :], half, ALU.pow).then_inc(rstd_ready, 1)

            def bias_in(name):
                pool.wait_ge(x_ready, due.now(x_ready))
                tt(XB[:, :, :], X[:, :, :], bc(w(name), [P, NT, P], 1), ALU.add).then_inc(xb_ready, 1)

            def attention(name):
                a = att[name]
                units = a["heads"] // 16 * NT
                pool.wait_ge(x_ready, due.now(x_ready))
                pool.memset(ON[:, :, :, :], 0.0).then_inc(on_clear, 1)
                if name == "x0":
                    for t in range(NT):
                        last = ts(XB[:, t, :], w("x0.bo"), m_tok[:, t:t + 1], None, ALU.mult)
                    link(last)
                    tt(XB[:, :, :], X[:, :, :], XB[:, :, :], ALU.add).then_inc(xb_ready, 1)
                else:
                    bias_in(f"{name}.bo")
                for step, u in attention_order(units, NT):
                    if step == "scores" and a["mask"] is not None:
                        for b in range(2):
                            slot = 2 * (u % 2) + b
                            pool.wait_ge(mx_ready, due(mx_ready))
                            v = sm[:, slot, :].rearrange("p (h k) -> p h k", h=8)
                            tt(v, v, bc(mx[:, slot, :], [P, 8, S], 2), ALU.subtract).then_inc(pcentered, 1)
                    if step == "residual":
                        rstds(u)
                due(x_ready, NT)

            def first_ffn(l):
                for u in range(2 * NT):
                    pool.wait_ge(raw_ready, due(raw_ready))
                    if u >= 4:
                        pool.wait_ge(rotated, 2 * NT * l + u - 3)
                    t, i = divmod(u, 2)
                    tt(M1[:, u % 4, :].rearrange("p (h d) -> p h d", d=S),
                       RAW[:, t, i, :].rearrange("p (h d) -> p h d", d=S),
                       bc(rot[:, l, 2 * i, :], [P, 8, S], 1), ALU.mult).then_inc(m1_ready, 1)
                if l == 0:
                    pool.memset(ON[:, :, :, :], 0.0).then_inc(zeroed, 1)
                for step, t in lagged(LOCAL, NT):
                    if step == "scores":
                        pool.wait_ge(mx_ready, due(mx_ready))
                        v = sm[:, t % 2, :].rearrange("p (h k) -> p h k", h=8)
                        tt(v, v, bc(mx[:, t % 2, :], [P, 8, S], 2), ALU.subtract).then_inc(pcentered, 1)
                    if step == "soft":
                        pool.wait_ge(sum_ready, due(sum_ready))
                        v = PR(t).rearrange("p (g k) -> p g k", g=8)
                        tt(v, v, bc(mx[:, 2 + t % 2, :], [P, 8, S], 2), ALU.mult).then_inc(pn_ready, 1)
                    if step == "stats":
                        rstds(t)
                if l == 1:
                    norms()
                    due(x_ready, NT)

            pool.wait_ge(init_dve, 1)
            with pool.Fori(0, 2) as it:
                pool.tensor_copy(OTh[:, :].rearrange("p (i j) -> p i j", j=S),
                                 OTall[:, bass.ds(it * NB, NB), :]).then_inc(oth_ready, 1)
                pool.wait_ge(x_in, 16)
                tt(XB[:, :, :], X[:, :, :], bc(w("Abo"), [P, NT, P], 1), ALU.add).then_inc(xb_ready, 1)
                pool.memset(QM[:, :, :, :, :], 0.0)
                pool.memset(PM[:, :, :, :], 0.0)
                pool.memset(HT[:, :, 0:1], 0.0)
                pool.memset(HS[:, :, :, :], 0.0).then_inc(zeroed, 1)
                norms()
                due(x_ready, NT)
                pool.wait_ge(ew_in, 16)
                tt(ew[:, :].unsqueeze(2), ew2[:, :, 0:1], ew2[:, :, 1:2], ALU.add).then_inc(ew_ready, 1)
                pool.wait_ge(masks_in, 16 * 6)
                attention("x0")
                first_ffn(0)
                first_ffn(1)
                attention("a1")
                attention("x1")
                norms()
                due(x_ready, NT)
                bias_in("ema.bout")
                norms()
                due(x_ready, NT)
                attention("x2")
                norms()
                due(x_ready, NT)
                attention("a3")
                attention("x3")
                norms()
                end_of_turn()


def tables():
    r = np.arange(P)
    q = r % S
    k = np.arange(S)
    one_hot = lambda a, n: (a[:, None] == np.arange(n)[None, :])
    half = np.arange(0, S, 2, dtype=np.float32)
    inv = (1.0 / 10000.0 ** (half / S)).astype(np.float32)
    pos = np.arange(S, dtype=np.float32)
    f = pos[:, None] * inv[None, :]
    f = np.concatenate([f, f], -1).astype(np.float64)
    base = (half + 0.4 * S) / (1.4 * S)
    power = (pos - S // 2) / (S // 2)
    scale = base[None, :].astype(np.float64) ** power[:, None]
    scale = np.concatenate([scale, scale], -1)
    sign = np.where(np.arange(S) < S // 2, -1.0, 1.0)[None, :]
    two = lambda a: np.concatenate([a, a], 0)
    c = {
        "ident": np.eye(P), "blocks": (r[:, None] // 8 == r[None, :] // 8), "seq_of": one_hot(r // 16, 8),
        "fold": one_hot(q, S), "par16": one_hot(r // 8 % 2, 2), "par32": one_hot(r // 4 % 2, 2),
        "pair16": one_hot(r // 16, 8), "pair32": one_hot(r // 8, 16),
        "causal": np.where(q[:, None] >= k[None, :], BIG, -1e30),
        "not_first": np.broadcast_to(np.arange(HALF) % S != 0, (P, HALF)),
        "down16": np.broadcast_to(np.arange(16, 0, -1), (P, 16)), "down8": np.broadcast_to(np.arange(8, 0, -1), (P, 8)),
        "cosq": two(np.cos(f) * scale), "sinq": two(np.sin(f) * scale * sign),
        "cosk": two(np.cos(f) / scale), "sink": two(np.sin(f) / scale * sign),
        "neghalf": np.full((P, 1), -0.5),
    }
    return {n: np.ascontiguousarray(v, dtype=np.float32) for n, v in c.items()}


def pack(names, parts):
    out = np.zeros((P, sum(n for _, n in names)), np.float32)
    a = 0
    for name, n in names:
        v = parts[name]
        out[:v.shape[0], a:a + n] = v
        a += n
    return out


def rows(v):
    return np.broadcast_to(v.reshape(1, -1), (P, v.size))


def chunks(v):
    return v.reshape(-1, P, v.shape[-1]).transpose(1, 0, 2).reshape(P, -1)


def kernel(**inputs):
    import concourse.bacc as bacc
    from concourse.bass_utils import run_bass_kernel_spmd as run

    i = {n: np.asarray(v) for n, v in inputs.items()}
    parts = tables()
    cat = np.concatenate
    parts["Aw"] = cat([i[f"L0_attn_W{n}_w"].T for n in "qkvwr"], 1)
    parts["Ab"] = cat([rows(i[f"L0_attn_W{n}_b"]) for n in "qkvwr"], 1)
    parts["Ao"], parts["Abo"] = i["L0_attn_Wo_w"].T, rows(i["L0_attn_Wo_b"])
    none = np.zeros(P, np.float32)
    qkv1, qkv2, b2 = i["L1_attn_W_qkv"].T, i["L2_xattn_Wqkv"], i["L2_xattn_bqkv"]
    weights = {
        "x0": [i["L0_xattn_W" + n] for n in "QKVO"] + [i["L0_xattn_b" + n] for n in "QKVO"],
        "a1": [qkv1[:, 0:P], qkv1[:, P:2 * P], qkv1[:, 2 * P:], np.eye(P, dtype=np.float32)] + [none] * 4,
        "x1": [i["L1_xattn_W" + n] for n in "qkvo"] + [i["L1_xattn_b" + n] for n in "qkvo"],
        "x2": [qkv2[:, 0:P], qkv2[:, P:2 * P], qkv2[:, 2 * P:], i["L2_xattn_Wo"], b2[0:P], b2[P:2 * P], b2[2 * P:],
               i["L2_xattn_bo"]],
        "a3": [i["L3_attn_W_" + n] for n in "qkvo"] + [none] * 3 + [i["L3_attn_b_o"]],
        "x3": [i["L3_xattn_W" + n].T for n in "qkvo"] + [none] * 4,
    }
    for a, (q, k, v, o, bq, bk, bv, bo) in weights.items():
        parts.update({f"{a}.q": q, f"{a}.k": k, f"{a}.v": v, f"{a}.o": o, f"{a}.bq": bq[:, None],
                      f"{a}.bk": bk[:, None], f"{a}.bv": rows(bv), f"{a}.bo": rows(bo)})
    swap = cat([np.arange(S // 2, S), np.arange(S // 2)])
    fill = np.zeros(3 * P - HID, np.float32)
    for l in range(2):
        b1 = i["L0_ffn_b1"][l]
        w2 = cat([i["L0_ffn_w2"][l], np.zeros((3 * P - HID, P), np.float32)], 0)
        parts.update({
            f"f{l}.b1a": cat([b1[:HID], fill]).reshape(3, P).T, f"f{l}.b1g": cat([b1[HID:], fill]).reshape(3, P).T,
            f"f{l}.b2": i["L0_ffn_b2"][l][:, None], f"f{l}.g": i["L0_ffn_ln_g"][l][:, None],
            f"f{l}.b": i["L0_ffn_ln_b"][l][:, None],
            f"f{l}.qs": rows(i["L0_ffn_q_scale"][l]), f"f{l}.ks": rows(i["L0_ffn_k_scale"][l]),
            f"f{l}.qsr": rows(i["L0_ffn_q_scale"][l][swap]), f"f{l}.ksr": rows(i["L0_ffn_k_scale"][l][swap]),
            f"f{l}.wqkv": i["L0_ffn_wqkv"][l], f"f{l}.wo": chunks(i["L0_ffn_wo"][l]), f"f{l}.w1": i["L0_ffn_w1"][l],
            f"f{l}.w2": chunks(w2)})
    parts.update({
        "g.w1": i["L1_ffn_w1"], "g.w2": chunks(i["L1_ffn_w2"]),
        "ema.in": i["L2_attn_W_in"].T, "ema.out": i["L2_attn_W_out"].T, "ema.bin": i["L2_attn_b_in"][:, None],
        "ema.bout": rows(i["L2_attn_b_out"]), "decay": rows(i["L2_attn_decay"]), "mix": rows(i["L2_attn_mix"]),
        "e2.r": i["L2_ffn_w_router"].T, "e2.g": i["L2_ffn_w_gate"].T, "e2.u": i["L2_ffn_w_up"].T,
        "e2.d": chunks(i["L2_ffn_w_down"].T), "e3.r": i["L3_ffn_Wg"].T,
        "e3.b1": i["L3_ffn_b1"].reshape(NE3 * 4, P).T, "e3.b2": i["L3_ffn_b2"],
        "rel": np.tile(i["L3_attn_rel_emb"][0:S].T, (16, 1)),
    })
    x = i["x"]
    mask = i["mask_BxSx1_ff1"].reshape(B, S)
    two = lambda v: cat([v, v], 0)
    exw = np.zeros((P, 2 * NT, 2), np.float32)
    ew = i["L1_ffn_expert_weights"]
    exw[:, 0:ew.shape[0] // P] = ew.reshape(-1, P, 2).transpose(1, 0, 2)
    arrays = {
        "small": pack(FIRST + REST, parts), "early": pack(EARLY, parts),
        "xperm": x.transpose(2, 1, 0).reshape(P, TOK),
        "xtok": x.reshape(2 * NT, P, P).transpose(1, 0, 2),
        "ctxT": i["ctx_1024"].reshape(TOK, P).T,
        "mrow": np.broadcast_to(mask[None], (P, B, S)), "mcol": two(mask.T),
        "mtok": mask.reshape(2 * NT, P).T,
        "pad_rows": np.broadcast_to(i["mask_BxS2_bk0"][None], (P, B, S)),
        "att_rows": two(i["mask_SxS2_bk1"]),
        "ik_rows": two(i["mask_Bx1xSxS2_ik1"].reshape(B, S, S).transpose(1, 0, 2)),
        "exw": exw,
        "gup": i["L2_ffn_gate_up_proj"], "down": i["L2_ffn_down_proj"], "e3w1": i["L3_ffn_W1"], "e3w2": i["L3_ffn_W2"],
    }
    nc = bacc.Bacc("TRN2", target_bir_lowering=False, num_devices=1)
    args = []
    for n, a in arrays.items():
        arrays[n] = a = np.ascontiguousarray(a)
        args.append(nc.dram_tensor(n, a.shape, mybir.dt.from_np(a.dtype), kind="ExternalInput").ap())
    y = nc.dram_tensor("y", (B, S, P), F32, kind="ExternalOutput").ap()
    decoder(nc, *args, y.rearrange("(t b) s d -> (b s) t d", b=2))
    r = run(nc, [arrays], core_ids=[0])
    return r.results[0]["y"]
```

```python
from contextlib import ExitStack

import numpy as np
import concourse.bass as bass
from concourse import mybir

ALU = mybir.AluOpType
ACT = mybir.ActivationFunctionType
F32 = mybir.dt.float32
I32 = mybir.dt.int32
U8 = mybir.dt.uint8
BF16 = mybir.dt.bfloat16
AX = mybir.AxisListType

P = 128
B, S = 16, 64
TOK = B * S
HALF = TOK // 2
NB = HALF // S
NT = HALF // P
HID = int(P * 4 * 2 / 3)
CH = [(0, 128), (128, 128), (256, HID - 256)]
EPS = 1e-5
BIG = 3e38
NE2, NF2 = 16, 256
NE3, NF3 = 8, 512
ATT = ["x0", "a1", "x1", "x2", "a3", "x3"]

FIRST = [("Aw", 416), ("Ab", 416), ("ident", 128), ("blocks", 128), ("seq_of", 8), ("neghalf", 1)]
REST = [("Ao", 128), ("Abo", 128), ("fold", 64), ("par16", 2), ("par32", 2), ("pair16", 8), ("pair32", 16),
        ("causal", 64), ("not_first", 512), ("down16", 16), ("down8", 8), ("cosq", 64), ("sinq", 64),
        ("cosk", 64), ("sink", 64)]
for _a in ATT:
    REST += [(f"{_a}.q", 128), (f"{_a}.k", 128), (f"{_a}.v", 128), (f"{_a}.o", 128),
             (f"{_a}.bq", 1), (f"{_a}.bk", 1), (f"{_a}.bv", 128), (f"{_a}.bo", 128)]
for _l in range(2):
    REST += [(f"f{_l}.b1a", 3), (f"f{_l}.b1g", 3), (f"f{_l}.b2", 1), (f"f{_l}.g", 1), (f"f{_l}.b", 1),
             (f"f{_l}.qs", 64), (f"f{_l}.ks", 64), (f"f{_l}.qsr", 64), (f"f{_l}.ksr", 64)]
REST += [("ema.in", 128), ("ema.out", 128), ("ema.bin", 1), ("ema.bout", 128),
         ("decay", 1), ("mix", 1), ("e2.r", 16), ("e2.g", 256), ("e2.u", 256), ("e2.d", 256),
         ("e3.r", 8), ("e3.b1", 32), ("e3.b2", 128), ("rel", 64)]
EARLY = []
for _l in range(2):
    EARLY += [(f"f{_l}.wqkv", 1536), (f"f{_l}.wo", 512), (f"f{_l}.w1", 2 * HID), (f"f{_l}.w2", 384)]
EARLY += [("g.w1", 1024), ("g.w2", 1024)]


def columns(names):
    at, n = {}, 0
    for name, w in names:
        at[name] = (n, w)
        n += w
    return at, n


class Tally:

    def __init__(self):
        self.count = {}

    def __call__(self, sem, n=1):
        self.count[id(sem)] = self.count.get(id(sem), 0) + n
        return self.count[id(sem)]

    def now(self, sem):
        return self.count.get(id(sem), 0)


ATT_STEPS = {"project": 0, "kv": -0.01, "scores": 1.91, "turn": 2.92, "values": 3.93, "fold": 5.24,
             "residual": 6.22, "finish": 7.26}
REL_STEPS = {"project": 0, "kv": -0.01, "rel": 1.01, "scores": 4.64, "turn": 5.65, "values": 6.66, "fold": 7.97,
             "residual": 8.95, "finish": 9.99}
TAIL_STEPS = {"back": 0, "residual": 1.0, "finish": 2.72}
EMA_STEPS = {"mix": 0, "inner": 1.01, "back": 2.02, "residual": 3.03, "finish": 4.04}
CONTEXT_EARLY = (3.0, 1.0)
GAP = 1.37
SHIFT = {("dve", "finish"): -0.5, ("dve", "project"): 0.24, ("act", "turn"): -0.03, ("pool", "project"): -0.3,
         ("pool", "scores"): 0.18}


def chain_order(stages, engine):
    plan, start = [], 0
    for k, name in enumerate(stages):
        steps = (REL_STEPS if name == "a3" else ATT_STEPS if name in ATT else EMA_STEPS if name == "ema" else
                 TAIL_STEPS)
        subs = 2 if name == "x2" else 1
        for u in range(subs * NT):
            for step, after in steps.items():
                if step == "kv" and name[0] == "x":
                    after -= CONTEXT_EARLY[subs - 1]
                if step in ("fold", "residual", "finish") and u % subs != subs - 1:
                    continue
                plan.append((start + u + after + SHIFT.get((engine, step), 0), k, u, name, step))
        start += subs - 1 + steps["finish"] + GAP
    for _, _, u, name, step in sorted(plan):
        subs = 2 if name == "x2" else 1
        yield name, step, u, u // subs, u % subs


def lagged(steps, n):
    for i in range(n + len(steps)):
        for lag, step in enumerate(steps):
            if 0 <= i - lag < n:
                yield step, i - lag


LOCAL_STEPS = {"rotate": -0.01, "turn_qk": 0.7, "scores": 2.01, "soft": 3.02, "turn": 4.03, "values": 5.04,
               "out": 6.05, "shift": 6.79, "stats": 8.07, "norm": 9.38, "up": 10.39, "down": 11.4}
BETWEEN_STEPS = {"again": 12.41, "feed": 13.12}
LOCAL_SHIFT = {("dve", "stats"): -0.6, ("dve", "up"): 0.3, ("act", "values"): -0.3, ("pool", "stats"): -0.3}


def local_order(layer, engine):
    steps = LOCAL_STEPS | (BETWEEN_STEPS if layer == 0 else {})
    return [(step, t) for _, step, t in sorted(
        (t + after + LOCAL_SHIFT.get((engine, step), 0), step, t) for step, after in steps.items() for t in range(NT))]


MIX0 = ["project", "scale", "state", "mix"]


def decoder(nc, small, early, xperm, xtok, ctxT, mrow, mcol, mtok, pad_rows, att_rows, ik_rows, exw,
            gup, down, e3w1, e3w2, out):
    at, width = columns(FIRST + REST)
    eat, ewidth = columns(EARLY)
    n_first = sum(n for _, n in FIRST)
    scratch = nc.dram_tensor("rel_scratch", (NB, P * 512), F32, kind="Internal")
    with ExitStack() as ctx:
        def sb(name, shape, dt=F32):
            return ctx.enter_context(nc.sbuf_tensor(name, shape, dt))

        def sem(name):
            return ctx.enter_context(nc.semaphore(name))

        W = sb("W", [P, width])
        big = sb("big", [P, ewidth + NT * 1024])
        pairs = sb("pairs", [P, 8, HALF])
        X = sb("X", [P, NT, P])
        X1 = sb("X1", [P, NT, P])
        XB = sb("XB", [P, NT, P])
        XT = sb("XT", [P, HALF])
        HT = sb("HT", [P, NB, S])
        CT = sb("CT", [P, HALF])
        Q = sb("Q", [P, NB, 2, S])
        VX = sb("VX", [P, NT, 8, 34])
        VX32 = sb("VX32", [P, NT, 16, 18])
        sm = sb("sm", [P, 4, 512])
        mx = sb("mx", [P, 4, 8])
        pr = sb("pr", [P, 2, 8, 2, S])
        pT = sb("pT", [P, 2, 8, P])
        rs = sb("rs", [P, 2, 8, 2])
        ON = sb("ON", [P, NT, 2, P])
        oT = sb("oT", [P, 2, P])
        cap = sb("cap", [P, 3, NB, S])
        bkm = sb("bkm", [P, 6, 16])
        relp = sb("relp", [P, 8, S])
        rot = sb("rot", [P, 2, 4, S])
        m_row = sb("m_row", [P, NB, S])
        m_col = sb("m_col", [P, NB])
        m_tok = sb("m_tok", [P, NT])
        m_pad = sb("m_pad", [P, NB, S], U8)
        m_att = sb("m_att", [P, S], U8)
        m_ik = sb("m_ik", [P, NB, S], I32)
        ew2 = sb("ew2", [P, NT, 2])
        ew = sb("ew", [P, NT])
        omix = sb("omix", [P, 1])
        res = sb("res", [P, 2, P])
        st = sb("st", [P, 2, 6])
        mv = sb("mv", [P, 2, 2])
        veps = sb("veps", [P, 2, 1])
        rstd = sb("rstd", [P, 2, 1])
        YF = sb("YF", [P, HALF])
        G = sb("G", [P, 4, HALF])
        OTall = sb("OTall", [P, B, S])
        OTh = sb("OTh", [P, HALF])
        lg = sb("lg", [P, NT, 16])
        one = sb("one", [P, NT, 16])
        two = sb("two", [P, NT, 16])
        tmp = sb("tmp", [P, NT, 16])
        sig = sb("sig", [P, NT, 16])
        gate = sb("gate", [P, NT, 16])
        col = sb("col", [P, 8, NT])
        oneT = sb("oneT", [NE2, HALF], BF16)
        pick = sb("pick", [NE2, NE2, P], BF16)
        gT = sb("gT", [NE3, HALF])
        QM = sb("QM", [P, 4, 2, 2, S])
        PM = sb("PM", [P, 4, 2, P])
        HS = sb("HS", [P, 2, 2, S])
        ss = sb("ss", [P, NT, 16])
        rn = sb("rn", [P, NT, 16])

        def w(name, a=0, b=None):
            o, n = at[name]
            return W[:, o + a:o + (n if b is None else b)]

        def early_w(name, a=0, b=None):
            o, n = eat[name]
            return big[:, o + a:o + (n if b is None else b)]

        M1, M2 = pairs[:, 0:4, :], pairs[:, 4:8, :]
        RAW = big[:, ewidth:ewidth + NT * 1024].rearrange("p (t i n) -> p t i n", t=NT, i=2)
        KT = [pT[:, 1, 0:4, :], pT[:, 1, 4:8, :]]
        QMs = [QM, ON[:, :, :, :].rearrange("p t b n -> p (t b n)").rearrange("p (j b c q) -> p j b c q", j=4, b=2, c=2)]
        oT0 = pT[:, 0, :, :].rearrange("p (j r) n -> p j (r n)", j=2).rearrange(
            "p j (r b q) -> p j r b q", r=4, b=2)
        VS = G
        RB = [QM[:, 0:2].rearrange("p a b c q -> p (a b c q)"), QM[:, 2:4].rearrange("p a b c q -> p (a b c q)"),
              PM[:, 0:2].rearrange("p a b q -> p (a b q)"), PM[:, 2:4].rearrange("p a b q -> p (a b q)")]

        def room(a, n, pattern, **k):
            return big[:, a:a + n].rearrange(pattern, **k)
        XP = big[:, 7424:7424 + TOK]
        Z = room(512, 832, "p (j n) -> p j n", j=2)
        SQ = room(1536, 512, "p (j n) -> p j n", j=2)
        RN = room(2048, 64, "p (j n) -> p j n", j=2)
        SS = room(2112, 64, "p (j n) -> p j n", j=2)
        SG = room(2176, 64, "p (j n) -> p j n", j=2)
        QK = room(2304, 512, "p (j n) -> p j n", j=2)
        VW = room(2816, 256, "p (j n) -> p j n", j=2)
        VJ = room(3072, 2048, "p (j s n) -> p j s n", j=2, s=8)
        AM = room(5120, 2048, "p (j s n) -> p j s n", j=2, s=8)
        QTp = room(7168, 256, "p (j n) -> p j n", j=2)
        gu_w = room(0, 8192, "p (e n) -> p e n", e=NE2)
        dn_w = room(8192, 4096, "p (e c n) -> p e c n", e=NE2, c=2)
        w1_w = room(0, 4096, "p (e n) -> p e n", e=NE3)
        w2_w = room(4096, 4096, "p (e c n) -> p e c n", e=NE3, c=4)

        bank = [ctx.enter_context(nc.psum_tensor(f"bank{i}", [P, 512], F32)) for i in range(8)]
        S0, S1, T0, T1, F0, F1, OB, YB = bank

        first_in = sem("first_in")
        rest_in = sem("rest_in")
        pool_init = sem("pool_init")
        init_pool = sem("init_pool")
        init_dve = sem("init_dve")
        init_act = sem("init_act")
        turn_done = sem("turn_done")
        go_pe, go_act, go_dve, go_pool = (sem(f"go_{e}") for e in ("pe", "act", "dve", "pool"))
        turn_sems = [turn_done]

        def tsem(name):
            q = sem(name)
            turn_sems.append(q)
            return q

        xp_in, x_in, ctx_in, masks_in, ew_in = (tsem(n) for n in ("xp_in", "x_in", "ctx_in", "masks_in", "ew_in"))
        f0_in, f1_in, g_in, e2_in, e3_in = (tsem(n) for n in ("f0_in", "f1_in", "g_in", "e2_in", "e3_in"))
        rel_stored = [tsem(f"rel_stored{i}") for i in range(2)]
        rel_back = [tsem(f"rel_back{i}") for i in range(4)]
        out_sent = tsem("out_sent")
        dma_sems = turn_sems[1:]
        dve_link, act_link, pool_link = tsem("dve_link"), tsem("act_link"), tsem("pool_link")
        (proj_full, qT_full, state_full, mix_full, qv_full, k_full, scored, turned, valued, folded, y_full,
         x_turned, qk_full, rot_full, shifted, restored, normed, up_full, down_full, rel_full, logit_full,
         choice_full, picked, gate_full, o3_full, v2_full, valued2, b2_full) = (tsem(n) for n in (
             "proj_full", "qT_full", "state_full", "mix_full", "qv_full", "k_full", "scored", "turned",
             "valued", "folded", "y_full", "x_turned", "qk_full", "rot_full", "shifted", "restored", "normed",
             "up_full", "down_full", "rel_full", "logit_full", "choice_full", "picked", "gate_full", "o3_full", "v2_full", "valued2",
             "b2_full"))
        (sig_ready, qT_ready, ot_stored, k_split, exped, pt_ready, o_ready, xt_ready, squared, raw_ready, v2_ready, qm_ready,
         kt_ready, pm_ready, ot_ready, hs_ready, h2_ready, act_ready, yf_ready, rel_ready, choice_ready,
         gt_ready) = (tsem(n) for n in (
             "sig_ready", "qT_ready", "ot_stored", "k_split", "exped", "pt_ready", "o_ready", "xt_ready", "squared", "raw_ready",
             "v2_ready", "qm_ready", "kt_ready", "pm_ready", "ot_ready", "hs_ready", "h2_ready", "act_ready",
             "yf_ready", "rel_ready", "choice_ready", "gt_ready"))
        (z_ready, ss_ready, qk_ready, vw_ready, am_ready, qv_split, capped, mx_ready, centered, on_ready,
         var_ready, x_ready, summed, m2_ready, rotated, zr_ready, sum_ready, x1_ready, back_used, hn_ready, h_ready, rel_added, y_used,
         inp_ready, ema_ready, lg_ready, one_ready, xs_ready, xe_ready, o3_used, gap_ready, acc_ready) = (
             tsem(n) for n in (
                 "z_ready", "ss_ready", "qk_ready", "vw_ready", "am_ready", "qv_split", "capped",
                 "mx_ready", "centered", "on_ready", "var_ready", "x_ready", "summed", "m2_ready", "rotated", "zr_ready", "sum_ready",
                 "x1_ready", "back_used", "hn_ready", "h_ready", "rel_added", "y_used", "inp_ready", "ema_ready", "lg_ready",
                 "one_ready", "xs_ready", "xe_ready", "o3_used", "gap_ready", "acc_ready"))
        (sq_ready, rn_ready, vj_ready, oth_ready, xb_ready, on_clear, pcentered, rstd_ready, m1_ready, zk_ready, pn_ready,
         zeroed, ew_ready) = (tsem(n) for n in (
             "sq_ready", "rn_ready", "vj_ready", "oth_ready", "xb_ready", "on_clear", "pcentered", "rstd_ready",
             "m1_ready", "zk_ready", "pn_ready", "zeroed", "ew_ready"))

        att = {
            "x0": dict(i=0, heads=16, scale=P ** -0.5, mask=0, ctx=True),
            "a1": dict(i=1, heads=16, scale=8 ** -0.5, mask=None, ctx=False),
            "x1": dict(i=2, heads=16, scale=8 ** -0.5, mask=None, ctx=True),
            "x2": dict(i=3, heads=32, scale=4 ** -0.5, mask=1, ctx=True),
            "a3": dict(i=4, heads=16, scale=8 ** -0.5, mask="rel", ctx=False),
            "x3": dict(i=5, heads=16, scale=8 ** -0.5, mask=2, ctx=True),
        }
        BIASED = ("a0", "x0", "x1", "ema", "x2", "a3")
        LAST_NORM = 12 * NT

        def tile(ap, t):
            return ap[:, t * P:(t + 1) * P]

        def PR(t):
            return pr[:, t % 2, 0:4, :, :].rearrange("p h b k -> p (h b k)")

        def keys(u):
            return pairs[:, :, (u % 4) * P:(u % 4 + 1) * P]

        def bc(ap, shape, dim):
            return ap.unsqueeze(dim).to_broadcast(shape)

        block = ctx.enter_context(nc.Block())

        @block.sync
        def _(sp):
            def clear(sems):
                for q in sems:
                    sp.sem_clear(q)

            def go():
                for q in (go_pe, go_act, go_dve, go_pool):
                    sp.sem_inc(q, 1)

            sp.dma_start(W[:, 0:n_first], small[:, 0:n_first]).then_inc(first_in, 16)
            sp.dma_start(XP, xperm).then_inc(xp_in, 16)
            sp.dma_start(W[:, n_first:], small[:, n_first:]).then_inc(rest_in, 16)
            sp.wait_ge(turn_done, 4)
            clear(dma_sems)
            sp.sem_clear(turn_done)
            with sp.Fori(0, 2) as it:
                sp.dma_start(X[:, :, :], xtok[:, bass.ds(it * NT, NT), :]).then_inc(x_in, 16)
                clear(q for q in turn_sems if q not in dma_sems)
                go()
                sp.dma_start(CT[:, :], ctxT[:, bass.ds(it * HALF, HALF)]).then_inc(ctx_in, 16)
                sp.dma_start(m_row[:, :, :], mrow[:, bass.ds(it * NB, NB), :]).then_inc(masks_in, 16)
                sp.dma_start(m_col[:, :], mcol[:, bass.ds(it * NB, NB)]).then_inc(masks_in, 16)
                sp.dma_start(m_tok[:, :], mtok[:, bass.ds(it * NT, NT)]).then_inc(masks_in, 16)
                sp.dma_start(m_pad[:, :, :], pad_rows[:, bass.ds(it * NB, NB), :]).then_inc(masks_in, 16)
                sp.dma_start(m_att[:, :], att_rows).then_inc(masks_in, 16)
                sp.dma_start(m_ik[:, :, :], ik_rows[:, bass.ds(it * NB, NB), :]).then_inc(masks_in, 16)
                sp.dma_start(ew2[:, :, :], exw[:, bass.ds(it * NT, NT), :]).then_inc(ew_in, 16)
                a1, a2 = eat["f1.wqkv"][0], eat["g.w1"][0]
                sp.dma_start(big[:, 0:a1], early[:, 0:a1]).then_inc(f0_in, 16)
                sp.dma_start(big[:, a1:a2], early[:, a1:a2]).then_inc(f1_in, 16)
                sp.dma_start(big[:, a2:ewidth], early[:, a2:ewidth]).then_inc(g_in, 16)
                sp.wait_ge(down_full, 2 * NT + 1)
                for e in range(0, NE2, 4):
                    sp.dma_start(gu_w[:, e:e + 4, :], gup[e:e + 4].rearrange("e p n -> p e n")).then_inc(e2_in, 16)
                    for c in range(2):
                        sp.dma_start(dn_w[:, e:e + 4, c, :], down[e:e + 4, c * P:(c + 1) * P, :].rearrange(
                            "e p n -> p e n")).then_inc(e2_in, 16)
                sp.wait_ge(down_full, 2 * NT + 2)
                for e in range(0, NE3, 4):
                    sp.dma_start(w1_w[:, e:e + 4, :], e3w1[e:e + 4].rearrange("e p n -> p e n")).then_inc(e3_in, 16)
                    for c in range(4):
                        sp.dma_start(w2_w[:, e:e + 4, c, :], e3w2[e:e + 4, c * P:(c + 1) * P, :].rearrange(
                            "e p n -> p e n")).then_inc(e3_in, 16)
                for t in range(NT):
                    for b in (2 * t, 2 * t + 1):
                        sp.wait_ge(rel_ready, b + 1)
                        sp.dma_start(scratch.ap()[b].rearrange("(p n) -> p n", n=512),
                                     G[:, b % 4, :]).then_inc(rel_stored[b % 2], 16)
                    for b in (2 * t, 2 * t + 1):
                        sp.wait_ge(rel_stored[b % 2], 16 * (t + 1))
                        if b >= 4:
                            sp.wait_ge(rel_added, b - 3)
                        for c in range(2):
                            skew = bass.AP(tensor=scratch, offset=b * P * 512 + c * S * 512 + S - 1,
                                           ap=[[511, S], [1, 512]])
                            sp.dma_start(RB[b % 4][c * S:(c + 1) * S, :], skew).then_inc(rel_back[b % 4], 16)
                for t in range(NT):
                    sp.wait_ge(x_ready, LAST_NORM - NT + t + 1)
                    sp.dma_start(out[:, bass.ds(it * NT + t, 1), :], X[:, t:t + 1, :]).then_inc(out_sent, 16)
                sp.wait_ge(turn_done, 4)
                sp.wait_ge(out_sent, 16 * NT)
                clear(dma_sems)

        @block.tensor
        def _(pe):
            due = Tally()
            hold = {}

            def fill(b, used_by):
                if b in hold:
                    pe.wait_ge(*hold[b])
                hold[b] = (used_by, due(used_by))
                return bank[b]

            def end_of_turn():
                pe.drain().then_inc(turn_done, 1)
                hold.clear()
                due.count.clear()

            def start_of_turn():
                pe.wait_ge(go_pe, 1)
                pe.sem_clear(go_pe)

            mm = pe.matmul
            ident = w("ident")
            pe.wait_ge(first_in, 16)
            pe.wait_ge(xp_in, 16)
            for step, g in lagged(MIX0, 8):
                j = g % 2
                if step == "project":
                    ps = fill(j, z_ready)
                    mm(ps[:, 0:416], tile(XP, g), w("Aw"), start=True, stop=True).then_inc(proj_full, 1)
                if step == "state":
                    pe.wait_ge(qk_ready, due(qk_ready))
                    pe.transpose(fill(2, qT_ready)[:, 0:P], QK[:, j, 0:P], ident).then_inc(qT_full, 1)
                    pe.wait_ge(vj_ready, due(vj_ready))
                    for h in range(2):
                        mm(fill(4 + h, am_ready)[:, :], QK[:, j, P:2 * P],
                           VJ[:, j, 4 * h:4 * h + 4, :].rearrange("p s n -> p (s n)"),
                           start=True, stop=True).then_inc(state_full, 1)
                if step == "mix":
                    pe.wait_ge(am_ready, 2 * g + 2)
                    pe.wait_ge(qT_ready, g + 1)
                    ps = fill(6, ot_stored)
                    for c in range(8):
                        last = mm(ps[:, 16 * c:16 * c + 16], AM[:, j, c, :], QTp[:, j, 16 * c:16 * c + 16],
                                  start=True, stop=True)
                    last.then_inc(mix_full, 1)
            end_of_turn()

            def x_to_features(src, t, b=6):
                pe.transpose(fill(b, xt_ready)[:, 0:P], src[:, t, :], ident).then_inc(x_turned, 1)

            def chain(*stages):
                at_ = {}
                for name, step, u, t, s_ in chain_order(stages, "pe"):
                    a = att.get(name)
                    if a:
                        wide = a["heads"] == 16
                        V, blk = (VX, 34) if wide else (VX32, 18)
                        src = CT if a["ctx"] else XT
                    if step == "inner":
                        pe.wait_ge(inp_ready, due(inp_ready))
                        mm(fill(4, act_ready)[:, 0:P], w("ema.in"), tile(YF, t), start=True, stop=True).then_inc(up_full, 1)
                    if step == "back":
                        ps = fill(7, y_used)
                        if name == "a0":
                            mm(ps[:, 0:P], tile(OTh, t), w("Ao"), start=True, stop=True).then_inc(y_full, 1)
                        elif name == "ema":
                            pe.wait_ge(ema_ready, due(ema_ready))
                            mm(ps[:, 0:P], tile(G[:, 1, :], t), w("ema.out"), start=True, stop=True).then_inc(y_full, 1)
                        else:
                            pe.transpose(ps[:, 0:P], tile(YF, t), ident).then_inc(y_full, 1)
                    if step == "kv":
                        if a["ctx"]:
                            pe.wait_ge(ctx_in, 16)
                        else:
                            pe.wait_ge(xt_ready, at_["x", t])
                        mm(fill(5, k_split)[:, 0:P], w(f"{name}.k"), tile(src, t), start=True, stop=True).then_inc(k_full, 1)
                        at_["k", u] = due.now(k_split)
                        if s_ == 0:
                            mm(fill(4, qv_split)[:, 0:P], tile(src, t), w(f"{name}.v"), start=True,
                               stop=True).then_inc(qv_full, 1)
                    if step == "project" and s_ == 0:
                        pe.wait_ge(xt_ready, at_["x", t])
                        mm(fill(4, qv_split)[:, 0:P], w(f"{name}.q"), tile(XT, t), start=True,
                           stop=True).then_inc(qv_full, 1)
                        at_["q", t] = due.now(qv_split)
                    if step == "rel":
                        pe.wait_ge(qv_split, at_["q", t])
                        for b in range(2):
                            mm(fill(6 + b, rel_ready)[:, :], Q[:, 2 * t + b, :, :].rearrange("p c q -> p (c q)"),
                               relp[:, :, :].rearrange("p h k -> p (h k)"), start=True, stop=True).then_inc(rel_full, 1)
                    if step == "scores":
                        pe.wait_ge(qv_split, at_["q", t])
                        pe.wait_ge(k_split, at_["k", u])
                        freed = {None: centered, "rel": rel_added}.get(a["mask"], capped)
                        for b in range(2):
                            mm(fill(b, freed)[:, :].rearrange("p (h k) -> p h k", h=8),
                               Q[:, 2 * t + b, :, :].rearrange("p c q -> p (c q)"),
                               keys(u)[:, :, b * S:(b + 1) * S], start=True, stop=True).then_inc(scored, 1)
                    if step == "turn":
                        pe.wait_ge(exped, due(exped, 2))
                        for h in range(2):
                            ps = fill(2 + h, pt_ready)
                            for p in range(4):
                                last = pe.transpose(tile(ps, p), pr[:, u % 2, 4 * h + p, :, :].rearrange(
                                    "p b k -> p (b k)"), ident)
                            last.then_inc(turned, 1)
                        at_["p", u] = due.now(pt_ready)
                    if step == "values":
                        pe.wait_ge(pt_ready, at_["p", u])
                        ps = fill(6, on_ready)
                        for p in range(8):
                            last = mm(ps[:, p * blk:(p + 1) * blk], pT[:, u % 2, p, :], V[:, t, 8 * s_ + p, :],
                                      start=True, stop=True)
                        last.then_inc(valued, 1)
                        at_["on", t] = due.now(on_ready)
                    if step == "fold":
                        pe.wait_ge(on_ready, at_["on", t])
                        ps = fill(4, o_ready)
                        for b in range(2):
                            last = mm(ps[:, b * S:(b + 1) * S], ON[:, t, b, :], w("fold"), start=True, stop=True)
                        last.then_inc(folded, 1)
                        at_["o", t] = due.now(o_ready)
                    if step == "residual" and a:
                        pe.wait_ge(o_ready, at_["o", t])
                        mm(fill(7, y_used)[:, 0:P], oT[:, t % 2, :], w(f"{name}.o"), start=True, stop=True).then_inc(y_full, 1)
                    if step == "finish":
                        pe.wait_ge(x_ready, due(x_ready))
                        x_to_features(X, t)
                        at_["x", t] = due.now(xt_ready)

            def first_ffn(l):
                pe.wait_ge(f0_in if l == 0 else f1_in, 16)
                o = {}
                for t in range(NT):
                    pe.wait_ge(xt_ready, due.now(xt_ready) - (NT - 1 - t))
                    h = HT[:, 2 * t:2 * t + 2, :].rearrange("p b k -> p (b k)")
                    for i in range(2):
                        mm(fill(4 * (1 - t % 2) + i, raw_ready)[:, :], h,
                           early_w(f"f{l}.wqkv", 512 * i, 512 * i + 512), start=True, stop=True).then_inc(qk_full, 1)
                    mm(fill(6 + t % 2, v2_ready)[:, :], h, early_w(f"f{l}.wqkv", 1024, 1536),
                       start=True, stop=True).then_inc(v2_full, 1)
                    o["v", t] = due.now(v2_ready)
                for step, t in local_order(l, "pe"):
                    if step == "turn_qk":
                        for i, used in enumerate((qm_ready, kt_ready)):
                            z = (zr_ready, zk_ready)[i]
                            pe.wait_ge(z, due(z))
                            ps = fill(2 + i, used)
                            for p in range(4):
                                last = pe.transpose(tile(ps, p), RAW[:, t, i, p * P:(p + 1) * P], ident)
                            last.then_inc(rot_full, 1)
                            o["qk"[i], t] = due.now(used)
                    if step == "scores":
                        pe.wait_ge(qm_ready, o["q", t])
                        pe.wait_ge(kt_ready, o["k", t])
                        ps = fill(0, capped)
                        for p in range(4):
                            for b in range(2):
                                last = mm(ps[:, p * P + b * S:p * P + (b + 1) * S],
                                          QMs[t % 2][:, p, b, :, :].rearrange("p c q -> p (c q)"),
                                          KT[t % 2][:, p, b * S:(b + 1) * S], start=True, stop=True)
                        last.then_inc(scored, 1)
                    if step == "turn":
                        pe.wait_ge(pn_ready, due(pn_ready))
                        ps = fill(2, pm_ready)
                        for p in range(4):
                            last = pe.transpose(tile(ps, p), PR(t)[:, p * P:(p + 1) * P], ident)
                        last.then_inc(turned, 1)
                        o["p", t] = due.now(pm_ready)
                    if step == "values":
                        pe.wait_ge(pm_ready, o["p", t])
                        pe.wait_ge(v2_ready, o["v", t])
                        for h, b in enumerate((1, 6)):
                            ps = fill(b, ot_ready)
                            for p in (2 * h, 2 * h + 1):
                                last = mm(ps[:, (p % 2) * 256:(p % 2) * 256 + 256], VS[:, t, p * P:(p + 1) * P],
                                          PM[:, p, :, :].rearrange("p b n -> p (b n)"), start=True, stop=True)
                            last.then_inc(valued2, 1)
                        o["o", t] = due.now(ot_ready)
                    if step == "out":
                        pe.wait_ge(ot_ready, o["o", t])
                        ps = fill(7, x1_ready)
                        o["x", t] = due.now(x1_ready)
                        for p in range(4):
                            last = mm(ps[:, 0:P], oT0[:, t % 2, p, :, :].rearrange("p b q -> p (b q)"),
                                      early_w(f"f{l}.wo", p * P, (p + 1) * P), start=(p == 0), stop=(p == 3))
                        last.then_inc(y_full, 1)
                    if step == "shift":
                        pe.wait_ge(x1_ready, o["x", t])
                        pe.transpose(fill(3, hs_ready)[:, 0:P], X1[:, t, :], ident).then_inc(shifted, 1)
                        o["s", t] = due.now(hs_ready)
                    if step == "stats":
                        pe.wait_ge(hs_ready, o["s", t])
                        pe.transpose(fill(3, back_used)[:, 0:P], HS[:, t % 2, :, :].rearrange("p b k -> p (b k)"),
                                     ident).then_inc(restored, 1)
                    if step == "norm":
                        pe.wait_ge(hn_ready, due(hn_ready))
                        pe.transpose(fill(3, h2_ready)[:, 0:P], res[:, t % 2, :], ident).then_inc(normed, 1)
                        o["h2", t] = due.now(h2_ready)
                    if step == "up":
                        pe.wait_ge(h2_ready, o["h2", t])
                        for i, b in enumerate((4, 5)):
                            ps = fill(b, h_ready if i == 0 else act_ready)
                            for c, (a, n) in enumerate(CH):
                                last = mm(ps[0:n, c * P:(c + 1) * P], early_w(f"f{l}.w1", i * HID + a, i * HID + a + n),
                                          tile(XT, t), start=True, stop=True)
                            last.then_inc(up_full, 1)
                        o["h", t] = due.now(h_ready)
                    if step == "down":
                        pe.wait_ge(h_ready, o["h", t])
                        ps = fill(6, yf_ready)
                        for c, (_, n) in enumerate(CH):
                            last = mm(ps[:, 0:P], early_w(f"f{l}.w2", c * P, (c + 1) * P)[0:n, :],
                                      tile(sm[0:n, 2 + t % 2, :], c), start=(c == 0), stop=(c == 2))
                        last.then_inc(down_full, 1)
                        o["yf", t] = due.now(yf_ready)
                    if step == "again":
                        pe.wait_ge(yf_ready, o["yf", t])
                        pe.transpose(fill(7, x1_ready)[:, 0:P], tile(YF, t), ident).then_inc(y_full, 1)
                        o["x", t] = due.now(x1_ready)
                    if step == "feed":
                        pe.wait_ge(x1_ready, o["x", t])
                        x_to_features(XB, t)
                due(exped, NT)
                pe.wait_ge(yf_ready, due.now(yf_ready))

            def gelu_ffn():
                pe.wait_ge(g_in, 16)
                pe.wait_ge(xt_ready, due.now(xt_ready))
                for c in range(9):
                    if c < 8:
                        mm(fill(4 + c % 2, act_ready)[:, :], early_w("g.w1", c * P, (c + 1) * P), XT[:, :],
                           start=True, stop=True).then_inc(up_full, 1)
                    if c >= 1:
                        pe.wait_ge(act_ready, due.now(act_ready) - (1 if c < 8 else 0))
                        ps = fill(6, yf_ready) if c == 1 else OB
                        last = mm(ps[:, :], early_w("g.w2", (c - 1) * P, c * P), G[:, (c - 1) % 4, :],
                                  start=(c == 1), stop=(c == 8))
                last.then_inc(down_full, 1)
                pe.wait_ge(yf_ready, due.now(yf_ready))

            def logits(name, n):
                pe.wait_ge(xt_ready, due.now(xt_ready))
                ps = fill(6, lg_ready)
                for t in range(NT):
                    last = mm(ps[:, t * n:(t + 1) * n], tile(XT, t), w(name), start=True, stop=True)
                last.then_inc(logit_full, 1)

            def top1_ffn():
                logits("e2.r", NE2)
                h_at, up_at = {}, {}

                def up(k):
                    if k == 0:
                        rhs = XT[:, :]
                    else:
                        pe.wait_ge(xe_ready, k)
                        rhs = G[:, k % 2, :]
                    for c in range(2):
                        for i, b in enumerate((4 + c, 2 + c)):
                            ps = fill(b, act_ready if i == 0 else h_ready)
                            lhs = (w("e2.g" if i == 0 else "e2.u", c * P, (c + 1) * P) if k == 0 else
                                   gu_w[:, k - 1, i * NF2 + c * P:i * NF2 + (c + 1) * P])
                            mm(ps[:, :], lhs, rhs, start=True, stop=True).then_inc(up_full, 1)
                    h_at[k] = due.now(h_ready)

                def choose(k):
                    mm(fill(0, xe_ready)[:, :], pick[:, k - 1, :], oneT[:, :], start=True,
                       stop=True).then_inc(picked, 1)

                def down_(k):
                    pe.wait_ge(h_ready, h_at[k])
                    for c in range(2):
                        first, stop = (k == 0 and c == 0), (k == NE2 and c == 1)
                        ps = fill(6, yf_ready) if first else OB
                        lhs = w("e2.d", c * P, (c + 1) * P) if k == 0 else dn_w[:, k - 1, c, :]
                        last = mm(ps[:, :], lhs, sm[:, 2 * (k % 2) + c, :], start=first, stop=stop)
                    if k == NE2:
                        last.then_inc(down_full, 1)

                up(0)
                down_(0)
                pe.wait_ge(one_ready, due(one_ready))
                ps = fill(1, choice_ready)
                for t in range(NT):
                    last = pe.transpose(ps[0:NE2, t * P:(t + 1) * P], one[:, t, :], ident)
                last.then_inc(choice_full, 1)
                pe.wait_ge(xs_ready, due(xs_ready))
                for t in range(NT):
                    x_to_features(XB, t, 5)
                pe.wait_ge(*hold[1])
                pe.wait_ge(e2_in, 16 * 12)
                choose(1)
                for k in range(1, NE2 + 1):
                    up(k)
                    if k < NE2:
                        choose(k + 1)
                    if k >= 2:
                        down_(k - 1)
                down_(NE2)
                pe.wait_ge(yf_ready, due.now(yf_ready))

            def top2_ffn():
                logits("e3.r", NE3)
                act_at = {}

                def up(e):
                    for c in range(4):
                        mm(fill(4 + c % 2, act_ready)[:, :], w1_w[:, e, c * P:(c + 1) * P], XT[:, :],
                           start=True, stop=True).then_inc(up_full, 1)
                    act_at[e] = due.now(act_ready)

                def down_(e):
                    pe.wait_ge(act_ready, act_at[e])
                    h = G if e % 2 == 0 else sm
                    ps = fill(2 + e % 2, o3_used)
                    for t in range(NT):
                        for c in range(4):
                            last = mm(tile(ps, t), tile(h[:, c, :], t), w2_w[:, e, c, :],
                                      start=(c == 0), stop=(c == 3))
                    last.then_inc(o3_full, 1)

                pe.wait_ge(e3_in, 16 * 10)
                up(0)
                pe.wait_ge(one_ready, due(one_ready))
                ps = fill(0, gt_ready)
                for t in range(NT):
                    last = pe.transpose(ps[0:NE3, t * P:(t + 1) * P], gate[:, t, 0:NE3], ident)
                last.then_inc(gate_full, 1)
                pe.wait_ge(*hold[0])
                ps = fill(1, acc_ready)
                for t in range(NT):
                    last = mm(tile(ps, t), tile(gT, t), w("e3.b2")[0:NE3, :], start=True, stop=True)
                last.then_inc(b2_full, 1)
                for e in range(1, NE3 + 1):
                    if e < NE3:
                        up(e)
                    down_(e - 1)

            pe.wait_ge(rest_in, 16)
            pe.wait_ge(init_pool, 1)
            with pe.Fori(0, 2):
                start_of_turn()
                pe.wait_ge(oth_ready, due(oth_ready))
                chain("a0", "x0")
                pe.wait_ge(init_dve, 1)
                pe.wait_ge(init_act, 1)
                first_ffn(0)
                first_ffn(1)
                chain("f1", "a1", "x1")
                gelu_ffn()
                chain("gelu", "ema", "x2")
                top1_ffn()
                chain("top1", "a3", "x3")
                top2_ffn()
                end_of_turn()

        @block.scalar
        def _(act):
            due = Tally()

            def end_of_turn():
                act.drain().then_inc(turn_done, 1)
                due.count.clear()

            def start_of_turn():
                act.wait_ge(go_act, 1)
                act.sem_clear(go_act)

            def inverse_roots(dst, src):
                act.wait_ge(ss_ready, due(ss_ready))
                act.activation(src, src, ACT.Ln).then_inc(act_link, 1)
                act.wait_ge(act_link, due(act_link))
                act.activation(dst, src, ACT.Exp, scale=-0.5).then_inc(rn_ready, 1)

            act.wait_ge(first_in, 16)
            for step, g in lagged(MIX0, 8):
                j = g % 2
                if step == "project":
                    act.wait_ge(z_ready, g + 1)
                    act.activation(SQ[:, j, :], Z[:, j, 0:256], ACT.Square).then_inc(sq_ready, 1)
                    act.activation(SG[:, j, :], Z[:, j, 384:416], ACT.Exp, scale=-1.0).then_inc(sig_ready, 1)
                    inverse_roots(RN[:, j, :], SS[:, j, :])
                if step == "state":
                    act.wait_ge(qT_full, g + 1)
                    act.copy(QTp[:, j, :], T0[:, 0:P]).then_inc(qT_ready, 1)
                if step == "mix":
                    act.wait_ge(mix_full, g + 1)
                    act.copy(OTall[:, :, g * 8:g * 8 + 8],
                             OB[:, 0:P].rearrange("p (j i) -> p i j", i=16)).then_inc(ot_stored, 1)
            end_of_turn()

            def stream_out(t, shifted_too):
                act.wait_ge(x_turned, due(x_turned))
                if shifted_too:
                    src = OB[:, 0:P].rearrange("p (b k) -> p b k", b=2)
                    act.copy(HT[0:S, 2 * t:2 * t + 2, :], src[0:S])
                    act.copy(HT[S:P, 2 * t:2 * t + 2, 1:S], src[S:P, :, 0:S - 1]).then_inc(xt_ready, 1)
                else:
                    act.copy(tile(XT, t), OB[:, 0:P]).then_inc(xt_ready, 1)

            def chain(*stages):
                for name, step, u, t, s_ in chain_order(stages, "act"):
                    a = att.get(name)
                    if step == "inner":
                        act.wait_ge(up_full, due(up_full))
                        act.activation(tile(G[:, 0, :], t), F0[:, 0:P], ACT.Relu, bias=w("ema.bin")).then_inc(act_ready, 1)
                    if step == "kv":
                        act.wait_ge(k_full, due(k_full))
                        pair = w("pair16") if a["heads"] == 16 else w("pair32")
                        for p in range(8):
                            g = 8 * s_ + p
                            last = act.activation(keys(u)[:, p, :], F1[:, 0:P], ACT.Identity,
                                                  bias=bkm[:, a["i"], g:g + 1], scale=pair[:, g:g + 1])
                        last.then_inc(k_split, 1)
                    if step == "rel":
                        for b in (2 * t, 2 * t + 1):
                            act.wait_ge(rel_full, b + 1)
                            if b >= 4:
                                act.wait_ge(rel_stored[b % 2], 16 * ((b - 4) // 2 + 1))
                            act.copy(G[:, b % 4, :], bank[6 + b % 2][:, :]).then_inc(rel_ready, 1)
                    if step == "scores":
                        ready = centered if a["mask"] is None else pcentered
                        due(scored, 2)
                        for b in range(2):
                            act.wait_ge(ready, due(ready))
                            act.activation(pr[:, u % 2, :, b, :],
                                           sm[:, 2 * (u % 2) + b, :].rearrange("p (h k) -> p h k", h=8),
                                           ACT.Exp, scale=a["scale"]).then_inc(exped, 1)
                    if step == "turn":
                        for h in range(2):
                            act.wait_ge(turned, due(turned))
                            act.copy(pT[:, u % 2, 4 * h:4 * h + 4, :],
                                     bank[2 + h][:, :].rearrange("p (h n) -> p h n", h=4)).then_inc(pt_ready, 1)
                    if step == "fold":
                        act.wait_ge(folded, due(folded))
                        act.copy(oT[:, t % 2, :], F0[:, 0:P]).then_inc(o_ready, 1)
                    if step == "finish":
                        stream_out(t, name == "x0")

            def output():
                act.wait_ge(down_full, due(down_full))
                act.copy(YF[:, :], OB[:, :]).then_inc(yf_ready, 1)

            def first_ffn(l):
                for t in range(NT):
                    for i in range(2):
                        u = 2 * t + i
                        if u >= 4:
                            act.wait_ge(summed, 2 * NT * l + u - 3)
                        act.wait_ge(qk_full, due(qk_full))
                        act.activation(sm[:, u % 4, :], bank[4 * (1 - t % 2) + i][:, :], ACT.Square).then_inc(squared, 1)
                        act.copy(RAW[:, t, i, :], bank[4 * (1 - t % 2) + i][:, :]).then_inc(raw_ready, 1)
                    act.wait_ge(v2_full, due(v2_full))
                    act.copy(VS[:, t, :], bank[6 + t % 2][:, :]).then_inc(v2_ready, 1)
                inverse_roots(rn[:, :, :], ss[:, :, :])
                if l == 0:
                    act.wait_ge(zeroed, 2)
                for step, t in local_order(l, "act"):
                    if step == "turn_qk":
                        if t >= 2:
                            act.wait_ge(scored, due(scored))
                        act.wait_ge(rot_full, due(rot_full))
                        for c in range(2):
                            r = slice(c * S, (c + 1) * S)
                            last = act.copy(QMs[t % 2][r, :, :, c, :].rearrange("p a b q -> p (a b) q"),
                                            T0[r, :].rearrange("p (a q) -> p a q", q=S))
                        last.then_inc(qm_ready, 1)
                        act.wait_ge(rot_full, due(rot_full))
                        act.copy(KT[t % 2], T1[:, :].rearrange("p (a n) -> p a n", a=4)).then_inc(kt_ready, 1)
                    if step == "scores":
                        if t >= 2:
                            act.wait_ge(turned, due.now(turned) + 1)
                        act.wait_ge(pcentered, due(pcentered))
                        act.activation(PR(t), sm[:, t % 2, :], ACT.Exp,
                                       scale=8.0).then_inc(exped, 1)
                    if step == "turn":
                        if t >= 1:
                            act.wait_ge(valued2, 2 * (NT * l + t))
                        act.wait_ge(turned, due(turned))
                        for b in range(2):
                            r = slice(b * S, (b + 1) * S)
                            last = act.copy(PM[r, :, b, :], T0[r, :].rearrange("p (a n) -> p a n", a=4))
                        last.then_inc(pm_ready, 1)
                    if step == "values":
                        for h, bk in enumerate((S1, OB)):
                            act.wait_ge(valued2, 2 * (NT * l + t) + h + 1)
                            for c in range(2):
                                r = slice(c * S, (c + 1) * S)
                                last = act.copy(
                                    oT0[r, t % 2, 2 * h:2 * h + 2, :, :].rearrange("p a b q -> p (a b) q"),
                                    bk[r, :].rearrange("p (a c q) -> p a c q", c=2, q=S)[:, :, c, :])
                            last.then_inc(ot_ready, 1)
                    if step == "shift":
                        act.wait_ge(shifted, due(shifted))
                        src = T1[:, 0:P].rearrange("p (b k) -> p b k", b=2)
                        act.copy(HS[0:S, t % 2, :, :], src[0:S])
                        act.copy(HS[S:P, t % 2, :, 1:S], src[S:P, :, 0:S - 1]).then_inc(hs_ready, 1)
                    if step == "norm":
                        act.wait_ge(normed, due(normed))
                        act.activation(tile(XT, t), T1[:, 0:P], ACT.Identity, bias=w(f"f{l}.b"),
                                       scale=w(f"f{l}.g")).then_inc(h2_ready, 1)
                    if step == "up":
                        act.wait_ge(up_full, due(up_full, 2))
                        for c, (_, n) in enumerate(CH):
                            last = act.activation(tile(sm[0:n, 2 + t % 2, :], c), tile(F1[0:n, :], c), ACT.Gelu,
                                                  bias=w(f"f{l}.b1g", c, c + 1)[0:n])
                        last.then_inc(act_ready, 1)
                    if step == "down":
                        act.wait_ge(down_full, due(down_full))
                        act.activation(tile(YF, t), OB[:, 0:P], ACT.Identity, bias=w(f"f{l}.b2")).then_inc(yf_ready, 1)
                    if step == "feed":
                        stream_out(t, True)
                due(scored, 2)

            def gelu_ffn():
                for c in range(8):
                    act.wait_ge(up_full, due(up_full))
                    act.activation(G[:, c % 4, :], bank[4 + c % 2][:, :], ACT.Gelu_apprx_tanh).then_inc(act_ready, 1)
                output()

            def top1_ffn():
                def gates(k):
                    for c in range(2):
                        act.wait_ge(up_full, due(up_full))
                        act.activation(sm[:, 2 * (k % 2) + c, :], bank[4 + c][:, :], ACT.Silu).then_inc(act_ready, 1)
                        due(up_full)
                act.wait_ge(lg_ready, due(lg_ready))
                act.activation(sig[:, :, :], lg[:, :, :], ACT.Sigmoid).then_inc(sig_ready, 1)
                gates(0)
                act.wait_ge(choice_full, due(choice_full))
                act.copy(oneT[:, :], S1[0:NE2, :]).then_inc(choice_ready, 1)
                for t in range(NT):
                    act.wait_ge(x_turned, due(x_turned))
                    act.copy(HT[:, 2 * t:2 * t + 2, :].rearrange("p b k -> p (b k)"), F1[:, 0:P]).then_inc(xt_ready, 1)
                for k in range(1, NE2 + 1):
                    gates(k)
                output()

            def top2_ffn():
                due(lg_ready)

                def gelus(e):
                    h = G if e % 2 == 0 else sm
                    for c in range(4):
                        act.wait_ge(up_full, due(up_full))
                        act.activation(h[:, c, :], bank[4 + c % 2][:, :], ACT.Gelu,
                                       bias=w("e3.b1", 4 * e + c, 4 * e + c + 1)).then_inc(act_ready, 1)
                act.wait_ge(gap_ready, due(gap_ready))
                act.activation(col[:, 4, :], col[:, 3, :], ACT.Exp).then_inc(sig_ready, 1)
                gelus(0)
                act.wait_ge(gate_full, due(gate_full))
                act.copy(gT[:, :], S0[0:NE3, :]).then_inc(gt_ready, 1)
                for e in range(1, NE3):
                    gelus(e)

            act.copy(pick[:, :, :], bc(w("ident")[0:NE2, 0:NE2], [NE2, NE2, P], 2)).then_inc(init_act, 1)
            act.wait_ge(rest_in, 16)
            act.wait_ge(init_pool, 1)
            with act.Fori(0, 2):
                start_of_turn()
                act.wait_ge(zeroed, 1)
                chain("a0", "x0")
                first_ffn(0)
                first_ffn(1)
                chain("f1", "a1", "x1")
                gelu_ffn()
                chain("gelu", "ema", "x2")
                top1_ffn()
                chain("top1", "a3", "x3")
                top2_ffn()
                end_of_turn()

        @block.vector
        def _(dve):
            due = Tally()

            def link(ins):
                ins.then_inc(dve_link, 1)
                dve.wait_ge(dve_link, due(dve_link))

            def end_of_turn():
                dve.drain().then_inc(turn_done, 1)
                due.count.clear()

            def start_of_turn():
                dve.wait_ge(go_dve, 1)
                dve.sem_clear(go_dve)

            tt, ts, stt = dve.tensor_tensor, dve.tensor_scalar, dve.scalar_tensor_tensor
            dve.wait_ge(first_in, 16)
            for step, g in lagged(MIX0, 8):
                j = g % 2
                if step == "project":
                    if g >= 2:
                        dve.wait_ge(sig_ready, g - 1)
                        dve.wait_ge(vw_ready, g - 1)
                    dve.wait_ge(proj_full, g + 1)
                    tt(Z[:, j, :], bank[j][:, 0:416], w("Ab"), ALU.add).then_inc(z_ready, 1)
                    dve.wait_ge(sq_ready, g + 1)
                    link(dve.tensor_reduce(SS[:, j, :], SQ[:, j, :].rearrange("p (h d) -> p h d", d=8), AX.X,
                                           ALU.add))
                    ts(SS[:, j, :], SS[:, j, :], 1e-24, None, ALU.max).then_inc(ss_ready, 1)
                if step == "scale":
                    dve.wait_ge(rn_ready, g + 1)
                    dve.wait_ge(sig_ready, g + 1)
                    if g >= 2:
                        dve.wait_ge(vj_ready, g - 1)
                        dve.wait_ge(state_full, 2 * g - 2)
                    link(ts(SG[:, j, :], SG[:, j, :], 1.0, None, ALU.add))
                    link(dve.reciprocal(SG[:, j, :], SG[:, j, :]))
                    link(tt(RN[:, j, 0:16], RN[:, j, 0:16], SG[:, j, 16:32], ALU.mult))
                    tt(QK[:, j, :].rearrange("p (h d) -> p h d", d=8),
                       Z[:, j, 0:256].rearrange("p (h d) -> p h d", d=8),
                       bc(RN[:, j, :], [P, 32, 8], 2), ALU.mult).then_inc(qk_ready, 1)
                    tt(VW[:, j, :].rearrange("p (h d) -> p h d", d=8),
                       Z[:, j, 256:384].rearrange("p (h d) -> p h d", d=8),
                       bc(SG[:, j, 0:16], [P, 16, 8], 2), ALU.mult).then_inc(vw_ready, 1)
                if step == "state":
                    if g >= 2:
                        dve.wait_ge(mix_full, g - 1)
                    for h in range(2):
                        dve.wait_ge(state_full, 2 * g + h + 1)
                        tt(AM[:, j, 4 * h:4 * h + 4, :], bank[4 + h][:, :].rearrange("p (s n) -> p s n", s=4),
                           bc(w("blocks"), [P, 4, P], 1), ALU.mult).then_inc(am_ready, 1)
            end_of_turn()

            dve.wait_ge(rest_in, 16)
            for name in ATT:
                a = att[name]
                n = a["heads"] // 2
                ts(bkm[:, a["i"], 0:n], w("pair16") if n == 8 else w("pair32"), w(f"{name}.bk"), None, ALU.mult)
            tt(relp[:, :, :], bc(w("rel"), [P, 8, S], 1), bc(w("pair16"), [P, 8, S], 2), ALU.mult)
            for l in range(2):
                for i, (table, scale) in enumerate((("cosq", "qs"), ("sinq", "qsr"), ("cosk", "ks"), ("sink", "ksr"))):
                    tt(rot[:, l, i, :], w(table), w(f"f{l}.{scale}"), ALU.mult)
            ts(w("not_first"), w("not_first"), w("decay"), None, ALU.mult)
            ts(omix[:, :], w("mix"), -1.0, 1.0, ALU.mult, ALU.add).then_inc(init_dve, 1)
            dve.wait_ge(init_dve, 1)

            def stats(src, t):
                link(dve.bn_stats(st[:, t % 2, :], src))
                dve.bn_aggr(mv[:, t % 2, :], st[:, t % 2, :]).then_inc(var_ready, 1)

            def finish(src, t):
                dve.wait_ge(rstd_ready, due(rstd_ready))
                ts(X[:, t, :], src, mv[:, t % 2, 0:1], rstd[:, t % 2, :], ALU.subtract, ALU.mult).then_inc(x_ready, 1)
                due(x_ready)

            def own_norms_done():
                if due.now(x_ready):
                    dve.wait_ge(x_ready, due.now(x_ready))

            def mask_x0():
                dve.wait_ge(masks_in, 16 * 6)
                c0 = cap[:, 0, :, :]
                link(tt(c0, m_row[:, :, :], bc(m_col[:, :], [P, NB, S], 2), ALU.mult))
                link(ts(c0, c0, 0.0, BIG, ALU.is_gt, ALU.mult))
                link(ts(c0, c0, -BIG, 10.0, ALU.add, ALU.mult))
                link(ts(c0, c0, BIG, None, ALU.add))

            def masks_x2_x3():
                c1, c2 = cap[:, 1, :, :], cap[:, 2, :, :]
                link(tt(c1, m_pad[:, :, :], bc(m_att[:, :], [P, NB, S], 1), ALU.max))
                f = sm[:, 0, :].rearrange("p (b k) -> p b k", b=NB)
                link(ts(f, c1, 0.0, BIG, ALU.is_equal, ALU.mult))
                link(stt(c1, c1, -1e9 / att["x2"]["scale"], f, ALU.mult, ALU.add))
                link(ts(f, m_ik[:, :, :], 0.0, -1e9 / att["x3"]["scale"], ALU.is_equal, ALU.mult))
                link(ts(c2, m_ik[:, :, :], 0.0, BIG, ALU.not_equal, ALU.mult))
                link(tt(c2, c2, f, ALU.add))

            def chain(*stages):
                used = {}
                cleared = False
                xb_at = {}
                for name, step, u, t, s_ in chain_order(stages, "dve"):
                    a = att.get(name)
                    if a:
                        wide = a["heads"] == 16
                        n = 16 if wide else 8
                        d = n // 2
                        V, blk = (VX, 34) if wide else (VX32, 18)
                        par = w("par16") if wide else w("par32")
                    if step == "mix":
                        dve.wait_ge(xt_ready, XT_BEFORE_EMA - NT + t + 1)
                        x, y = tile(XT, t), tile(YF, t)
                        link(ts(y, x, w("mix"), None, ALU.mult))
                        x, y = (v.rearrange("p (b k) -> p b k", b=2) for v in (x, y))
                        stt(y[:, :, 1:S], x[:, :, 0:S - 1], omix[:, :], y[:, :, 1:S], ALU.mult, ALU.add).then_inc(inp_ready, 1)
                    if step == "inner":
                        dve.wait_ge(act_ready, due(act_ready))
                        dve.tensor_tensor_scan(tile(G[:, 1, :], t), tile(w("not_first"), t), tile(G[:, 0, :], t), 0.0,
                                               ALU.mult, ALU.add).then_inc(ema_ready, 1)
                    if step in ("project", "back") and name in BIASED and s_ == 0:
                        xb_at[name, t] = due(xb_ready)
                    if step == "kv" and s_ == 0:
                        dve.wait_ge(qv_full, due(qv_full))
                        for b in range(2):
                            r = slice(b * S, (b + 1) * S)
                            last = tt(V[r, t, :, b * n:(b + 1) * n], F0[r, 0:P].rearrange("p (h d) -> p h d", d=n),
                                      w(f"{name}.bv")[r].rearrange("p (h d) -> p h d", d=n), ALU.add)
                        last.then_inc(qv_split, 1)
                    if step == "project" and s_ == 0:
                        dve.wait_ge(qv_full, due(qv_full))
                        for c in range(2):
                            last = ts(Q[:, 2 * t:2 * t + 2, c, :], F0[:, 0:P].rearrange("p (b q) -> p b q", b=2),
                                      w(f"{name}.bq"), par[:, c:c + 1], ALU.add, ALU.mult)
                        last.then_inc(qv_split, 1)
                    if step == "scores":
                        if name == "x0" and u == 0:
                            mask_x0()
                        if u % 2 in used:
                            dve.wait_ge(exped, used[u % 2])
                        for b in range(2):
                            slot = 2 * (u % 2) + b
                            dve.wait_ge(scored, due(scored))
                            sc = bank[b][:, :].rearrange("p (h k) -> p h k", h=8)
                            dst = sm[:, slot, :].rearrange("p (h k) -> p h k", h=8)
                            top = mx[:, slot, :]
                            if a["mask"] is None:
                                link(dve.tensor_reduce(top, sc, AX.X, ALU.max))
                                tt(dst, sc, bc(top, [P, 8, S], 2), ALU.subtract).then_inc(centered, 1)
                                continue
                            if a["mask"] == "rel":
                                dve.wait_ge(rel_back[(2 * t + b) % 4], 32 * ((2 * t + b) // 4 + 1))
                                tt(sm[:, slot, :], bank[b][:, :], RB[(2 * t + b) % 4], ALU.add).then_inc(rel_added, 1)
                                dve.wait_ge(rel_added, due(rel_added))
                                link(tt(dst, dst, bc(w("causal"), [P, 8, S], 1), ALU.min))
                            else:
                                tt(dst, sc, bc(cap[:, a["mask"], 2 * t + b, :], [P, 8, S], 1),
                                   ALU.min).then_inc(capped, 1)
                                dve.wait_ge(capped, due(capped))
                            dve.tensor_reduce(top, dst, AX.X, ALU.max).then_inc(mx_ready, 1)
                        used[u % 2] = due(exped, 2)
                    if step == "values":
                        dve.wait_ge(valued, due(valued))
                        o = OB[:, 0:8 * blk].rearrange("p (h n) -> p h n", h=8)
                        link(dve.reciprocal(rs[:, u % 2, :, :], o[:, :, 2 * n:2 * n + 2]))
                        if not cleared:
                            dve.wait_ge(on_clear, due(on_clear))
                            cleared = True
                        for c in range(2):
                            r = slice(c * S, (c + 1) * S)
                            src = o[r, :, 0:2 * n].rearrange("p h (b c d) -> p b c h d", b=2, c=2)
                            dst = ON[r, t, :, :].rearrange("p b (h c d) -> p b c h d", c=2, d=d)
                            last = tt(dst[:, :, c, 8 * s_:8 * s_ + 8, :], src[:, :, c, :, :],
                                      bc(rs[r, u % 2, :, :].rearrange("p h b -> p b h"), [S, 2, 8, d], 3), ALU.mult)
                        last.then_inc(on_ready, 1)
                    if step == "residual":
                        out_ = res[:, t % 2, :]
                        if name in BIASED:
                            dve.wait_ge(xb_ready, xb_at[name, t])
                        own_norms_done()
                        dve.wait_ge(y_full, due(y_full))
                        if name == "x0":
                            stt(out_, YB[:, 0:P], m_tok[:, t:t + 1], XB[:, t, :], ALU.mult, ALU.add).then_inc(y_used, 1)
                        elif name == "gelu":
                            stt(out_, YB[:, 0:P], ew[:, t:t + 1], X[:, t, :], ALU.mult, ALU.add).then_inc(y_used, 1)
                        else:
                            other = XB if name in BIASED else X1 if name == "f1" else X
                            tt(out_, YB[:, 0:P], other[:, t, :], ALU.add).then_inc(y_used, 1)
                        dve.wait_ge(y_used, due(y_used))
                        if name == "f1":
                            link(tt(out_, out_, X[:, t, :], ALU.add))
                        stats(out_, t)
                    if step == "finish":
                        finish(res[:, t % 2, :], t)

            def first_ffn(l):
                cur = X if l == 0 else XB
                def swapped(t, i):
                    dve.wait_ge(raw_ready, 2 * (NT * l + t) + i + 1)
                    z = RAW[:, t, i, :].rearrange("p (h c d) -> p h c d", h=8, c=2)
                    m = M2[:, (2 * t + i) % 4, :].rearrange("p (h c d) -> p h c d", h=8, c=2)
                    table = rot[:, l, 2 * i + 1, :].rearrange("p (c d) -> p c d", c=2)
                    for c in range(2):
                        last = tt(m[:, :, c, :], z[:, :, 1 - c, :], bc(table[:, c, :], [P, 8, 32], 1), ALU.mult)
                    last.then_inc(m2_ready, 1)

                def rotate(t, i):
                    dve.wait_ge(m1_ready, due(m1_ready))
                    dve.wait_ge(m2_ready, due(m2_ready))
                    tt(RAW[:, t, i, :], M1[:, (2 * t + i) % 4, :], M2[:, (2 * t + i) % 4, :],
                       ALU.add).then_inc(rotated, 1)

                for t in range(NT):
                    for i in range(2):
                        dve.wait_ge(squared, due(squared))
                        dve.tensor_reduce(ss[:, t, 8 * i:8 * i + 8],
                                          sm[:, (2 * t + i) % 4, :].rearrange("p (h d) -> p h d", d=S), AX.X,
                                          ALU.add).then_inc(summed, 1)
                        if t < 2:
                            swapped(t, i)
                    for i in range(2):
                        if t < 2:
                            rotate(t, i)
                dve.wait_ge(summed, due(summed, 2 * NT))
                ts(ss[:, :, :], ss[:, :, :], 1e-24, None, ALU.max).then_inc(ss_ready, 1)
                for step, t in local_order(l, "dve"):
                    if step == "rotate":
                        if t >= 2:
                            swapped(t, 0)
                            swapped(t, 1)
                            rotate(t, 0)
                            rotate(t, 1)
                        if t == 0:
                            dve.wait_ge(rn_ready, due(rn_ready))
                        dve.wait_ge(rotated, 2 * NT * l + 2 * t + 1)
                        zr = RAW[:, t, 0, :].rearrange("p (h d) -> p h d", d=S)
                        tt(zr, zr, bc(rn[:, t, 0:8], [P, 8, S], 2), ALU.mult).then_inc(zr_ready, 1)
                    if step == "scores":
                        dve.wait_ge(scored, due(scored))
                        tt(sm[:, t % 2, :].rearrange("p (h k) -> p h k", h=8),
                           S0[:, :].rearrange("p (h k) -> p h k", h=8), bc(w("causal"), [P, 8, S], 1),
                           ALU.min).then_inc(capped, 1)
                        dve.wait_ge(capped, due(capped))
                        dve.tensor_reduce(mx[:, t % 2, :], sm[:, t % 2, :].rearrange("p (h k) -> p h k", h=8), AX.X,
                                          ALU.max).then_inc(mx_ready, 1)
                    if step == "soft":
                        dve.wait_ge(exped, due(exped))
                        link(dve.tensor_reduce(mx[:, 2 + t % 2, :], PR(t).rearrange("p (g k) -> p g k", g=8), AX.X,
                                               ALU.add))
                        dve.reciprocal(mx[:, 2 + t % 2, :], mx[:, 2 + t % 2, :]).then_inc(sum_ready, 1)
                    if step == "out":
                        dve.wait_ge(y_full, due(y_full))
                        tt(X1[:, t, :], YB[:, 0:P], cur[:, t, :], ALU.add).then_inc(x1_ready, 1)
                    if step == "stats":
                        dve.wait_ge(restored, due(restored))
                        dve.tensor_copy(res[:, t % 2, :], T1[:, 0:P]).then_inc(back_used, 1)
                        dve.wait_ge(back_used, due(back_used))
                        stats(res[:, t % 2, :], t)
                    if step == "norm":
                        dve.wait_ge(rstd_ready, due(rstd_ready))
                        ts(res[:, t % 2, :], res[:, t % 2, :], mv[:, t % 2, 0:1], rstd[:, t % 2, :], ALU.subtract,
                           ALU.mult).then_inc(hn_ready, 1)
                    if step == "up":
                        dve.wait_ge(act_ready, due(act_ready))
                        for c, (_, n) in enumerate(CH):
                            h = tile(sm[0:n, 2 + t % 2, :], c)
                            last = stt(h, tile(F0[0:n, :], c), w(f"f{l}.b1a", c, c + 1)[0:n], h, ALU.add, ALU.mult)
                        last.then_inc(h_ready, 1)
                    if step == "again":
                        dve.wait_ge(y_full, due(y_full))
                        tt(XB[:, t, :], YB[:, 0:P], X1[:, t, :], ALU.add).then_inc(x1_ready, 1)

            def gelu_ffn():
                masks_x2_x3()
                due(act_ready, 8)
                dve.wait_ge(ew_ready, due(ew_ready))

            def choose_first(dst, src, n, table):
                link(dve.tensor_reduce(col[:, 0, :], src, AX.X, ALU.max))
                link(tt(tmp[:, :, 0:n], src, bc(col[:, 0, :], [P, NT, n], 2), ALU.is_equal))
                link(tt(tmp[:, :, 0:n], tmp[:, :, 0:n], bc(table, [P, NT, n], 1), ALU.mult))
                link(dve.tensor_reduce(col[:, 1, :], tmp[:, :, 0:n], AX.X, ALU.max))
                return tt(dst, tmp[:, :, 0:n], bc(col[:, 1, :], [P, NT, n], 2), ALU.is_equal)

            def top1_ffn():
                dve.wait_ge(logit_full, due(logit_full))
                dve.tensor_copy(lg[:, :, :], OB[:, 0:NT * NE2].rearrange("p (t e) -> p t e", t=NT)).then_inc(lg_ready, 1)
                dve.wait_ge(lg_ready, due(lg_ready))
                choose_first(one[:, :, :], lg[:, :, :], NE2, w("down16")).then_inc(one_ready, 1)
                dve.wait_ge(one_ready, due(one_ready))
                dve.wait_ge(sig_ready, due(sig_ready))
                link(tt(gate[:, :, :], one[:, :, :], sig[:, :, :], ALU.mult))
                link(dve.tensor_reduce(col[:, 2, :], gate[:, :, :], AX.X, ALU.add))
                for t in range(NT):
                    last = ts(XB[:, t, :], X[:, t, :], col[:, 2, t:t + 1], None, ALU.mult)
                last.then_inc(xs_ready, 1)

                def hidden(k):
                    for c in range(2):
                        dve.wait_ge(act_ready, due(act_ready))
                        dve.wait_ge(up_full, UP_BEFORE_TOP1 + 4 * k + 2 * c + 2)
                        tt(sm[:, 2 * (k % 2) + c, :], bank[2 + c][:, :], sm[:, 2 * (k % 2) + c, :],
                           ALU.mult).then_inc(h_ready, 1)

                def tokens(k):
                    dve.wait_ge(picked, due(picked))
                    tt(G[:, k % 2, :], HT[:, :, :].rearrange("p b k -> p (b k)"), S0[:, :], ALU.mult).then_inc(xe_ready, 1)
                hidden(0)
                dve.wait_ge(xt_ready, XT_BEFORE_EMA + 3 * NT)
                tokens(1)
                for k in range(1, NE2 + 1):
                    if k < NE2:
                        tokens(k + 1)
                    hidden(k)

            def top2_ffn():
                dve.wait_ge(logit_full, due(logit_full))
                l8, g8 = lg[:, :, 0:NE3], gate[:, :, 0:NE3]
                dve.tensor_copy(l8, OB[:, 0:NT * NE3].rearrange("p (t e) -> p t e", t=NT)).then_inc(lg_ready, 1)
                dve.wait_ge(lg_ready, due(lg_ready))
                link(choose_first(one[:, :, 0:NE3], l8, NE3, w("down8")))
                link(dve.tensor_copy(col[:, 2, :], col[:, 0, :]))
                link(stt(l8, one[:, :, 0:NE3], -BIG, l8, ALU.mult, ALU.add))
                link(choose_first(two[:, :, 0:NE3], l8, NE3, w("down8")))
                tt(col[:, 3, :], col[:, 0, :], col[:, 2, :], ALU.subtract).then_inc(gap_ready, 1)
                dve.wait_ge(sig_ready, due(sig_ready))
                link(ts(col[:, 5, :], col[:, 4, :], 1.0, None, ALU.add))
                link(dve.reciprocal(col[:, 5, :], col[:, 5, :]))
                link(tt(col[:, 6, :], col[:, 5, :], col[:, 4, :], ALU.mult))
                link(tt(g8, one[:, :, 0:NE3], bc(col[:, 5, :], [P, NT, NE3], 2), ALU.mult))
                link(tt(two[:, :, 0:NE3], two[:, :, 0:NE3], bc(col[:, 6, :], [P, NT, NE3], 2), ALU.mult))
                tt(g8, g8, two[:, :, 0:NE3], ALU.add).then_inc(one_ready, 1)
                dve.wait_ge(one_ready, due(one_ready))
                dve.wait_ge(b2_full, 1)
                tt(XB[:, :, :], S1[:, :].rearrange("p (t n) -> p t n", t=NT), X[:, :, :], ALU.add).then_inc(acc_ready, 1)
                dve.wait_ge(acc_ready, 1)
                for e in range(NE3):
                    dve.wait_ge(o3_full, e + 1)
                    if e >= 1:
                        dve.wait_ge(o3_used, e)
                    for t in range(NT):
                        last = stt(XB[:, t, :], tile(bank[2 + e % 2], t), gate[:, t, e:e + 1], XB[:, t, :],
                                   ALU.mult, ALU.add)
                    last.then_inc(o3_used, 1)
                dve.wait_ge(o3_used, NE3)
                for step, t in lagged(["residual", "finish"], NT):
                    if step == "residual":
                        own_norms_done()
                        stats(XB[:, t, :], t)
                    if step == "finish":
                        finish(XB[:, t, :], t)

            XT_BEFORE_EMA = 7 * NT
            UP_BEFORE_TOP1 = 2 * 2 * NT + 8 + NT
            dve.wait_ge(init_pool, 1)
            with dve.Fori(0, 2):
                start_of_turn()
                chain("a0", "x0")
                first_ffn(0)
                first_ffn(1)
                chain("f1", "a1", "x1")
                gelu_ffn()
                chain("gelu", "ema", "x2")
                top1_ffn()
                chain("top1", "a3", "x3")
                top2_ffn()
                end_of_turn()

        @block.gpsimd
        def _(pool):
            due = Tally()

            def link(ins):
                ins.then_inc(pool_link, 1)
                pool.wait_ge(pool_link, due(pool_link))

            def end_of_turn():
                pool.drain().then_inc(turn_done, 1)
                due.count.clear()

            def start_of_turn():
                pool.wait_ge(go_pool, 1)
                pool.sem_clear(go_pool)

            tt, ts = pool.tensor_tensor, pool.tensor_scalar
            half = w("neghalf")
            pool.wait_ge(first_in, 16)
            for step, g in lagged(MIX0, 8):
                j = g % 2
                if step == "scale":
                    pool.wait_ge(vw_ready, g + 1)
                    if g >= 2:
                        pool.wait_ge(state_full, 2 * g - 2)
                    tt(VJ[:, j, :, :], bc(VW[:, j, :], [P, 8, P], 1), bc(w("seq_of"), [P, 8, P], 2),
                       ALU.mult).then_inc(vj_ready, 1)
            end_of_turn()

            pool.memset(VX[:, :, :, :], 0.0)
            pool.memset(VX32[:, :, :, :], 0.0).then_inc(pool_init, 1)
            pool.wait_ge(pool_init, 1)
            n_init = 1
            for b in range(2):
                r = slice(b * S, (b + 1) * S)
                for v, c in ((VX, 32), (VX32, 16)):
                    pool.memset(v[r, :, :, c + b:c + b + 1], 1.0).then_inc(pool_init, 1)
                    n_init += 1
                    pool.wait_ge(pool_init, n_init)
            pool.sem_inc(init_pool, 1)
            pool.wait_ge(rest_in, 16)

            def norms(n=NT):
                for t in range(n):
                    rstds(t)

            def rstds(t):
                pool.wait_ge(var_ready, due(var_ready))
                link(ts(veps[:, t % 2, :], mv[:, t % 2, 1:2], EPS, None, ALU.add))
                tt(rstd[:, t % 2, :], veps[:, t % 2, :], half, ALU.pow).then_inc(rstd_ready, 1)

            def chain(*stages):
                at_ = {}
                if due.now(x_ready):
                    pool.wait_ge(x_ready, due.now(x_ready))
                if stages[-1] in ATT:
                    pool.memset(ON[:, :, :, :], 0.0).then_inc(on_clear, 1)
                for name, step, u, t, s_ in chain_order(stages, "pool"):
                    if step in ("project", "back") and name in BIASED and s_ == 0:
                        if t in at_:
                            pool.wait_ge(x_ready, at_[t])
                        if name == "x0":
                            pool.wait_ge(masks_in, 16 * 6)
                            link(ts(XB[:, t, :], w("x0.bo"), m_tok[:, t:t + 1], None, ALU.mult))
                            tt(XB[:, t, :], X[:, t, :], XB[:, t, :], ALU.add).then_inc(xb_ready, 1)
                        else:
                            b = w("Abo") if name == "a0" else w("ema.bout") if name == "ema" else w(f"{name}.bo")
                            tt(XB[:, t, :], X[:, t, :], b, ALU.add).then_inc(xb_ready, 1)
                    if step == "scores" and att[name]["mask"] is not None:
                        for b in range(2):
                            slot = 2 * (u % 2) + b
                            pool.wait_ge(mx_ready, due(mx_ready))
                            v = sm[:, slot, :].rearrange("p (h k) -> p h k", h=8)
                            tt(v, v, bc(mx[:, slot, :], [P, 8, S], 2), ALU.subtract).then_inc(pcentered, 1)
                    if step == "residual":
                        rstds(t)
                    if step == "finish":
                        at_[t] = due(x_ready)

            def first_ffn(l):
                if l == 0:
                    pool.memset(QM[:, :, :, :, :], 0.0)
                    pool.memset(PM[:, :, :, :], 0.0)
                for u in range(2 * NT):
                    pool.wait_ge(raw_ready, due(raw_ready))
                    if u >= 4:
                        pool.wait_ge(rotated, 2 * NT * l + u - 3)
                    t, i = divmod(u, 2)
                    tt(M1[:, u % 4, :].rearrange("p (h d) -> p h d", d=S),
                       RAW[:, t, i, :].rearrange("p (h d) -> p h d", d=S),
                       bc(rot[:, l, 2 * i, :], [P, 8, S], 1), ALU.mult).then_inc(m1_ready, 1)
                if l == 0:
                    pool.memset(ON[:, :, :, :], 0.0).then_inc(zeroed, 1)
                for step, t in local_order(l, "pool"):
                    if step == "rotate":
                        if t == 0:
                            pool.wait_ge(rn_ready, l + 1)
                        pool.wait_ge(rotated, 2 * NT * l + 2 * t + 2)
                        zk = RAW[:, t, 1, :].rearrange("p (h d) -> p h d", d=S)
                        tt(zk, zk, bc(rn[:, t, 8:16], [P, 8, S], 2), ALU.mult).then_inc(zk_ready, 1)
                    if step == "scores":
                        pool.wait_ge(mx_ready, due(mx_ready))
                        v = sm[:, t % 2, :].rearrange("p (h k) -> p h k", h=8)
                        tt(v, v, bc(mx[:, t % 2, :], [P, 8, S], 2), ALU.subtract).then_inc(pcentered, 1)
                    if step == "soft":
                        pool.wait_ge(sum_ready, due(sum_ready))
                        v = PR(t).rearrange("p (g k) -> p g k", g=8)
                        tt(v, v, bc(mx[:, 2 + t % 2, :], [P, 8, S], 2), ALU.mult).then_inc(pn_ready, 1)
                    if step == "stats":
                        rstds(t)

            pool.wait_ge(init_dve, 1)
            with pool.Fori(0, 2) as it:
                start_of_turn()
                pool.tensor_copy(OTh[:, :].rearrange("p (i j) -> p i j", j=S),
                                 OTall[:, bass.ds(it * NB, NB), :]).then_inc(oth_ready, 1)
                pool.wait_ge(x_in, 16)
                pool.memset(HT[:, :, 0:1], 0.0)
                pool.memset(HS[:, :, :, :], 0.0).then_inc(zeroed, 1)
                chain("a0", "x0")
                first_ffn(0)
                first_ffn(1)
                chain("f1", "a1", "x1")
                pool.wait_ge(ew_in, 16)
                tt(ew[:, :].unsqueeze(2), ew2[:, :, 0:1], ew2[:, :, 1:2], ALU.add).then_inc(ew_ready, 1)
                chain("gelu", "ema", "x2")
                chain("top1", "a3", "x3")
                norms()
                end_of_turn()


def tables():
    r = np.arange(P)
    q = r % S
    k = np.arange(S)
    one_hot = lambda a, n: (a[:, None] == np.arange(n)[None, :])
    half = np.arange(0, S, 2, dtype=np.float32)
    inv = (1.0 / 10000.0 ** (half / S)).astype(np.float32)
    pos = np.arange(S, dtype=np.float32)
    f = pos[:, None] * inv[None, :]
    f = np.concatenate([f, f], -1).astype(np.float64)
    base = (half + 0.4 * S) / (1.4 * S)
    power = (pos - S // 2) / (S // 2)
    scale = base[None, :].astype(np.float64) ** power[:, None]
    scale = np.concatenate([scale, scale], -1)
    sign = np.where(np.arange(S) < S // 2, -1.0, 1.0)[None, :]
    two = lambda a: np.concatenate([a, a], 0)
    c = {
        "ident": np.eye(P), "blocks": (r[:, None] // 8 == r[None, :] // 8), "seq_of": one_hot(r // 16, 8),
        "fold": one_hot(q, S), "par16": one_hot(r // 8 % 2, 2), "par32": one_hot(r // 4 % 2, 2),
        "pair16": one_hot(r // 16, 8), "pair32": one_hot(r // 8, 16),
        "causal": np.where(q[:, None] >= k[None, :], BIG, -1e30),
        "not_first": np.broadcast_to(np.arange(HALF) % S != 0, (P, HALF)),
        "down16": np.broadcast_to(np.arange(16, 0, -1), (P, 16)), "down8": np.broadcast_to(np.arange(8, 0, -1), (P, 8)),
        "cosq": two(np.cos(f) * scale), "sinq": two(np.sin(f) * scale * sign),
        "cosk": two(np.cos(f) / scale), "sink": two(np.sin(f) / scale * sign),
        "neghalf": np.full((P, 1), -0.5),
    }
    return {n: np.ascontiguousarray(v, dtype=np.float32) for n, v in c.items()}


def pack(names, parts):
    out = np.zeros((P, sum(n for _, n in names)), np.float32)
    a = 0
    for name, n in names:
        v = parts[name]
        out[:v.shape[0], a:a + n] = v
        a += n
    return out


def rows(v):
    return np.broadcast_to(v.reshape(1, -1), (P, v.size))


def chunks(v):
    return v.reshape(-1, P, v.shape[-1]).transpose(1, 0, 2).reshape(P, -1)


def kernel(**inputs):
    import concourse.bacc as bacc
    from concourse.bass_utils import run_bass_kernel_spmd as run

    i = {n: np.asarray(v) for n, v in inputs.items()}
    parts = tables()
    cat = np.concatenate
    parts["Aw"] = cat([i[f"L0_attn_W{n}_w"].T for n in "qkvwr"], 1)
    parts["Ab"] = cat([rows(i[f"L0_attn_W{n}_b"]) for n in "qkvwr"], 1)
    parts["Ao"], parts["Abo"] = i["L0_attn_Wo_w"].T, rows(i["L0_attn_Wo_b"])
    none = np.zeros(P, np.float32)
    qkv1, qkv2, b2 = i["L1_attn_W_qkv"].T, i["L2_xattn_Wqkv"], i["L2_xattn_bqkv"]
    weights = {
        "x0": [i["L0_xattn_W" + n] for n in "QKVO"] + [i["L0_xattn_b" + n] for n in "QKVO"],
        "a1": [qkv1[:, 0:P], qkv1[:, P:2 * P], qkv1[:, 2 * P:], np.eye(P, dtype=np.float32)] + [none] * 4,
        "x1": [i["L1_xattn_W" + n] for n in "qkvo"] + [i["L1_xattn_b" + n] for n in "qkvo"],
        "x2": [qkv2[:, 0:P], qkv2[:, P:2 * P], qkv2[:, 2 * P:], i["L2_xattn_Wo"], b2[0:P], b2[P:2 * P], b2[2 * P:],
               i["L2_xattn_bo"]],
        "a3": [i["L3_attn_W_" + n] for n in "qkvo"] + [none] * 3 + [i["L3_attn_b_o"]],
        "x3": [i["L3_xattn_W" + n].T for n in "qkvo"] + [none] * 4,
    }
    for a, (q, k, v, o, bq, bk, bv, bo) in weights.items():
        parts.update({f"{a}.q": q, f"{a}.k": k, f"{a}.v": v, f"{a}.o": o, f"{a}.bq": bq[:, None],
                      f"{a}.bk": bk[:, None], f"{a}.bv": rows(bv), f"{a}.bo": rows(bo)})
    swap = cat([np.arange(S // 2, S), np.arange(S // 2)])
    fill = np.zeros(3 * P - HID, np.float32)
    for l in range(2):
        b1 = i["L0_ffn_b1"][l]
        w2 = cat([i["L0_ffn_w2"][l], np.zeros((3 * P - HID, P), np.float32)], 0)
        parts.update({
            f"f{l}.b1a": cat([b1[:HID], fill]).reshape(3, P).T, f"f{l}.b1g": cat([b1[HID:], fill]).reshape(3, P).T,
            f"f{l}.b2": i["L0_ffn_b2"][l][:, None], f"f{l}.g": i["L0_ffn_ln_g"][l][:, None],
            f"f{l}.b": i["L0_ffn_ln_b"][l][:, None],
            f"f{l}.qs": rows(i["L0_ffn_q_scale"][l]), f"f{l}.ks": rows(i["L0_ffn_k_scale"][l]),
            f"f{l}.qsr": rows(i["L0_ffn_q_scale"][l][swap]), f"f{l}.ksr": rows(i["L0_ffn_k_scale"][l][swap]),
            f"f{l}.wqkv": i["L0_ffn_wqkv"][l], f"f{l}.wo": chunks(i["L0_ffn_wo"][l]), f"f{l}.w1": i["L0_ffn_w1"][l],
            f"f{l}.w2": chunks(w2)})
    parts.update({
        "g.w1": i["L1_ffn_w1"], "g.w2": chunks(i["L1_ffn_w2"]),
        "ema.in": i["L2_attn_W_in"].T, "ema.out": i["L2_attn_W_out"].T, "ema.bin": i["L2_attn_b_in"][:, None],
        "ema.bout": rows(i["L2_attn_b_out"]), "decay": rows(i["L2_attn_decay"]), "mix": rows(i["L2_attn_mix"]),
        "e2.r": i["L2_ffn_w_router"].T, "e2.g": i["L2_ffn_w_gate"].T, "e2.u": i["L2_ffn_w_up"].T,
        "e2.d": chunks(i["L2_ffn_w_down"].T), "e3.r": i["L3_ffn_Wg"].T,
        "e3.b1": i["L3_ffn_b1"].reshape(NE3 * 4, P).T, "e3.b2": i["L3_ffn_b2"],
        "rel": np.tile(i["L3_attn_rel_emb"][0:S].T, (16, 1)),
    })
    x = i["x"]
    mask = i["mask_BxSx1_ff1"].reshape(B, S)
    two = lambda v: cat([v, v], 0)
    exw = np.zeros((P, 2 * NT, 2), np.float32)
    ew = i["L1_ffn_expert_weights"]
    exw[:, 0:ew.shape[0] // P] = ew.reshape(-1, P, 2).transpose(1, 0, 2)
    arrays = {
        "small": pack(FIRST + REST, parts), "early": pack(EARLY, parts),
        "xperm": x.transpose(2, 1, 0).reshape(P, TOK),
        "xtok": x.reshape(2 * NT, P, P).transpose(1, 0, 2),
        "ctxT": i["ctx_1024"].reshape(TOK, P).T,
        "mrow": np.broadcast_to(mask[None], (P, B, S)), "mcol": two(mask.T),
        "mtok": mask.reshape(2 * NT, P).T,
        "pad_rows": np.broadcast_to(i["mask_BxS2_bk0"][None], (P, B, S)),
        "att_rows": two(i["mask_SxS2_bk1"]),
        "ik_rows": two(i["mask_Bx1xSxS2_ik1"].reshape(B, S, S).transpose(1, 0, 2)),
        "exw": exw,
        "gup": i["L2_ffn_gate_up_proj"], "down": i["L2_ffn_down_proj"], "e3w1": i["L3_ffn_W1"], "e3w2": i["L3_ffn_W2"],
    }
    nc = bacc.Bacc("TRN2", target_bir_lowering=False, num_devices=1)
    args = []
    for n, a in arrays.items():
        arrays[n] = a = np.ascontiguousarray(a)
        args.append(nc.dram_tensor(n, a.shape, mybir.dt.from_np(a.dtype), kind="ExternalInput").ap())
    y = nc.dram_tensor("y", (B, S, P), F32, kind="ExternalOutput").ap()
    decoder(nc, *args, y.rearrange("(t b) s d -> (b s) t d", b=2))
    r = run(nc, [arrays], core_ids=[0])
    return r.results[0]["y"]
```
